# Optimizing a Trainium2 kernel written in Bass

```python
import numpy as np
import jax
import jax.numpy as jnp

def _softmax(x, axis=-1):
    return jax.nn.softmax(x, axis=axis)

def _gelu(x):
    return jax.nn.gelu(x, approximate=True)

def _silu(x):
    return jax.nn.silu(x)

def _sigmoid(x):
    return jax.nn.sigmoid(x)

def _layernorm(x, axis=-1, eps=1e-05):
    m = jnp.mean(x, axis=axis, keepdims=True)
    v = jnp.var(x, axis=axis, keepdims=True)
    return (x - m) / jnp.sqrt(v + eps)

def _scatter_add(tgt, idx, src, axis=0):
    return tgt.at[idx].add(src)

def _segment_sum(src, seg, n):
    return jax.ops.segment_sum(src, seg, n)
kernel_name = 'mk_gnn_resnorm_d2_gnn_r8_30dd6c'

def setup_inputs(seed: int=0):
    np.random.seed(seed)
    _w = jnp.asarray

    def _rec_inputs():
        import jax
        import jax.numpy as jnp
        _gk = jax.random.key(seed)
        x = -0.000202 + 1 * jax.random.normal(jax.random.fold_in(_gk, 1), (6250, 128), jnp.float32)
        _s = jax.random.randint(jax.random.fold_in(_gk, 2), (50000,), 0, 6250, jnp.int32)
        _d = jax.random.randint(jax.random.fold_in(_gk, 3), (50000,), 0, 6250, jnp.int32)
        _loop = jnp.arange(6250, dtype=jnp.int32)
        src = jnp.concatenate([_s, _d, _loop])
        dst = jnp.concatenate([_d, _s, _loop])
        _o = jnp.argsort(dst, stable=True)
        src = src[_o]
        dst = dst[_o]
        edge_attr_3 = -0.000451519 + 1.00018 * jax.random.normal(jax.random.fold_in(_gk, 12), (106250, 3), jnp.float32)
        edge_type_4 = jax.random.randint(jax.random.fold_in(_gk, 14), (106250,), 0, 4, jnp.int32)
        edge_weight = jax.random.uniform(jax.random.fold_in(_gk, 15), (106250,), jnp.float32, 0.0, 0.999998)
        return (x, src, dst, edge_attr_3, edge_type_4, edge_weight)
    x, src, dst, edge_attr_3, edge_type_4, edge_weight = _rec_inputs()

    def _L0_gnn_setup():
        import jax, jax.numpy as jnp
        import numpy as np
        N = 6250
        E = 100000
        MUL = 32
        NB = 8
        R_MAX = 1.0
        AVG = 16.0
        SQ3 = 3.0 ** 0.5

        def _radial_embedding(r):
            x = jnp.clip(r / R_MAX, 0.0, 1.0)
            centers = jnp.arange(NB, dtype=jnp.float32) / (NB - 1)
            sigma = 1.0 / (NB - 1)
            emb = jnp.exp(-0.5 * ((x[:, None] - centers[None, :]) / sigma) ** 2)
            emb = emb * NB ** 0.5 * (r <= R_MAX).astype(jnp.float32)[:, None]
            return emb
        key = jax.random.key(seed)
        k = jax.random.split(key, 12)
        inp = {'node_feats': jax.random.normal(k[0], (N, 4 * MUL), dtype=jnp.float32), 'edge_vec': jax.random.normal(k[1], (E, 3), dtype=jnp.float32), 'edge_length': jax.random.uniform(k[2], (E,), dtype=jnp.float32), 'senders': jax.random.randint(k[3], (E,), 0, N, dtype=jnp.int32), 'receivers': jax.random.randint(k[4], (E,), 0, N, dtype=jnp.int32), 'num_nodes': N, 'W_up0': jax.random.normal(k[5], (MUL, MUL), dtype=jnp.float32), 'W_up1': jax.random.normal(k[6], (MUL, MUL), dtype=jnp.float32), 'mlp_w0': jax.random.normal(k[7], (NB, 64), dtype=jnp.float32) / NB ** 0.5, 'mlp_b0': jnp.zeros((64,), dtype=jnp.float32), 'mlp_w1': jax.random.normal(k[8], (64, 64), dtype=jnp.float32) / 8.0, 'mlp_b1': jnp.zeros((64,), dtype=jnp.float32), 'mlp_w2': jax.random.normal(k[9], (64, 4 * MUL), dtype=jnp.float32) / 8.0, 'mlp_b2': jnp.zeros((4 * MUL,), dtype=jnp.float32), 'W_out0': jax.random.normal(k[10], (2 * MUL, MUL), dtype=jnp.float32), 'W_out1': jax.random.normal(k[11], (2 * MUL, MUL), dtype=jnp.float32)}
        return inp
    _L0_gnn_all = _L0_gnn_setup()
    _L0_gnn_in = {k: v for k, v in _L0_gnn_all.items() if k in ('W_up0', 'W_up1', 'mlp_w0', 'mlp_b0', 'mlp_w1', 'mlp_b1', 'mlp_w2', 'mlp_b2', 'W_out0', 'W_out1')}
    del _L0_gnn_all

    def _L1_gnn_setup():
        import jax, jax.numpy as jnp
        import numpy as np
        N, E, H, T = (6250, 75000, 128, 4)
        LN_EPS = 1e-05
        key = jax.random.key(seed)
        ks = jax.random.split(key, 16)
        x = jax.random.normal(ks[0], (N, H), jnp.float32)
        edge_index = jax.random.randint(ks[1], (2, E), 0, N, dtype=jnp.int64)
        edge_type = jax.random.randint(ks[2], (E,), 0, T, dtype=jnp.int64)
        s1 = 1.0 / np.sqrt(2 * H).astype(np.float32)
        s2 = 1.0 / np.sqrt(H).astype(np.float32)
        W1 = jax.random.uniform(ks[3], (T, 2 * H, H), jnp.float32, -s1, s1)
        b1 = jax.random.uniform(ks[4], (T, H), jnp.float32, -s1, s1)
        W2 = jax.random.uniform(ks[5], (T, H, H), jnp.float32, -s2, s2)
        b2 = jax.random.uniform(ks[6], (T, H), jnp.float32, -s2, s2)
        attn_w = jax.random.uniform(ks[7], (T, 2 * H), jnp.float32, -s1, s1)
        attn_b = jax.random.uniform(ks[8], (T,), jnp.float32, -s1, s1)
        w_ih = jax.random.uniform(ks[9], (3 * H, H), jnp.float32, -s2, s2)
        w_hh = jax.random.uniform(ks[10], (3 * H, H), jnp.float32, -s2, s2)
        b_ih = jax.random.uniform(ks[11], (3 * H,), jnp.float32, -s2, s2)
        b_hh = jax.random.uniform(ks[12], (3 * H,), jnp.float32, -s2, s2)
        ln_gamma = jnp.ones((H,), jnp.float32)
        ln_beta = jnp.zeros((H,), jnp.float32)
        return dict(x=x, edge_index=edge_index, edge_type=edge_type, W1=W1, b1=b1, W2=W2, b2=b2, attn_w=attn_w, attn_b=attn_b, w_ih=w_ih, w_hh=w_hh, b_ih=b_ih, b_hh=b_hh, ln_gamma=ln_gamma, ln_beta=ln_beta)
    _L1_gnn_all = _L1_gnn_setup()
    _L1_gnn_in = {k: v for k, v in _L1_gnn_all.items() if k in ('W1', 'b1', 'W2', 'b2', 'attn_w', 'attn_b', 'w_ih', 'w_hh', 'b_ih', 'b_hh', 'ln_gamma', 'ln_beta')}
    del _L1_gnn_all
    return {'x': x, 'src': src, 'dst': dst, 'edge_attr_3': edge_attr_3, 'edge_type_4': edge_type_4, 'edge_weight': edge_weight, 'L0_gnn_W_up0': _L0_gnn_in['W_up0'], 'L0_gnn_W_up1': _L0_gnn_in['W_up1'], 'L0_gnn_mlp_w0': _L0_gnn_in['mlp_w0'], 'L0_gnn_mlp_b0': _L0_gnn_in['mlp_b0'], 'L0_gnn_mlp_w1': _L0_gnn_in['mlp_w1'], 'L0_gnn_mlp_b1': _L0_gnn_in['mlp_b1'], 'L0_gnn_mlp_w2': _L0_gnn_in['mlp_w2'], 'L0_gnn_mlp_b2': _L0_gnn_in['mlp_b2'], 'L0_gnn_W_out0': _L0_gnn_in['W_out0'], 'L0_gnn_W_out1': _L0_gnn_in['W_out1'], 'L1_gnn_W1': _L1_gnn_in['W1'], 'L1_gnn_b1': _L1_gnn_in['b1'], 'L1_gnn_W2': _L1_gnn_in['W2'], 'L1_gnn_b2': _L1_gnn_in['b2'], 'L1_gnn_attn_w': _L1_gnn_in['attn_w'], 'L1_gnn_attn_b': _L1_gnn_in['attn_b'], 'L1_gnn_w_ih': _L1_gnn_in['w_ih'], 'L1_gnn_w_hh': _L1_gnn_in['w_hh'], 'L1_gnn_b_ih': _L1_gnn_in['b_ih'], 'L1_gnn_b_hh': _L1_gnn_in['b_hh'], 'L1_gnn_ln_gamma': _L1_gnn_in['ln_gamma'], 'L1_gnn_ln_beta': _L1_gnn_in['ln_beta']}

def reference(x, src, dst, edge_attr_3, edge_type_4, edge_weight, L0_gnn_W_up0, L0_gnn_W_up1, L0_gnn_mlp_w0, L0_gnn_mlp_b0, L0_gnn_mlp_w1, L0_gnn_mlp_b1, L0_gnn_mlp_w2, L0_gnn_mlp_b2, L0_gnn_W_out0, L0_gnn_W_out1, L1_gnn_W1, L1_gnn_b1, L1_gnn_W2, L1_gnn_b2, L1_gnn_attn_w, L1_gnn_attn_b, L1_gnn_w_ih, L1_gnn_w_hh, L1_gnn_b_ih, L1_gnn_b_hh, L1_gnn_ln_gamma, L1_gnn_ln_beta):
    import jax
    import jax.numpy as jnp

    def _L0_gnn_ref(node_feats, edge_vec, edge_length, senders, receivers, num_nodes, W_up0, W_up1, mlp_w0, mlp_b0, mlp_w1, mlp_b1, mlp_w2, mlp_b2, W_out0, W_out1):
        import jax, jax.numpy as jnp
        import numpy as np
        N = 6250
        E = 100000
        MUL = 32
        NB = 8
        R_MAX = 1.0
        AVG = 16.0
        SQ3 = 3.0 ** 0.5

        def _radial_embedding(r):
            x = jnp.clip(r / R_MAX, 0.0, 1.0)
            centers = jnp.arange(NB, dtype=jnp.float32) / (NB - 1)
            sigma = 1.0 / (NB - 1)
            emb = jnp.exp(-0.5 * ((x[:, None] - centers[None, :]) / sigma) ** 2)
            emb = emb * NB ** 0.5 * (r <= R_MAX).astype(jnp.float32)[:, None]
            return emb
        f32 = jnp.float32
        rhat = edge_vec / (jnp.linalg.norm(edge_vec, axis=-1, keepdims=True) + 1e-12)
        Y1 = SQ3 * rhat
        emb = _radial_embedding(edge_length)
        h = jax.nn.silu(emb @ mlp_w0 + mlp_b0)
        h = jax.nn.silu(h @ mlp_w1 + mlp_b1)
        w = (h @ mlp_w2 + mlp_b2).reshape(-1, 4, MUL)
        s = node_feats[:, :MUL]
        v = node_feats[:, MUL:].reshape(-1, MUL, 3)
        xs = s @ W_up0 / f32(MUL) ** 0.5
        xv = jnp.einsum('nmc,mk->nkc', v, W_up1) / f32(MUL) ** 0.5
        ss = xs[senders]
        vv = xv[senders]
        m0 = w[:, 0] * ss
        m1 = w[:, 1][:, :, None] * ss[:, :, None] * Y1[:, None, :]
        m2 = w[:, 2][:, :, None] * vv
        m3 = w[:, 3] * (jnp.einsum('emc,ec->em', vv, Y1) / SQ3)
        mid_s = jnp.concatenate([m0, m3], axis=1)
        mid_v = jnp.concatenate([m1, m2], axis=1)
        msg_s = jax.ops.segment_sum(mid_s, receivers, num_segments=num_nodes)
        msg_v = jax.ops.segment_sum(mid_v, receivers, num_segments=num_nodes)
        out_s = msg_s @ W_out0 / f32(2 * MUL) ** 0.5
        out_v = jnp.einsum('nmc,mk->nkc', msg_v, W_out1) / f32(2 * MUL) ** 0.5
        out = jnp.concatenate([out_s, out_v.reshape(-1, 3 * MUL)], axis=1)
        return out / max(AVG, 1e-08)

    def _L1_gnn_ref(x, edge_index, edge_type, W1, b1, W2, b2, attn_w, attn_b, w_ih, w_hh, b_ih, b_hh, ln_gamma, ln_beta):
        import jax, jax.numpy as jnp
        import numpy as np
        N, E, H, T = (6250, 75000, 128, 4)
        LN_EPS = 1e-05
        src, dst = (edge_index[0], edge_index[1])
        msg_in = jnp.concatenate([x[src], x[dst]], axis=1)
        n_types = W1.shape[0]
        msgs = jnp.zeros((msg_in.shape[0], W1.shape[2]), x.dtype)
        for t in range(n_types):
            h = jax.nn.relu(msg_in @ W1[t] + b1[t])
            m = h @ W2[t] + b2[t]
            score = jax.nn.sigmoid(msg_in @ attn_w[t] + attn_b[t])
            m = m * score[:, None]
            msgs = msgs + jnp.where((edge_type == t)[:, None], m, 0.0)
        agg = jnp.zeros_like(x).at[dst].add(msgs)
        Hd = x.shape[1]
        gi = agg @ w_ih.T + b_ih
        gh = x @ w_hh.T + b_hh
        r = jax.nn.sigmoid(gi[:, :Hd] + gh[:, :Hd])
        z = jax.nn.sigmoid(gi[:, Hd:2 * Hd] + gh[:, Hd:2 * Hd])
        n = jnp.tanh(gi[:, 2 * Hd:] + r * gh[:, 2 * Hd:])
        x_new = (1.0 - z) * n + z * x
        x_new = x_new + x
        mu = jnp.mean(x_new, axis=-1, keepdims=True)
        var = jnp.mean(jnp.square(x_new - mu), axis=-1, keepdims=True)
        return (x_new - mu) * jax.lax.rsqrt(var + LN_EPS) * ln_gamma + ln_beta
    edge_index = jnp.stack([src, dst])
    x = _layernorm(x + _L0_gnn_ref(x, edge_attr_3, edge_weight, src, dst, 6250, L0_gnn_W_up0, L0_gnn_W_up1, L0_gnn_mlp_w0, L0_gnn_mlp_b0, L0_gnn_mlp_w1, L0_gnn_mlp_b1, L0_gnn_mlp_w2, L0_gnn_mlp_b2, L0_gnn_W_out0, L0_gnn_W_out1), axis=-1)
    x = _layernorm(x + _L1_gnn_ref(x, edge_index, edge_type_4, L1_gnn_W1, L1_gnn_b1, L1_gnn_W2, L1_gnn_b2, L1_gnn_attn_w, L1_gnn_attn_b, L1_gnn_w_ih, L1_gnn_w_hh, L1_gnn_b_ih, L1_gnn_b_hh, L1_gnn_ln_gamma, L1_gnn_ln_beta), axis=-1)
    return x

_drawn_inputs = setup_inputs


def setup_inputs(seed=0):
    import zlib

    import numpy as np

    out = dict(_drawn_inputs(seed))
    spreads = {'L0_gnn_mlp_b0': (0.0, 0.8),
     'L0_gnn_mlp_b1': (0.0, 0.57),
     'L0_gnn_mlp_b2': (0.0, 0.345),
     'L1_gnn_ln_gamma': (1.0, 0.2),
     'L1_gnn_ln_beta': (0.0, 0.1)}
    factors = {'L1_gnn_b1': 8.0,
     'L1_gnn_b2': 3.192,
     'L1_gnn_attn_w': 3.281,
     'L1_gnn_attn_b': 58.784,
     'L1_gnn_b_ih': 7.121,
     'L1_gnn_b_hh': 8.0}
    for name, (base, spread) in spreads.items():
        noise = np.random.default_rng([zlib.crc32(name.encode()), seed]).standard_normal(out[name].shape)
        drawn = base * np.exp(spread * noise) if base else spread * noise
        out[name] = jnp.asarray(drawn.astype(out[name].dtype))
    for name, factor in factors.items():
        out[name] = (out[name] * factor).astype(out[name].dtype)
    return out
```

```python
import concourse.bass as bass
from concourse import mybir
from concourse.alu_op_type import AluOpType as ALU
from contextlib import ExitStack

P = 128
N = 6250
E = 106250
H = 128
MUL = 32
NB = 8
T = 4
WIN = 32
TPS = 8
PPS = TPS // 2
STEPS = -(-E // (P * TPS))
TILES = STEPS * TPS
LTILES = TILES + 2 * TPS
NT = -(-N // P)
NP = NT * P
NACC = NP + 16
GRP = 7
NG = NT // GRP
PW = H + 1
HID = 64
ECH = 16
SPC = STEPS // (ECH // 2)
HALF = P * TPS // 2
LN_EPS = 1e-5
FAR = 1.0e6

f32, bf16 = mybir.dt.float32, mybir.dt.bfloat16
i32, u32 = mybir.dt.int32, mybir.dt.uint32
ACT = mybir.ActivationFunctionType
AX = mybir.AxisListType


def spread(ap, at, n):
    ap = ap.unsqueeze(at)
    shape = list(ap.shape)
    shape[at] = n
    return ap.to_broadcast(shape)


class Own:

    def __init__(self, eng, sem):
        self.eng, self.sem, self.n = eng, sem, 0

    def did(self, ins):
        self.n += 1
        ins.then_inc(self.sem, 1)
        return self.n

    def then(self, ins):
        self.eng.wait_ge(self.sem, self.did(ins))


class Mem:

    def __init__(self, nc, ctx):
        self.nc, self.ctx = nc, ctx

    def sb(self, name, shape, dt=f32):
        return self.ctx.enter_context(self.nc.sbuf_tensor(name, shape, dt))

    def ps(self, name, shape, dt=f32):
        return self.ctx.enter_context(self.nc.psum_tensor(name, shape, dt))

    def sem(self, name):
        return self.ctx.enter_context(self.nc.semaphore(name))

    def sems(self, name, n):
        return [self.sem(f"{name}{k}") for k in range(n)]


def build(nc, a, out):
    top = ExitStack()
    with top:
        m = Mem(nc, top)
        k = dict(
            acc=m.sb("acc", [P, T * NACC]),
            acc_s=m.sb("acc_s", [P, NACC]),
            ident=m.sb("ident", [P, P]),
            iota=m.sb("iota", [P, T * P]),
            key=m.sb("key", [P, LTILES]),
            dloc=m.sb("dloc", [P, LTILES]),
            typef=m.sb("typef", [P, LTILES]),
            left=m.sb("left", [P, LTILES]),
            start=m.sb("start", [1, LTILES // 2], i32),
            n_left=m.sb("n_left", [1, 1], i32),
            zero=m.sb("zero", [P, 512]),
        )
        dram = dict(
            emb=nc.dram_tensor("emb_d", [STEPS + 2, 2 * NB, HALF], f32).ap(),
            node0=nc.dram_tensor("node0_d", [NP, H], f32).ap(),
            p_idx=nc.dram_tensor("p_idx_d", [P, LTILES], u32).ap(),
            q_idx=nc.dram_tensor("q_idx_d", [P, LTILES], u32).ap(),
            x1=nc.dram_tensor("x1_d", [NP, H], f32).ap(),
            p_tab=nc.dram_tensor("p_tab_d", [NP * T, PW], f32).ap(),
            q_tab=nc.dram_tensor("q_tab_d", [NACC * T, PW], f32).ap(),
        )
        with ExitStack() as layer0:
            w = layer0_weights(nc, Mem(nc, layer0))
            prepare(nc, a, k, dram, w)
            edges0(nc, a, k, dram, w)
            leftover0(nc, a, k, dram, w)
        between(nc, a, k, dram)
        clear_sums(nc, k)
        edges1(nc, k, dram)
        leftover1(nc, k, dram)
        update(nc, a, k, dram, out)


def layer0_weights(nc, m):
    return dict(
        w0=m.sb("w0", [2 * NB, P]), b0=m.sb("b0", [P, 1]),
        w1=m.sb("w1", [P, P]), b1=m.sb("b1", [P, 1]),
        w2=m.sb("w2", [P, P]),
        b2=m.sb("b2", [3, P], bf16), ones=m.sb("ones", [3, P], bf16),
        y=m.sb("y", [P, TILES, 3]),
    )


def split3(e, own, src, hi, mid, lo, rest):
    own.then(e.tensor_copy(hi, src))
    own.then(e.tensor_tensor(rest, src, hi, ALU.subtract))
    own.then(e.tensor_copy(mid, rest))
    own.then(e.tensor_tensor(rest, rest, mid, ALU.subtract))
    own.then(e.tensor_copy(lo, rest))


def prepare(nc, a, k, dram, w):
    with ExitStack() as ctx:
        m = Mem(nc, ctx)
        acc = k["acc"]
        cols = SPC * HALF
        emb, mask = acc[:, 0:cols], acc[:, cols:2 * cols]
        vec = acc[:, 2 * cols:2 * cols + 3 * TILES].rearrange("p (t c) -> p t c", c=3)
        vec2 = acc[:, 2 * cols + 3 * TILES:2 * cols + 6 * TILES].rearrange("p (t c) -> p t c", c=3)
        src_i, dst_i, type_i = (m.sb(n, [P, LTILES], i32) for n in ("src_i", "dst_i", "type_i"))
        start_i = m.sb("start_i", [P, LTILES // 2], i32)
        dstf, srcf, hit = (m.sb(n, [P, LTILES]) for n in ("dstf", "srcf", "hit"))
        startf = m.sb("startf", [P, LTILES // 2])
        p_idx, q_idx = m.sb("p_idx", [P, LTILES], u32), m.sb("q_idx", [P, LTILES], u32)
        n_hit, one = m.sb("n_hit", [P, 1]), m.sb("one", [P, 1])
        norm2 = m.sb("norm2", [P, TILES])
        centre_i, centre = m.sb("centre_i", [P, 1], i32), m.sb("centre", [P, 1])
        b2f = m.sb("b2f", [3, P])
        b2_hi, b2_mid, b2_lo = (m.sb(n, [3, P], bf16) for n in ("b2_hi", "b2_mid", "b2_lo"))
        w_up = m.sb("w_up", [P, P])
        x_in = m.sb("x_in", [P, GRP, H])
        x_t = m.sb("x_t", [P, GRP * P])
        tab = m.sb("tab", [P, GRP, H])
        ps_t = m.ps("ps_t", [P, 8, P])
        ps_m = m.ps("ps_m", [P, 8, P])
        ps_n = m.ps("ps_n", [1, 1])
        ld_edge, ld_len, ld_vec, ld_w, ld_up, ld_x, ld_b2 = (m.sem(n) for n in (
            "ld_edge", "ld_len", "ld_vec", "ld_w", "ld_up", "ld_x", "ld_b2"))
        clear_ok, up_clear, w_clear, tab_free, gate = (m.sem(n) for n in (
            "clear_ok", "up_clear", "w_clear", "tab_free", "gate"))
        v_own, s_own, g_own = (m.sem(n) for n in ("v_own", "s_own", "g_own"))
        clip_ok, exp_ok, emb_ok, norm_ok, root_ok, hits_ok, count_ok, idx_ok, split_ok = (m.sem(n) for n in (
            "clip_ok", "exp_ok", "emb_ok", "norm_ok", "root_ok", "hits_ok", "count_ok", "idx_ok", "split_ok"))
        emb_st, stored, tr_ok, xt_ok, mm_ok, tab_ok, tab_st = (m.sem(n) for n in (
            "emb_st", "stored", "tr_ok", "xt_ok", "mm_ok", "tab_ok", "tab_st"))

        with nc.Block() as block:

            @block.sync
            def _(e):
                for q in range(ECH):
                    e.dma_start(emb[NB * q:NB * q + NB, :],
                                a["length"][q:q + 1, :].to_broadcast([NB, cols])).then_inc(ld_len, 16)
                e.dma_start(dst_i[:], a["dst"]).then_inc(ld_edge, 16)
                e.dma_start(start_i[:], a["start"].to_broadcast([P, LTILES // 2])).then_inc(ld_edge, 16)
                e.dma_start(type_i[:], a["type"]).then_inc(ld_edge, 16)
                e.dma_start(src_i[:], a["src"]).then_inc(ld_edge, 16)
                e.dma_start(k["start"][:], a["start"]).then_inc(ld_edge, 16)
                e.dma_start(vec, a["vec"]).then_inc(ld_vec, 16)
                e.wait_ge(emb_ok, 1)
                for g in range(ECH // 2):
                    e.dma_start(dram["emb"][SPC * g:SPC * g + SPC].rearrange("s r n -> r s n"),
                                emb[2 * NB * g:2 * NB * (g + 1), :].rearrange("r (s n) -> r s n", s=SPC))\
                        .then_inc(emb_st, 16)
                e.wait_ge(clear_ok, 1)
                for s in range(2):
                    e.dma_start(dram["emb"][STEPS + s], k["zero"][0:2 * NB, :]).then_inc(stored, 16)
                e.wait_ge(idx_ok, 2)
                e.dma_start(dram["p_idx"], p_idx[:]).then_inc(stored, 16)
                e.dma_start(dram["q_idx"], q_idx[:]).then_inc(stored, 16)
                e.wait_ge(split_ok, 1)
                for r, part in enumerate((b2_hi, b2_mid, b2_lo)):
                    e.dma_start(w["b2"][r:r + 1, :], part[r:r + 1, :]).then_inc(stored, 16)
                e.wait_ge(stored, 16 * (2 + 2 + 3))
                e.wait_ge(emb_st, 16 * (ECH // 2))

            @block.scalar
            def _(e):
                e.wait_ge(up_clear, 1)
                e.dma_start(w_up[0:MUL, 0:MUL], a["W_up0"]).then_inc(ld_up, 16)
                for c in range(3):
                    e.dma_start(w_up[MUL + c:MUL + c + 3 * (MUL - 1) + 1:3, MUL * (c + 1):MUL * (c + 2)],
                                a["W_up1"]).then_inc(ld_up, 16)
                e.wait_ge(w_clear, 2)
                for half in range(2):
                    lo, hi = HID * half, HID * (half + 1)
                    e.dma_start(w["w0"][NB * half:NB * (half + 1), lo:hi], a["mlp_w0"]).then_inc(ld_w, 16)
                    e.dma_start(w["w1"][lo:hi, lo:hi], a["mlp_w1"]).then_inc(ld_w, 16)
                    e.dma_start(w["w2"][lo:hi, :], a["mlp_w2"]).then_inc(ld_w, 16)
                    e.dma_start(w["b0"][lo:hi, :], a["mlp_b0"]).then_inc(ld_w, 16)
                    e.dma_start(w["b1"][lo:hi, :], a["mlp_b1"]).then_inc(ld_w, 16)
                e.dma_start(b2f[:], a["mlp_b2"].to_broadcast([3, P])).then_inc(ld_b2, 16)
                e.wait_ge(clip_ok, 1)
                e.activation(emb, emb, ACT.Square, bias=centre[:], scale=float(NB - 1)).then_inc(s_own, 1)
                e.wait_ge(s_own, 1)
                e.activation(emb, emb, ACT.Exp, scale=-0.5).then_inc(exp_ok, 1)
                e.wait_ge(norm_ok, 1)
                e.activation(norm2[:], norm2[:], ACT.Sqrt).then_inc(root_ok, 1)
                with e.Fori(0, NG) as g:
                    e.wait_ge(mm_ok, g + 1)
                    e.wait_ge(tab_free, g + 1)
                    e.activation(tab[:], ps_m[:, 0:GRP, :], ACT.Copy, scale=float(MUL) ** -0.5)\
                        .then_inc(tab_ok, 1)
                e.wait_ge(ld_w, 16 * 10)

            @block.gpsimd
            def _(e):
                own = Own(e, g_own)
                e.memset(w_up[:], 0.0).then_inc(up_clear, 1)
                own.then(e.memset(k["ident"][:], 0.0))
                own.then(e.affine_select(out=k["ident"][:], in_=k["ident"][:], compare_op=ALU.not_equal,
                                         fill=1.0, base=0, pattern=[[-1, P]], channel_multiplier=1))
                own.then(e.iota(centre_i[:], pattern=[[0, 1]], base=0, channel_multiplier=1))
                e.iota(k["iota"][:], pattern=[[1, T * P]], base=0, channel_multiplier=0,
                       allow_small_or_imprecise_dtypes=True)
                e.memset(w["w0"][:], 0.0).then_inc(w_clear, 1)
                e.memset(w["w1"][:], 0.0).then_inc(w_clear, 1)
                e.memset(k["zero"][:], 0.0).then_inc(clear_ok, 1)
                x_g = a["x"].rearrange("(t p) f -> p t f", p=P)
                node0_g = dram["node0"].rearrange("(t p) f -> p t f", p=P)
                e.sem_inc(tab_free, 1)
                with e.Fori(0, NG) as g:
                    e.wait_ge(tr_ok, g + 1)
                    e.sem_inc(gate, 1)
                    e.dma_start(x_in[:], x_g[:, bass.ds(g * GRP, GRP), :]).then_inc(ld_x, 16)
                    e.wait_ge(tab_ok, g + 1)
                    e.sem_inc(gate, 1)
                    e.dma_start(node0_g[:, bass.ds(g * GRP, GRP), :], tab[:]).then_inc(tab_st, 16)
                    e.wait_ge(tab_st, g * 16 + 16)
                    e.sem_inc(tab_free, 1)

            @block.vector
            def _(e):
                own = Own(e, v_own)
                e.wait_ge(g_own, 3)
                own.then(e.tensor_scalar(centre_i[:], centre_i[:], NB - 1, None, ALU.bitwise_and))
                own.then(e.tensor_scalar(centre[:], centre_i[:], -1.0, None, ALU.mult))
                e.wait_ge(ld_len, 16 * ECH)
                own.did(e.tensor_scalar(mask, emb, 1.0, float(NB) ** 0.5, ALU.is_le, ALU.mult))
                e.wait_ge(v_own, own.n)
                e.tensor_scalar(emb, emb, 0.0, 1.0, ALU.max, ALU.min).then_inc(clip_ok, 1)
                e.wait_ge(ld_vec, 16)
                own.then(e.tensor_tensor(vec2, vec, vec, ALU.mult))
                e.tensor_reduce(norm2[:], vec2, AX.X, ALU.add).then_inc(norm_ok, 1)
                e.wait_ge(ld_edge, 16 * 5)
                own.did(e.tensor_copy(dstf[:], dst_i[:]))
                own.did(e.tensor_copy(startf[:], start_i[:]))
                own.did(e.tensor_copy(k["typef"][:], type_i[:]))
                own.then(e.tensor_copy(srcf[:], src_i[:]))
                pairs = "p (g t) -> p g t"
                own.did(e.scalar_tensor_tensor(p_idx[:], srcf[:], float(T), k["typef"][:], ALU.mult, ALU.add))
                own.did(e.scalar_tensor_tensor(q_idx[:], dstf[:], float(T), k["typef"][:], ALU.mult, ALU.add))
                own.then(e.tensor_tensor(k["dloc"][:].rearrange(pairs, t=2), dstf[:].rearrange(pairs, t=2),
                                         spread(startf[:], 2, 2), ALU.subtract))
                e.sem_inc(idx_ok, 2)
                own.did(e.scalar_tensor_tensor(k["key"][:], k["dloc"][:], float(T), k["typef"][:],
                                               ALU.mult, ALU.add))
                own.then(e.tensor_scalar(hit[:], k["dloc"][:], 0.0, None, ALU.is_ge))
                own.then(e.scalar_tensor_tensor(hit[:], k["dloc"][:], float(WIN), hit[:], ALU.is_lt, ALU.mult))
                own.did(e.scalar_tensor_tensor(k["left"][:], hit[:], -FAR, dstf[:], ALU.mult, ALU.add))
                own.did(e.memset(one[:], 1.0))
                e.memset(w["ones"][:], 1.0)
                e.tensor_reduce(n_hit[:], hit[:, 0:TILES], AX.X, ALU.add).then_inc(hits_ok, 1)
                e.wait_ge(root_ok, 1)
                own.then(e.tensor_scalar(norm2[:], norm2[:], 1e-12, None, ALU.add))
                own.then(e.reciprocal(norm2[:], norm2[:]))
                own.then(e.tensor_scalar(norm2[:], norm2[:], 3.0 ** 0.5, None, ALU.mult))
                own.did(e.tensor_tensor(w["y"][:], vec, spread(norm2[:], 2, 3), ALU.mult))
                e.wait_ge(count_ok, 1)
                own.did(e.tensor_scalar(k["n_left"][:], ps_n[:], -1.0, float(P * TILES), ALU.mult, ALU.add))
                e.wait_ge(exp_ok, 1)
                e.tensor_tensor(emb, emb, mask, ALU.mult).then_inc(emb_ok, 1)
                e.wait_ge(ld_b2, 16)
                split3(e, own, b2f[:], b2_hi[:], b2_mid[:], b2_lo[:], b2f[:])
                e.sem_inc(split_ok, 1)
                with e.Fori(0, NG) as g:
                    e.wait_ge(tr_ok, g + 2)
                    e.tensor_copy(x_t[:].rearrange("p (t n) -> p t n", t=GRP), ps_t[:, 0:GRP, :])\
                        .then_inc(xt_ok, 1)
                e.wait_ge(emb_st, 16 * (ECH // 2))
                e.wait_ge(v_own, own.n)
                e.wait_ge(emb_ok, 1)
                e.memset(acc[:], 0.0)

            @block.tensor
            def _(e):
                e.wait_ge(hits_ok, 1)
                e.matmul(ps_n[:], n_hit[:], one[:], start=True, stop=True).then_inc(count_ok, 1)
                e.wait_ge(g_own, 2)
                e.wait_ge(ld_up, 16 * 4)
                e.sem_inc(tr_ok, 1)
                with e.Fori(0, NG) as g:
                    e.wait_ge(ld_x, g * 16 + 16)
                    for t in range(GRP):
                        last = e.transpose(ps_t[:, t, :], x_in[:, t, :], k["ident"][:])
                    last.then_inc(tr_ok, 1)
                    e.wait_ge(xt_ok, g + 1)
                    for t in range(GRP):
                        last = e.matmul(ps_m[:, t, :], x_t[:, t * P:(t + 1) * P], w_up[:], start=True, stop=True)
                    last.then_inc(mm_ok, 1)


def start_registers(e, tag):
    return [e.alloc_register(f"{tag}_start{p}") for p in range(PPS)]


def run_starts(e, k, j, regs):
    e.load(regs, k["start"][0:1, bass.ds(j * PPS, PPS)])
    return [e.snap(r, min_val=0, max_val=N) for r in regs]


def gather_loop(e, idx, idx_in, table, buf, landed, used, gate):
    with e.Fori(0, STEPS // 2) as i:
        for h in range(2):
            e.wait_ge(idx_in[h], i * 16 + 16)
            e.sem_inc(gate, 1)
            e.wait_ge(used, i * 2 + (h + 1))
            e.sem_inc(gate, 1)
            for t in range(TPS):
                e.indirect_dma_start(
                    out=buf[:, h, t, :], out_offset=None, in_=table,
                    in_offset=bass.IndirectOffsetOnAxis(ap=idx[:, h, t:t + 1], axis=0),
                ).then_inc(landed[h], 16)


def layer0_messages(e, w, ps_w, gx, msg):
    out = msg[:].rearrange("p t (b c m) -> p t b c m", b=2, c=4)
    wt = ps_w[:].rearrange("p t (i m) -> p t i m", i=4)
    e.tensor_tensor(out[:, :, :, 3, :], wt[:, :, 0:2, :], spread(gx[:, :, 0:MUL], 2, 2), ALU.mult)
    for b in range(2):
        last = e.tensor_tensor(out[:, :, b, 0:3, :], spread(wt[:, :, 2 + b, :], 2, 3),
                               gx[:, :, MUL:H].rearrange("p t (c m) -> p t c m", c=3), ALU.mult)
    return last


def layer0_mlp1(e, w, emb, ps_h):
    return e.matmul(ps_h[:], w["w0"][:], emb, start=True, stop=True)


def layer0_mlp3(e, w, h2, ps_w):
    for half in range(2):
        lo = HID * half
        for t in range(T):
            ps = ps_w[:, T * half + t, :]
            e.matmul(ps, w["ones"][:], w["b2"][:], start=True, stop=False)
            last = e.matmul(ps, h2[lo:lo + HID, t * P:(t + 1) * P], w["w2"][lo:lo + HID, :],
                            start=False, stop=True)
    return last


def edges0(nc, a, k, dram, w):
    with ExitStack() as ctx:
        m = Mem(nc, ctx)
        idx = m.sb("idx0", [P, 2, TPS], u32)
        emb = m.sb("emb0", [2 * NB, 2, HALF])
        gx = m.sb("gx0", [P, 2, TPS, H])
        h1, h2 = m.sb("h1", [P, HALF]), m.sb("h2", [P, HALF])
        msg = m.sb("msg", [P, TPS, 2 * H])
        hot = m.sb("hot0", [P, TPS, 4, WIN])
        ps_h1, ps_h2 = m.ps("ps_h1", [P, HALF]), m.ps("ps_h2", [P, HALF])
        ps_w = m.ps("ps_w", [P, TPS, H])
        ps_a = m.ps("ps_a", [P, PPS, 4, WIN])
        idx_in, emb_in, landed = m.sems("idx_in", 2), m.sems("emb_in", 2), m.sems("landed", 2)
        used, gate, h1_mm, h1_ok, h2_mm, h2_ok, w_mm, hot_own, msg_ok, sum_mm, acc_own = (m.sem(n) for n in (
            "used", "gate0", "h1_mm", "h1_ok", "h2_mm", "h2_ok", "w_mm", "hot_own", "msg_ok", "sum_mm", "acc_own"))
        src_v = a["src"].bitcast(u32)

        with nc.Block() as block:

            @block.sync
            def _(e):
                for h in range(2):
                    e.dma_start(idx[:, h, :], src_v[:, h * TPS:(h + 1) * TPS]).then_inc(idx_in[h], 16)
                    e.dma_start(emb[:, h, :], dram["emb"][h]).then_inc(emb_in[h], 16)
                with e.Fori(0, STEPS // 2) as i:
                    for h in range(2):
                        e.wait_ge(h1_mm, i * 2 + (h + 1))
                        e.dma_start(emb[:, h, :], dram["emb"][bass.ds(i * 2 + (h + 2), 1)]
                                    .rearrange("s r n -> (s r) n")).then_inc(emb_in[h], 16)
                        e.wait_ge(landed[h], i * (16 * TPS) + 16 * TPS)
                        e.dma_start(idx[:, h, :], src_v[:, bass.ds(i * (2 * TPS) + (h + 2) * TPS, TPS)])\
                            .then_inc(idx_in[h], 16)
                for h in range(2):
                    e.wait_ge(emb_in[h], 16 * (STEPS // 2 + 1))
                    e.wait_ge(idx_in[h], 16 * (STEPS // 2 + 1))

            @block.gpsimd
            def _(e):
                gather_loop(e, idx, idx_in, dram["node0"], gx, landed, used, gate)

            @block.scalar
            def _(e):
                def silu(out, ps, bias, mm, ok, value):
                    e.wait_ge(mm, value)
                    e.activation(out[:], ps[:], ACT.Silu, bias=bias[:]).then_inc(ok, 1)

                silu(h1, ps_h1, w["b0"], h1_mm, h1_ok, 1)
                silu(h2, ps_h2, w["b1"], h2_mm, h2_ok, 1)
                with e.Fori(0, STEPS) as j:
                    silu(h1, ps_h1, w["b0"], h1_mm, h1_ok, j + 2)
                    silu(h2, ps_h2, w["b1"], h2_mm, h2_ok, j + 2)

            @block.tensor
            def _(e):
                def first(h, emb_value, value):
                    e.wait_ge(emb_in[h], emb_value)
                    layer0_mlp1(e, w, emb[:, h, :], ps_h1).then_inc(h1_mm, 1)

                def second(value):
                    e.wait_ge(h1_ok, value)
                    e.matmul(ps_h2[:], w["w1"][:], h1[:], start=True, stop=True).then_inc(h2_mm, 1)

                first(0, 16, 1)
                second(1)
                with e.Fori(0, STEPS // 2) as i:
                    for h in range(2):
                        first(1 - h, i * 16 + 16 * (1 + h), i * 2 + (h + 2))
                        e.wait_ge(h2_ok, i * 2 + (h + 1))
                        layer0_mlp3(e, w, h2, ps_w).then_inc(w_mm, 1)
                        second(i * 2 + (h + 2))
                        e.wait_ge(msg_ok, i * 2 + (h + 1))
                        for p in range(PPS):
                            for lhs, rhs in ((slice(0, H), slice(0, 1)), (slice(H, 2 * H), slice(1, 4))):
                                for t in range(2):
                                    last = e.matmul(ps_a[:, p, rhs, :], msg[:, 2 * p + t, lhs],
                                                    hot[:, 2 * p + t, rhs, :], start=t == 0, stop=t == 1)
                        last.then_inc(sum_mm, 1)

            @block.vector
            def _(e):
                acc = k["acc"][:].rearrange("p (v n) -> p v n", v=4)
                regs = start_registers(e, "sum0")
                e.sem_inc(used, 2)
                with e.Fori(0, STEPS // 2) as i:
                    for h in range(2):
                        j = i * 2 + h
                        tiles = bass.ds(j * TPS, TPS)
                        e.tensor_tensor(hot[:, :, 0, :], spread(k["iota"][:, 0:WIN], 1, TPS),
                                        spread(k["dloc"][:, tiles], 2, WIN), ALU.is_equal).then_inc(hot_own, 1)
                        e.wait_ge(hot_own, j + 1)
                        e.tensor_tensor(hot[:, :, 1:4, :], spread(hot[:, :, 0, :], 2, 3),
                                        spread(w["y"][:, tiles, :], 3, WIN), ALU.mult)
                        e.wait_ge(w_mm, j + 1)
                        e.wait_ge(landed[h], i * (16 * TPS) + 16 * TPS)
                        layer0_messages(e, w, ps_w, gx[:, h], msg).then_inc(msg_ok, 1)
                        e.wait_ge(msg_ok, j + 1)
                        e.sem_inc(used, 1)
                        starts = run_starts(e, k, j, regs)
                        e.wait_ge(sum_mm, j + 1)
                        for p in range(PPS):
                            at = acc[:, :, bass.ds(starts[p], WIN)]
                            if p:
                                e.wait_ge(acc_own, j * PPS + p)
                            e.tensor_tensor(at, at, ps_a[:, p], ALU.add).then_inc(acc_own, 1)
                        e.wait_ge(acc_own, j * PPS + PPS)


class Turns:

    def __init__(self, turn, gate):
        self.turn, self.gate = turn, gate

    def length(self, plan):
        return sum(x[0] * self.length(x[1]) if isinstance(x[0], int) else 1 for x in plan)

    def emit(self, e, name, plan, done=0, index=()):
        for x in plan:
            if isinstance(x[0], int):
                count, body = x
                size = self.length(body)
                with e.Fori(0, count) as r:
                    self.emit(e, name, body, r * size + done, (*index, r))
                done = done + count * size
            else:
                who, work = x
                if who == name:
                    e.wait_ge(self.turn, done + 1)
                    e.sem_inc(self.gate, 1)
                    work(e, index).then_inc(self.turn, 1)
                done = done + 1


def run_if_left(nc, k, m, layer, plan):
    turns = Turns(m.sem("turn"), m.sem("turn_gate"))
    with nc.Block() as block:
        def part(name):
            def run(e):
                flag = e.alloc_register(f"left{layer}_{name}")
                e.load([flag], k["n_left"][0:1, 0:1])
                with e.If_ne(flag, 0):
                    if name == "sync":
                        e.sem_inc(turns.turn, 1)
                    turns.emit(e, name, plan)
            return run
        for name, where in (("sync", block.sync), ("gpsimd", block.gpsimd), ("scalar", block.scalar),
                            ("tensor", block.tensor), ("vector", block.vector)):
            where(part(name))


def arrived(e, sem, value, turn_nop):
    e.wait_ge(sem, value)
    e.sem_inc(turn_nop, 1)
    return e.nop()


def gather_all(e, idx, table, buf, sem):
    for t in range(TPS):
        e.indirect_dma_start(out=buf[:, t, :], out_offset=None, in_=table,
                             in_offset=bass.IndirectOffsetOnAxis(ap=idx[:, t:t + 1], axis=0)).then_inc(sem, 16)


def leftover0(nc, a, k, dram, w):
    with ExitStack() as ctx:
        m = Mem(nc, ctx)
        idx, emb = m.sb("idx_l", [P, TPS], u32), m.sb("emb_l", [2 * NB, HALF])
        gx, msg = m.sb("gx_l", [P, TPS, H]), m.sb("msg_l", [P, TPS, 2 * H])
        h1, h2 = m.sb("h1_l", [P, HALF]), m.sb("h2_l", [P, HALF])
        hot, at_node = m.sb("hot_l", [P, TPS, 4, P]), m.sb("at_node", [P, TPS])
        ps_h, ps_w, ps_a = m.ps("ps_hl", [P, HALF]), m.ps("ps_wl", [P, TPS, H]), m.ps("ps_al", [P, 4, P])
        in_l, gather_l, nop = m.sem("in_l"), m.sem("gather_l"), m.sem("nop_l")
        src_v = a["src"].bitcast(u32)
        acc = k["acc"][:].rearrange("p (v n) -> p v n", v=4)

        def load(e, index):
            j, = index
            e.dma_start(emb[:], dram["emb"][bass.ds(j, 1)].rearrange("s r n -> (s r) n")).then_inc(in_l, 16)
            e.dma_start(idx[:], src_v[:, bass.ds(j * TPS, TPS)]).then_inc(in_l, 16)
            return arrived(e, in_l, j * 32 + 32, nop)

        def gather(e, index):
            gather_all(e, idx, dram["node0"], gx, gather_l)
            return arrived(e, gather_l, index[0] * (16 * TPS) + 16 * TPS, nop)

        def messages(e, index):
            e.tensor_copy(at_node[:], k["left"][:, bass.ds(index[0] * TPS, TPS)])
            return layer0_messages(e, w, ps_w, gx, msg)

        def match(e, index):
            return e.tensor_tensor(hot[:, :, 0, :], spread(k["iota"][:, 0:P], 1, TPS),
                                   spread(at_node[:], 2, P), ALU.is_equal)

        def scale(e, index):
            for c in range(3):
                last = e.tensor_tensor(hot[:, :, 1 + c, :], hot[:, :, 0, :],
                                       spread(w["y"][:, bass.ds(index[0] * TPS, TPS), c], 2, P), ALU.mult)
            return last

        def sums(e, index):
            for cols, kinds in ((slice(0, H), slice(0, 1)), (slice(H, 2 * H), slice(1, 4))):
                for t in range(TPS):
                    last = e.matmul(ps_a[:, kinds, :], msg[:, t, cols], hot[:, t, kinds, :],
                                    start=t == 0, stop=t == TPS - 1)
            return last

        def add(e, index):
            at = acc[:, :, bass.ds(index[1] * P, P)]
            e.tensor_scalar(at_node[:], at_node[:], float(P), None, ALU.subtract)
            return e.tensor_tensor(at, at, ps_a[:], ALU.add)

        run_if_left(nc, k, m, 0, [(STEPS, [
            ("sync", load), ("gpsimd", gather),
            ("tensor", lambda e, _: layer0_mlp1(e, w, emb[:], ps_h)),
            ("scalar", lambda e, _: e.activation(h1[:], ps_h[:], ACT.Silu, bias=w["b0"][:])),
            ("tensor", lambda e, _: e.matmul(ps_h[:], w["w1"][:], h1[:], start=True, stop=True)),
            ("scalar", lambda e, _: e.activation(h2[:], ps_h[:], ACT.Silu, bias=w["b1"][:])),
            ("tensor", lambda e, _: layer0_mlp3(e, w, h2, ps_w)),
            ("vector", messages),
            (NT, [("vector", match), ("vector", scale), ("tensor", sums), ("vector", add)]),
        ])])


def leftover1(nc, k, dram):
    with ExitStack() as ctx:
        m = Mem(nc, ctx)
        idx, idx_q = m.sb("idx_r", [P, TPS], u32), m.sb("idx_rq", [P, TPS], u32)
        gp, gq = m.sb("gp_r", [P, TPS, PW]), m.sb("gq_r", [P, TPS, PW])
        hid, score = m.sb("hid_r", [P, TPS, H]), m.sb("score_r", [P, TPS])
        sc_t = m.sb("sc_tr", [P, TPS, T])
        hot, hot_n = m.sb("hot_r", [P, TPS, T * P]), m.sb("hot_nr", [P, TPS, P])
        at_key, at_node = m.sb("at_key", [P, TPS]), m.sb("at_node_r", [P, TPS])
        ps_g, ps_s = m.ps("ps_gr", [P, T * P]), m.ps("ps_sr", [T, P])
        in_r, gather_r, nop = m.sem("in_r"), m.sem("gather_r"), m.sem("nop_r")

        def load(e, index):
            j, = index
            cols = bass.ds(j * TPS, TPS)
            e.dma_start(idx[:], dram["p_idx"][:, cols]).then_inc(in_r, 16)
            e.dma_start(idx_q[:], dram["q_idx"][:, cols]).then_inc(in_r, 16)
            return arrived(e, in_r, j * 32 + 32, nop)

        def gather(e, index):
            gather_all(e, idx, dram["p_tab"], gp, gather_r)
            gather_all(e, idx_q, dram["q_tab"], gq, gather_r)
            return arrived(e, gather_r, index[0] * (32 * TPS) + 32 * TPS, nop)

        def add_rows(e, index):
            cols = bass.ds(index[0] * TPS, TPS)
            e.tensor_copy(at_node[:], k["left"][:, cols])
            e.scalar_tensor_tensor(at_key[:], k["left"][:, cols], float(T), k["typef"][:, cols], ALU.mult, ALU.add)
            e.tensor_tensor(sc_t[:], spread(k["iota"][:, 0:T], 1, TPS), spread(k["typef"][:, cols], 2, T),
                            ALU.is_equal)
            return e.tensor_tensor(gp[:], gp[:], gq[:], ALU.add)

        def hidden(e, index):
            for t in range(TPS):
                last = e.activation(hid[:, t, :], gp[:, t, 0:H], ACT.Relu, scale=score[:, t:t + 1])
            return last

        def match(e, index):
            e.tensor_tensor(hot_n[:], spread(k["iota"][:, 0:P], 1, TPS), spread(at_node[:], 2, P), ALU.is_equal)
            return e.tensor_tensor(hot[:], spread(k["iota"][:], 1, TPS), spread(at_key[:], 2, T * P), ALU.is_equal)

        def sums(e, index):
            for t in range(TPS):
                e.matmul(ps_g[:], hid[:, t, :], hot[:, t, :], start=t == 0, stop=t == TPS - 1)
            for t in range(TPS):
                last = e.matmul(ps_s[:], sc_t[:, t, :], hot_n[:, t, :], start=t == 0, stop=t == TPS - 1)
            return last

        def add(e, index):
            at = k["acc"][:, bass.ds(index[1] * (T * P), T * P)]
            at_s = k["acc_s"][0:T, bass.ds(index[1] * P, P)]
            e.tensor_scalar(at_node[:], at_node[:], float(P), None, ALU.subtract)
            e.tensor_scalar(at_key[:], at_key[:], float(T * P), None, ALU.subtract)
            e.tensor_tensor(at_s, at_s, ps_s[:], ALU.add)
            return e.tensor_tensor(at, at, ps_g[:], ALU.add)

        run_if_left(nc, k, m, 1, [(STEPS, [
            ("sync", load), ("gpsimd", gather), ("vector", add_rows),
            ("scalar", lambda e, _: e.activation(score[:], gp[:, :, H], ACT.Sigmoid)),
            ("vector", lambda e, _: e.tensor_tensor(sc_t[:], sc_t[:], spread(score[:], 2, T), ALU.mult)),
            ("scalar", hidden),
            (NT, [("vector", match), ("tensor", sums), ("vector", add)]),
        ])])


def between(nc, a, k, dram):
    with ExitStack() as ctx:
        m = Mem(nc, ctx)
        half_n = GRP * P // 2
        out_a, out_b = m.sb("out_a", [P, MUL]), m.sb("out_b", [P, MUL])
        w_out = m.sb("w_out", [P, 4, H])
        w_p, w_q, bias_q = m.sb("w_p", [P, T, PW]), m.sb("w_q", [P, T, PW]), m.sb("bias_q", [P, T, PW])
        att, att_b = m.sb("att", [P, 2, T]), m.sb("att_b", [P, T])
        x_in, x1 = m.sb("x_in1", [P, GRP, H]), m.sb("x1", [P, GRP, H])
        o_t, x1_t = m.sb("o_t", [P, GRP * P]), m.sb("x1_t", [P, GRP * P])
        p_buf, q_buf = m.sb("p_buf", [P, GRP, T * PW]), m.sb("q_buf", [P, GRP, T * PW])
        stats, mv, rstd = m.sb("stats", [P, GRP, 6]), m.sb("mv", [P, GRP, 2]), m.sb("rstd", [P, GRP])
        ps_o, ps_t = m.ps("ps_o", [P, 2, 512]), m.ps("ps_t1", [P, 8, P])
        ps_p, ps_q = m.ps("ps_p", [P, 2, 512]), m.ps("ps_q", [P, 2, 512])
        ld_w, w_clear, w_ok, own_s, x_ld, x_used, o_mm, o_ok, t_mm, sum_ok, var_ok, root_ok, x1_ok = (
            m.sem(n + "_b") for n in ("ld_w", "w_clear", "w_ok", "own", "x_ld", "x_used", "o_mm", "o_ok", "t_mm",
                                      "sum_ok", "var_ok", "root_ok", "x1_ok"))
        gate = m.sem("gate_b")
        t1_mm, t1_ok, p_mm, q_mm, p_ok, q_ok, x1_st, p_st, q_st, z_st = (
            m.sem(n + "_b") for n in ("t1_mm", "t1_ok", "p_mm", "q_mm", "p_ok", "q_ok", "x1_st", "p_st", "q_st", "z_st"))
        x_g = a["x"].rearrange("(t p) f -> p t f", p=P)
        x1_g = dram["x1"].rearrange("(t p) f -> p t f", p=P)
        p_g = dram["p_tab"].rearrange("(t p y) f -> p t (y f)", p=P, y=T)
        q_g = dram["q_tab"][0:NP * T, :].rearrange("(t p y) f -> p t (y f)", p=P, y=T)

        with nc.Block() as block:

            @block.sync
            def _(e):
                for c in range(3):
                    e.dma_start(out_a[MUL * c:MUL * (c + 1), :], a["W_out1"][MUL:2 * MUL, :]).then_inc(ld_w, 16)
                    e.dma_start(out_b[MUL * c:MUL * (c + 1), :], a["W_out0"][MUL:2 * MUL, :]).then_inc(ld_w, 16)
                e.dma_start(out_a[3 * MUL:P, :], a["W_out0"][0:MUL, :]).then_inc(ld_w, 16)
                e.dma_start(out_b[3 * MUL:P, :], a["W_out1"][0:MUL, :]).then_inc(ld_w, 16)
                for part, tab in enumerate((w_p, w_q)):
                    e.dma_start(att[:, part, :], a["attn_wT"][H * part:H * (part + 1), :]).then_inc(ld_w, 16)
                    e.dma_start(tab[:, :, 0:H], a["W1"][:, H * part:H * (part + 1), :]
                                .rearrange("t i o -> i t o")).then_inc(ld_w, 16)
                e.dma_start(bias_q[:, :, 0:H], spread(a["b1"], 0, P)).then_inc(ld_w, 16)
                e.dma_start(att_b[:], a["attn_b"].to_broadcast([P, T])).then_inc(ld_w, 16)
                pad = (NACC - NP) * T
                e.dma_start(dram["q_tab"][NP * T:NACC * T, :], k["zero"][0:pad, 0:PW]).then_inc(z_st, 16)
                for s in (p_st, q_st):
                    e.sem_inc(s, 16)
                with e.Fori(0, NG) as g:
                    rows = bass.ds(g * GRP, GRP)
                    e.wait_ge(x_used, g + 1)
                    e.dma_start(x_in[:], x_g[:, rows, :]).then_inc(x_ld, 16)
                    e.wait_ge(x1_ok, g + 1)
                    e.dma_start(x1_g[:, rows, :], x1[:]).then_inc(x1_st, 16)
                    e.wait_ge(p_ok, g * GRP + GRP)
                    e.dma_start(p_g[:, rows, :], p_buf[:]).then_inc(p_st, 16)
                    e.wait_ge(q_ok, g * GRP + GRP)
                    e.dma_start(q_g[:, rows, :], q_buf[:]).then_inc(q_st, 16)
                for s, v in ((x1_st, NG), (p_st, NG + 1), (q_st, NG + 1), (z_st, 1), (ld_w, 14)):
                    e.wait_ge(s, 16 * v)

            @block.gpsimd
            def _(e):
                e.memset(w_out[:], 0.0).then_inc(w_clear, 1)

            @block.scalar
            def _(e):
                with e.Fori(0, NG) as g:
                    e.wait_ge(o_mm, g + 1)
                    e.activation(o_t[:].rearrange("p (b n) -> p b n", b=2), ps_o[:, :, 0:half_n], ACT.Copy)\
                        .then_inc(o_ok, 1)
                    e.wait_ge(var_ok, g + 1)
                    e.activation(rstd[:], rstd[:], ACT.Sqrt).then_inc(root_ok, 1)
                    e.wait_ge(t1_mm, g + 1)
                    e.activation(x1_t[:].rearrange("p (t n) -> p t n", t=GRP), ps_t[:, 0:GRP, :], ACT.Copy)\
                        .then_inc(t1_ok, 1)
                    for t in range(GRP):
                        e.wait_ge(p_mm, g * GRP + (t + 1))
                        if t == 0:
                            e.wait_ge(p_st, g * 16 + 16)
                        e.activation(p_buf[:, t, :].rearrange("p (b n) -> p b n", b=2), ps_p[:, :, 0:2 * PW],
                                     ACT.Copy).then_inc(p_ok, 1)

            @block.tensor
            def _(e):
                acc = k["acc"][:].rearrange("p (v n) -> p v n", v=4)
                wp, wq = (x[:].rearrange("p t n -> p (t n)") for x in (w_p, w_q))
                e.wait_ge(w_ok, 1)
                with e.Fori(0, NG) as g:
                    for b in range(2):
                        for v in range(4):
                            last = e.matmul(ps_o[:, b, 0:half_n], w_out[:, v, :],
                                            acc[:, v, bass.ds(g * (GRP * P) + b * half_n, half_n)],
                                            start=v == 0, stop=v == 3)
                    last.then_inc(o_mm, 1)
                    e.wait_ge(o_ok, g + 1)
                    for t in range(GRP):
                        last = e.transpose(ps_t[:, t, :], o_t[:, t * P:(t + 1) * P], k["ident"][:])
                    last.then_inc(t_mm, 1)
                    e.wait_ge(x1_ok, g + 1)
                    for t in range(GRP):
                        last = e.transpose(ps_t[:, t, :], x1[:, t, :], k["ident"][:])
                    last.then_inc(t1_mm, 1)
                    e.wait_ge(t1_ok, g + 1)
                    for t in range(GRP):
                        lhs = x1_t[:, t * P:(t + 1) * P]
                        for wt, ps, mm, ok in ((wp, ps_p, p_mm, p_ok), (wq, ps_q, q_mm, q_ok)):
                            if t:
                                e.wait_ge(ok, g * GRP + t)
                            for b in range(2):
                                last = e.matmul(ps[:, b, 0:2 * PW], lhs, wt[:, 2 * PW * b:2 * PW * (b + 1)],
                                                start=True, stop=True)
                            last.then_inc(mm, 1)

            @block.vector
            def _(e):
                own = Own(e, own_s)
                e.wait_ge(ld_w, 16 * 14)
                e.wait_ge(w_clear, 1)
                for c in range(3):
                    rows, vec = slice(MUL * c, MUL * (c + 1)), slice(MUL + c, MUL + c + 3 * (MUL - 1) + 1, 3)
                    e.tensor_copy(w_out[rows, 0, vec], out_a[rows, :])
                    e.tensor_scalar(w_out[rows, 1 + c, 0:MUL], out_b[rows, :], 3.0 ** -0.5, None, ALU.mult)
                    e.tensor_copy(w_out[3 * MUL:P, 1 + c, vec], out_b[3 * MUL:P, :])
                e.tensor_copy(w_out[3 * MUL:P, 0, 0:MUL], out_a[3 * MUL:P, :])
                e.tensor_copy(bias_q[:, :, H], att_b[:])
                e.tensor_copy(w_p[:, :, H], att[:, 0, :])
                e.tensor_copy(w_q[:, :, H], att[:, 1, :]).then_inc(w_ok, 1)
                e.sem_inc(x_used, 1)
                bias = bias_q[:].rearrange("p t n -> p (t n)")
                with e.Fori(0, NG) as g:
                    e.wait_ge(t_mm, g + 1)
                    e.wait_ge(x_ld, g * 16 + 16)
                    e.scalar_tensor_tensor(x1[:], ps_t[:, 0:GRP, :], 1.0 / ((2 * MUL) ** 0.5 * 16.0), x_in[:],
                                           ALU.mult, ALU.add).then_inc(sum_ok, 1)
                    e.wait_ge(sum_ok, g * 4 + 1)
                    e.sem_inc(x_used, 1)
                    norm_stats(e, x1, stats, mv, rstd, sum_ok, g * 4 + 1, var_ok, gate)
                    e.wait_ge(root_ok, g + 1)
                    norm_apply(e, x1, x1, mv, rstd, sum_ok, g * 4 + 4).then_inc(x1_ok, 1)
                    for t in range(GRP):
                        e.wait_ge(q_mm, g * GRP + (t + 1))
                        if t == 0:
                            e.wait_ge(q_st, g * 16 + 16)
                        e.tensor_tensor(q_buf[:, t, :].rearrange("p (b n) -> p b n", b=2), ps_q[:, :, 0:2 * PW],
                                        bias.rearrange("p (b n) -> p b n", b=2), ALU.add).then_inc(q_ok, 1)


def norm_stats(e, x, stats, mv, rstd, own, at, var_ok, gate):
    for t in range(GRP):
        last = e.bn_stats(stats[:, t, :], x[:, t, :])
    last.then_inc(own, 1)
    e.wait_ge(own, at + 1)
    e.sem_inc(gate, 1)
    for t in range(GRP):
        last = e.bn_aggr(mv[:, t, :], stats[:, t, :])
    last.then_inc(own, 1)
    e.wait_ge(own, at + 2)
    e.tensor_scalar(rstd[:], mv[:, :, 1], LN_EPS, None, ALU.add).then_inc(var_ok, 1)


def norm_apply(e, x, out, mv, rstd, own, at):
    e.reciprocal(rstd[:], rstd[:]).then_inc(own, 1)
    e.wait_ge(own, at)
    for t in range(GRP):
        last = e.tensor_scalar(out[:, t, :], x[:, t, :], mv[:, t, 0:1], rstd[:, t:t + 1],
                               ALU.subtract, ALU.mult)
    return last


def clear_sums(nc, k):
    with ExitStack() as ctx:
        with nc.Block() as block:
            half = T * NACC // 2

            @block.vector
            def _(e):
                e.memset(k["acc"][:, 0:half], 0.0)

            @block.gpsimd
            def _(e):
                e.memset(k["acc"][:, half:], 0.0)
                e.memset(k["acc_s"][0:T, :], 0.0)


def edges1(nc, k, dram):
    with ExitStack() as ctx:
        m = Mem(nc, ctx)
        QT = TPS // 2
        idx = m.sb("idx1", [P, 2, TPS], u32)
        gp = m.sb("gp", [P, 2, TPS, PW])
        win = m.sb("win", [P, 2, PPS, PW])
        hot = m.sb("hot1", [P, 2, TPS, P])
        hot_n = m.sb("hot_n", [P, 2, TPS, WIN])
        hot_t = m.sb("hot_t", [P, 2, TPS, T])
        hot_x = m.sb("hot_x", [P, 2, QT, P])
        pre = m.sb("pre", [P, 2, QT, PW])
        hid = m.sb("hid", [P, 2, QT, H])
        score = m.sb("score", [P, 2, QT])
        sc_t = m.sb("sc_t", [P, TPS, T])
        ps_x = m.ps("ps_x", [P, 2, QT, P])
        ps_e = m.ps("ps_e", [P, 2, QT, 2 * P])
        ps_g = m.ps("ps_g", [P, PPS, P])
        ps_s = m.ps("ps_s", [T, PPS, 128])
        idx_in, win_in, landed = m.sems("idx_in1", 2), m.sems("win_in", 2), m.sems("landed1", 2)
        used, gate, hot_ok, x_mm, x_ok, e_mm, pre_ok, score_ok, hid_ok, sc_ok, sum_mm, acc_own, acc_own2 = (
            m.sem(n + "_1") for n in ("used", "gate", "hot_ok", "x_mm", "x_ok", "e_mm", "pre_ok", "score_ok",
                                      "hid_ok", "sc_ok", "sum_mm", "acc_own", "acc_own2"))

        with nc.Block() as block:

            @block.sync
            def _(e):
                regs = start_registers(e, "window")

                def load_windows(j, h):
                    for p, start in enumerate(run_starts(e, k, j, regs)):
                        e.dma_start(win[:, h, p, :], dram["q_tab"][bass.ds(start * T, P), :]).then_inc(win_in[h], 16)

                for h in range(2):
                    e.dma_start(idx[:, h, :], dram["p_idx"][:, h * TPS:(h + 1) * TPS]).then_inc(idx_in[h], 16)
                    load_windows(h, h)
                with e.Fori(0, STEPS // 2) as i:
                    for h in range(2):
                        e.wait_ge(e_mm, i * 4 + (2 * h + 2))
                        load_windows(i * 2 + (h + 2), h)
                        e.wait_ge(landed[h], i * (16 * TPS) + 16 * TPS)
                        e.dma_start(idx[:, h, :], dram["p_idx"][:, bass.ds(i * (2 * TPS) + (h + 2) * TPS, TPS)])\
                            .then_inc(idx_in[h], 16)
                for h in range(2):
                    e.wait_ge(win_in[h], 16 * PPS * (STEPS // 2 + 1))
                    e.wait_ge(idx_in[h], 16 * (STEPS // 2 + 1))

            @block.gpsimd
            def _(e):
                gather_loop(e, idx, idx_in, dram["p_tab"], gp, landed, used, gate)

            @block.scalar
            def _(e):
                with e.Fori(0, STEPS) as j:
                    for q in range(2):
                        e.wait_ge(x_mm, j * 2 + (q + 1))
                        e.activation(hot_x[:, q], ps_x[:, q], ACT.Copy).then_inc(x_ok, 1)
                    for q in range(2):
                        e.wait_ge(pre_ok, j * 2 + (q + 1))
                        e.activation(score[:, q, :], pre[:, q, :, H], ACT.Sigmoid).then_inc(score_ok, 1)
                        e.wait_ge(score_ok, j * 2 + (q + 1))
                        for t in range(QT):
                            last = e.activation(hid[:, q, t, :], pre[:, q, t, 0:H], ACT.Relu,
                                                scale=score[:, q, t:t + 1])
                        last.then_inc(hid_ok, 1)

            @block.tensor
            def _(e):
                with e.Fori(0, STEPS // 2) as i:
                    for h in range(2):
                        j = i * 2 + h
                        e.wait_ge(hot_ok, j + 1)
                        for q in range(2):
                            for t in range(QT):
                                last = e.transpose(ps_x[:, q, t, :], hot[:, h, QT * q + t, :], k["ident"][:])
                            last.then_inc(x_mm, 1)
                        e.wait_ge(win_in[h], i * (16 * PPS) + 16 * PPS)
                        for q in range(2):
                            e.wait_ge(x_ok, i * 4 + (2 * h + q + 1))
                            for t in range(QT):
                                last = e.matmul(ps_e[:, q, t, 0:PW], hot_x[:, q, t, :],
                                                win[:, h, (QT * q + t) // 2, :], start=True, stop=True)
                            last.then_inc(e_mm, 1)
                        for q in range(2):
                            e.wait_ge(hid_ok, i * 4 + (2 * h + q + 1))
                            for p in range(QT // 2):
                                pair = QT // 2 * q + p
                                for t in range(2):
                                    e.matmul(ps_g[:, pair, :], hid[:, q, 2 * p + t, :], hot[:, h, 2 * pair + t, :],
                                             start=t == 0, stop=t == 1)
                            e.wait_ge(sc_ok, i * 4 + (2 * h + q + 1))
                            for p in range(QT // 2):
                                pair = QT // 2 * q + p
                                for t in range(2):
                                    last = e.matmul(ps_s[:, pair, 0:WIN], sc_t[:, 2 * pair + t, :],
                                                    hot_n[:, h, 2 * pair + t, :], start=t == 0, stop=t == 1)
                        last.then_inc(sum_mm, 1)

            @block.vector
            def _(e):
                def one_hot(j, h):
                    tiles = bass.ds(j * TPS, TPS) if not isinstance(j, int) else slice(j * TPS, (j + 1) * TPS)
                    e.tensor_tensor(hot_n[:, h], spread(k["iota"][:, 0:WIN], 1, TPS),
                                    spread(k["dloc"][:, tiles], 2, WIN), ALU.is_equal)
                    e.tensor_tensor(hot_t[:, h], spread(k["iota"][:, 0:T], 1, TPS),
                                    spread(k["typef"][:, tiles], 2, T), ALU.is_equal)
                    e.tensor_tensor(hot[:, h], spread(k["iota"][:, 0:P], 1, TPS),
                                    spread(k["key"][:, tiles], 2, P), ALU.is_equal).then_inc(hot_ok, 1)

                regs = start_registers(e, "sum1")
                e.sem_inc(used, 2)
                one_hot(0, 0)
                with e.Fori(0, STEPS // 2) as i:
                    for h in range(2):
                        j = i * 2 + h
                        one_hot(j + 1, 1 - h)
                        e.wait_ge(landed[h], i * (16 * TPS) + 16 * TPS)
                        for q in range(2):
                            e.wait_ge(e_mm, i * 4 + (2 * h + q + 1))
                            e.tensor_tensor(pre[:, q], ps_e[:, q, :, 0:PW], gp[:, h, QT * q:QT * (q + 1), :],
                                            ALU.add).then_inc(pre_ok, 1)
                        e.wait_ge(pre_ok, i * 4 + (2 * h + 2))
                        e.sem_inc(used, 1)
                        e.wait_ge(hot_ok, j + 1)
                        for q in range(2):
                            e.wait_ge(score_ok, i * 4 + (2 * h + q + 1))
                            mine = slice(QT * q, QT * (q + 1))
                            e.tensor_tensor(sc_t[:, mine, :], hot_t[:, h, mine, :], spread(score[:, q, :], 2, T),
                                            ALU.mult).then_inc(sc_ok, 1)
                        starts = run_starts(e, k, j, regs)
                        e.wait_ge(sum_mm, j + 1)
                        for p in range(PPS):
                            at = k["acc"][:, bass.ds(starts[p] * T, P)]
                            at_s = k["acc_s"][0:T, bass.ds(starts[p], WIN)]
                            if p:
                                e.wait_ge(acc_own, i * (2 * PPS) + (h * PPS + p))
                            e.tensor_tensor(at, at, ps_g[:, p, :], ALU.add).then_inc(acc_own, 1)
                            if p:
                                e.wait_ge(acc_own2, i * (2 * PPS) + (h * PPS + p))
                            e.tensor_tensor(at_s, at_s, ps_s[:, p, 0:WIN], ALU.add).then_inc(acc_own2, 1)
                        e.wait_ge(acc_own, i * (2 * PPS) + (h * PPS + PPS))
                        e.wait_ge(acc_own2, i * (2 * PPS) + (h * PPS + PPS))


def update(nc, a, k, dram, out):
    with ExitStack() as ctx:
        m = Mem(nc, ctx)
        half_n = GRP * P // 2
        w2, b2 = m.sb("w2_1", [P, T, H]), m.sb("b2_1", [T, H])
        w_ih, w_hh = m.sb("w_ih", [P, 3 * H]), m.sb("w_hh", [P, 3 * H])
        bf = m.sb("bf", [6, 4 * H])
        b_hi, b_mid, b_lo = (m.sb(n, [6, 4 * H], bf16) for n in ("bg_hi", "bg_mid", "bg_lo"))
        bias, ones = m.sb("bias_g", [6, 4 * H], bf16), m.sb("ones_g", [6, P], bf16)
        gamma, beta = m.sb("gamma", [P, H]), m.sb("beta", [P, H])
        x1, x1_t, agg_t = m.sb("x1u", [P, GRP, H]), m.sb("x1_tu", [P, GRP * P]), m.sb("agg_t", [P, GRP * P])
        rz, cand, d = m.sb("rz", [P, GRP, 2 * H]), m.sb("cand", [P, GRP, H]), m.sb("d", [P, GRP, H])
        u, y = m.sb("u", [P, GRP, H]), m.sb("yu", [P, GRP, H])
        stats, mv, rstd = m.sb("stats_u", [P, GRP, 6]), m.sb("mv_u", [P, GRP, 2]), m.sb("rstd_u", [P, GRP])
        ps_t, ps_a = m.ps("ps_tu", [P, 8, P]), m.ps("ps_au", [P, 2, 512])
        ps_u = m.ps("ps_u", [P, 4, 512])
        ld_w, clear_b, own_s, split_ok, b_mv, x_ld, x_used, t_mm, t_ok, a_mm, a_ok, u_mm = (
            m.sem(n + "_u") for n in ("ld_w", "clear_b", "own", "split_ok", "b_mv", "x_ld", "x_used", "t_mm",
                                      "t_ok", "a_mm", "a_ok", "u_mm"))
        gate = m.sem("gate_u")
        gate_ok, cand_ok, tanh_ok, step, var_ok, root_ok, out_ok, out_st, r_own, r2_own = (
            m.sem(n + "_u") for n in ("gate_ok", "cand_ok", "tanh_ok", "step", "var_ok", "root_ok", "out_ok",
                                      "out_st", "r_own", "r2_own"))
        x1_g = dram["x1"].rearrange("(t p) f -> p t f", p=P)
        out_g = out.rearrange("(t p) f -> p t f", p=P)

        with nc.Block() as block:

            @block.sync
            def _(e):
                e.wait_ge(clear_b, 1)
                e.dma_start(bf[0:3, 0:3 * H], a["b_ih"].to_broadcast([3, 3 * H])).then_inc(ld_w, 16)
                e.dma_start(bf[3:6, 0:2 * H], a["b_hh"][:, 0:2 * H].to_broadcast([3, 2 * H])).then_inc(ld_w, 16)
                e.dma_start(bf[3:6, 3 * H:4 * H], a["b_hh"][:, 2 * H:3 * H].to_broadcast([3, H])).then_inc(ld_w, 16)
                e.dma_start(w2[:], a["W2"].rearrange("t i o -> i t o")).then_inc(ld_w, 16)
                e.dma_start(b2[:], a["b2"]).then_inc(ld_w, 16)
                e.dma_start(w_ih[:], a["w_ihT"]).then_inc(ld_w, 16)
                e.dma_start(w_hh[:], a["w_hhT"]).then_inc(ld_w, 16)
                e.dma_start(gamma[:], a["gamma"].to_broadcast([P, H])).then_inc(ld_w, 16)
                e.dma_start(beta[:], a["beta"].to_broadcast([P, H])).then_inc(ld_w, 16)
                e.wait_ge(split_ok, 1)
                for r, part in enumerate((b_hi, b_mid, b_lo)):
                    e.dma_start(bias[r:r + 1, :], part[r:r + 1, :]).then_inc(b_mv, 16)
                    e.dma_start(bias[3 + r:4 + r, :], part[3 + r:4 + r, :]).then_inc(b_mv, 16)
                e.sem_inc(out_st, 16)
                with e.Fori(0, NG) as g:
                    rows = bass.ds(g * GRP, GRP)
                    e.wait_ge(x_used, g + 1)
                    e.dma_start(x1[:], x1_g[:, rows, :]).then_inc(x_ld, 16)
                    e.wait_ge(out_ok, g + 1)
                    e.dma_start(out_g[:, rows, :], y[:]).then_inc(out_st, 16)
                e.wait_ge(out_st, 16 * (NG + 1))

            @block.scalar
            def _(e):
                with e.Fori(0, NG) as g:
                    e.wait_ge(t_mm, g + 1)
                    e.activation(x1_t[:].rearrange("p (t n) -> p t n", t=GRP), ps_t[:, 0:GRP, :], ACT.Copy)\
                        .then_inc(t_ok, 1)
                    e.wait_ge(a_mm, g + 1)
                    e.activation(agg_t[:].rearrange("p (b n) -> p b n", b=2), ps_a[:, :, 0:half_n], ACT.Copy)\
                        .then_inc(a_ok, 1)
                    for t in range(GRP):
                        e.wait_ge(u_mm, g * GRP + (t + 1))
                        e.activation(rz[:, t, :], ps_u[:, t % 4, 0:2 * H], ACT.Sigmoid).then_inc(gate_ok, 1)
                    e.wait_ge(cand_ok, g * GRP + GRP)
                    e.activation(cand[:], cand[:], ACT.Tanh).then_inc(tanh_ok, 1)
                    for n in range(2):
                        e.wait_ge(var_ok, g * 2 + (n + 1))
                        e.activation(rstd[:], rstd[:], ACT.Sqrt).then_inc(root_ok, 1)

            @block.tensor
            def _(e):
                acc = k["acc"][:].rearrange("p (n t) -> p t n", t=T)
                e.wait_ge(ld_w, 16 * 9)
                e.wait_ge(b_mv, 16 * 6)
                with e.Fori(0, NG) as g:
                    e.wait_ge(x_ld, g * 16 + 16)
                    for t in range(GRP):
                        last = e.transpose(ps_t[:, t, :], x1[:, t, :], k["ident"][:])
                    last.then_inc(t_mm, 1)
                    for b in range(2):
                        nodes = bass.ds(g * (GRP * P) + b * half_n, half_n)
                        for t in range(T):
                            e.matmul(ps_a[:, b, 0:half_n], w2[:, t, :], acc[:, t, nodes], start=t == 0, stop=False)
                        last = e.matmul(ps_a[:, b, 0:half_n], b2[:], k["acc_s"][0:T, nodes], start=False, stop=True)
                    last.then_inc(a_mm, 1)
                    e.wait_ge(t_ok, g + 1)
                    e.wait_ge(a_ok, g + 1)
                    for t in range(GRP):
                        ps, at = ps_u[:, t % 4, :], slice(t * P, (t + 1) * P)
                        if t >= 4:
                            e.wait_ge(cand_ok, g * GRP + (t - 3))
                        for cols, parts in ((slice(0, 2 * H), ((agg_t, w_ih[:, 0:2 * H]), (x1_t, w_hh[:, 0:2 * H]))),
                                            (slice(2 * H, 3 * H), ((agg_t, w_ih[:, 2 * H:3 * H]),)),
                                            (slice(3 * H, 4 * H), ((x1_t, w_hh[:, 2 * H:3 * H]),))):
                            e.matmul(ps[:, cols], ones[:], bias[:, cols], start=True, stop=False)
                            for lhs, rhs in parts:
                                last = e.matmul(ps[:, cols], lhs[:, at], rhs, start=False, stop=lhs is parts[-1][0])
                        last.then_inc(u_mm, 1)

            @block.vector
            def _(e):
                own = Own(e, own_s)
                e.memset(ones[:], 1.0)
                e.memset(bf[:], 0.0).then_inc(clear_b, 1)
                e.wait_ge(ld_w, 16 * 9)
                split3(e, own, bf[:], b_hi[:], b_mid[:], b_lo[:], bf[:])
                e.sem_inc(split_ok, 1)
                e.sem_inc(x_used, 1)
                SC = 11
                with e.Fori(0, NG) as g:
                    for t in range(GRP):
                        e.wait_ge(gate_ok, g * GRP + (t + 1))
                        e.tensor_tensor(cand[:, t, :], rz[:, t, 0:H], ps_u[:, t % 4, 3 * H:4 * H], ALU.mult)\
                            .then_inc(r_own, 1)
                        e.wait_ge(r_own, g * GRP + (t + 1))
                        e.tensor_tensor(cand[:, t, :], cand[:, t, :], ps_u[:, t % 4, 2 * H:3 * H], ALU.add)\
                            .then_inc(cand_ok, 1)
                    e.wait_ge(tanh_ok, g + 1)
                    n = [0]

                    def then(ins):
                        n[0] += 1
                        ins.then_inc(step, 1)
                        e.wait_ge(step, g * SC + n[0])

                    then(e.tensor_tensor(d[:], x1[:], cand[:], ALU.subtract))
                    then(e.tensor_tensor(d[:], d[:], rz[:, :, H:2 * H], ALU.mult))
                    then(e.tensor_tensor(u[:], x1[:], cand[:], ALU.add))
                    then(e.tensor_tensor(u[:], u[:], d[:], ALU.add))
                    norm_stats(e, u, stats, mv, rstd, step, g * SC + 4, var_ok, gate)
                    e.wait_ge(root_ok, g * 2 + 1)
                    n[0] = 7
                    then(norm_apply(e, u, u, mv, rstd, step, g * SC + 7))
                    then(e.tensor_tensor(u[:], u[:], spread(gamma[:], 1, GRP), ALU.mult))
                    then(e.tensor_tensor(u[:], u[:], spread(beta[:], 1, GRP), ALU.add))
                    then(e.tensor_tensor(u[:], u[:], x1[:], ALU.add))
                    e.sem_inc(x_used, 1)
                    norm_stats(e, u, stats, mv, rstd, r2_own, g * 3, var_ok, gate)
                    e.wait_ge(root_ok, g * 2 + 2)
                    e.wait_ge(out_st, g * 16 + 16)
                    norm_apply(e, u, y, mv, rstd, r2_own, g * 3 + 3).then_inc(out_ok, 1)


_OUTS = [((NP, H), "float32")]


def kernel(**inputs):
    import numpy as np
    import concourse.bacc as bacc
    from concourse.bass_utils import run_bass_kernel_spmd

    arrays = lay_out(np, inputs)
    nc = bacc.Bacc("TRN2", target_bir_lowering=False, num_devices=1)
    aps = {n: nc.dram_tensor(f"in_{n}", v.shape, mybir.dt.from_np(v.dtype), kind="ExternalInput").ap()
           for n, v in arrays.items()}
    out = nc.dram_tensor("out", (NP, H), f32, kind="ExternalOutput").ap()
    build(nc, aps, out)
    r = run_bass_kernel_spmd(nc, [{f"in_{n}": v for n, v in arrays.items()}], core_ids=[0])
    return r.results[0]["out"][0:N]


def lay_out(np, inputs):
    def flat(v, fill, n):
        v = np.asarray(v)
        pad = np.full((n - v.shape[0],) + v.shape[1:], fill, v.dtype)
        return np.concatenate([v, pad])

    def by_partition(v, tiles):
        v = v.reshape(tiles, P, *v.shape[1:]).swapaxes(0, 1)
        return np.ascontiguousarray(v)

    dst = flat(inputs["dst"], N, LTILES * P)
    length = flat(inputs["edge_weight"], 0.0, TILES * P).reshape(ECH // 2, SPC, 2, HALF)
    L0, L1 = "L0_gnn_", "L1_gnn_"
    arrays = {
        "x": flat(inputs["x"], 0.0, NP),
        "src": by_partition(flat(inputs["src"], 0, LTILES * P), LTILES),
        "dst": by_partition(dst, LTILES),
        "type": by_partition(flat(inputs["edge_type_4"], 0, LTILES * P), LTILES),
        "start": dst[::2 * P].reshape(1, LTILES // 2),
        "vec": by_partition(flat(inputs["edge_attr_3"], 0.0, TILES * P), TILES),
        "length": length.transpose(0, 2, 1, 3).reshape(ECH, SPC * HALF),
        "mlp_b0": inputs[L0 + "mlp_b0"].reshape(HID, 1),
        "mlp_b1": inputs[L0 + "mlp_b1"].reshape(HID, 1),
        "mlp_b2": inputs[L0 + "mlp_b2"].reshape(1, P),
        "attn_wT": inputs[L1 + "attn_w"].T,
        "attn_b": inputs[L1 + "attn_b"].reshape(1, T),
        "w_ihT": inputs[L1 + "w_ih"].T,
        "w_hhT": inputs[L1 + "w_hh"].T,
        "b_ih": inputs[L1 + "b_ih"].reshape(1, 3 * H),
        "b_hh": inputs[L1 + "b_hh"].reshape(1, 3 * H),
        "gamma": inputs[L1 + "ln_gamma"].reshape(1, H),
        "beta": inputs[L1 + "ln_beta"].reshape(1, H),
    }
    for n in ("W_up0", "W_up1", "mlp_w0", "mlp_w1", "mlp_w2", "W_out0", "W_out1"):
        arrays[n] = inputs[L0 + n]
    for n in ("W1", "b1", "W2", "b2"):
        arrays[n] = inputs[L1 + n]
    return {n: np.ascontiguousarray(v) for n, v in arrays.items()}
```

```python
import concourse.bass as bass
from concourse import mybir
from concourse.alu_op_type import AluOpType as ALU
from contextlib import ExitStack

P = 128
N = 6250
E = 106250
H = 128
MUL = 32
NB = 8
T = 4
WIN = 32
TPS = 8
PPS = TPS // 2
STEPS = -(-E // (P * TPS))
TILES = STEPS * TPS
LTILES = TILES + 2 * TPS
NT = -(-N // P)
NP = NT * P
NACC = NP + 16
GRP = 7
NG = NT // GRP
PW = H + 1
HID = 64
ECH = 16
SPC = STEPS // (ECH // 2)
HALF = P * TPS // 2
LN_EPS = 1e-5
FAR = 1.0e6

f32, bf16 = mybir.dt.float32, mybir.dt.bfloat16
i32, u32 = mybir.dt.int32, mybir.dt.uint32
ACT = mybir.ActivationFunctionType
AX = mybir.AxisListType


def spread(ap, at, n):
    ap = ap.unsqueeze(at)
    shape = list(ap.shape)
    shape[at] = n
    return ap.to_broadcast(shape)


class Own:

    def __init__(self, eng, sem):
        self.eng, self.sem, self.n = eng, sem, 0

    def did(self, ins):
        self.n += 1
        ins.then_inc(self.sem, 1)
        return self.n

    def then(self, ins):
        self.eng.wait_ge(self.sem, self.did(ins))


class Mem:

    def __init__(self, nc, ctx):
        self.nc, self.ctx = nc, ctx

    def sb(self, name, shape, dt=f32):
        return self.ctx.enter_context(self.nc.sbuf_tensor(name, shape, dt))

    def ps(self, name, shape, dt=f32):
        return self.ctx.enter_context(self.nc.psum_tensor(name, shape, dt))

    def sem(self, name):
        return self.ctx.enter_context(self.nc.semaphore(name))

    def sems(self, name, n):
        return [self.sem(f"{name}{k}") for k in range(n)]


def build(nc, a, out):
    top = ExitStack()
    with top:
        m = Mem(nc, top)
        k = dict(
            acc=m.sb("acc", [P, T * NACC]),
            ident=m.sb("ident", [P, P]),
            iota=m.sb("iota", [P, T * P]),
            key=m.sb("key", [P, LTILES]),
            dloc=m.sb("dloc", [P, LTILES]),
            typef=m.sb("typef", [P, LTILES]),
            left=m.sb("left", [P, LTILES]),
            start=m.sb("start", [1, LTILES // 2], i32),
            n_left=m.sb("n_left", [1, 1], i32),
            zero=m.sb("zero", [P, 512]),
        )
        dram = dict(
            emb=nc.dram_tensor("emb_d", [STEPS + 3, 2 * NB, HALF], f32).ap(),
            node0=nc.dram_tensor("node0_d", [NP, H], f32).ap(),
            p_idx=nc.dram_tensor("p_idx_d", [P, LTILES], u32).ap(),
            q_idx=nc.dram_tensor("q_idx_d", [P, LTILES], u32).ap(),
            x1=nc.dram_tensor("x1_d", [NP, H], f32).ap(),
            p_tab=nc.dram_tensor("p_tab_d", [NP * T, PW], f32).ap(),
            q_tab=nc.dram_tensor("q_tab_d", [NACC * T, PW], f32).ap(),
        )
        with ExitStack() as layer0:
            w = layer0_weights(nc, Mem(nc, layer0))
            prepare(nc, a, k, dram, w)
            edges0(nc, a, k, dram, w)
            leftover0(nc, a, k, dram, w)
        k["acc_s"] = m.sb("acc_s", [P, NACC])
        between(nc, a, k, dram)
        clear_sums(nc, k)
        edges1(nc, k, dram)
        leftover1(nc, k, dram)
        update(nc, a, k, dram, out)


def layer0_weights(nc, m):
    return dict(
        w0=m.sb("w0", [2 * NB, P]), b0=m.sb("b0", [P, 1]),
        w1=m.sb("w1", [P, P]), b1=m.sb("b1", [P, 1]),
        w2=m.sb("w2", [P, 2 * P]),
        b2=m.sb("b2", [3, 2 * P], bf16), ones=m.sb("ones", [3, P], bf16),
        y=m.sb("y", [P, TILES, 3]),
    )


def split3(e, own, src, hi, mid, lo, rest):
    own.then(e.tensor_copy(hi, src))
    own.then(e.tensor_tensor(rest, src, hi, ALU.subtract))
    own.then(e.tensor_copy(mid, rest))
    own.then(e.tensor_tensor(rest, rest, mid, ALU.subtract))
    own.then(e.tensor_copy(lo, rest))


def prepare(nc, a, k, dram, w):
    with ExitStack() as ctx:
        m = Mem(nc, ctx)
        acc = k["acc"]
        cols = SPC * HALF
        emb, mask = acc[:, 0:cols], acc[:, cols:2 * cols]
        vec = acc[:, 2 * cols:2 * cols + 3 * TILES].rearrange("p (t c) -> p t c", c=3)
        vec2 = acc[:, 2 * cols + 3 * TILES:2 * cols + 6 * TILES].rearrange("p (t c) -> p t c", c=3)
        src_i, dst_i, type_i = (m.sb(n, [P, LTILES], i32) for n in ("src_i", "dst_i", "type_i"))
        start_i = m.sb("start_i", [P, LTILES // 2], i32)
        dstf, srcf, hit = (m.sb(n, [P, LTILES]) for n in ("dstf", "srcf", "hit"))
        startf = m.sb("startf", [P, LTILES // 2])
        p_idx, q_idx = m.sb("p_idx", [P, LTILES], u32), m.sb("q_idx", [P, LTILES], u32)
        n_hit, one = m.sb("n_hit", [P, 1]), m.sb("one", [P, 1])
        norm2 = m.sb("norm2", [P, TILES])
        centre_i, centre = m.sb("centre_i", [P, 1], i32), m.sb("centre", [P, 1])
        b2f = m.sb("b2f", [3, P])
        b2_hi, b2_mid, b2_lo = (m.sb(n, [3, P], bf16) for n in ("b2_hi", "b2_mid", "b2_lo"))
        w_up = m.sb("w_up", [P, P])
        x_in = m.sb("x_in", [P, GRP, H])
        x_t = m.sb("x_t", [P, GRP * P])
        tab = m.sb("tab", [P, GRP, H])
        ps_t = m.ps("ps_t", [P, 8, P])
        ps_m = m.ps("ps_m", [P, 8, P])
        ps_n = m.ps("ps_n", [1, 1])
        ld_edge, ld_len, ld_vec, ld_w, ld_up, ld_x, ld_b2 = (m.sem(n) for n in (
            "ld_edge", "ld_len", "ld_vec", "ld_w", "ld_up", "ld_x", "ld_b2"))
        clear_ok, up_clear, w_clear, tab_free, gate = (m.sem(n) for n in (
            "clear_ok", "up_clear", "w_clear", "tab_free", "gate"))
        v_own, s_own, g_own = (m.sem(n) for n in ("v_own", "s_own", "g_own"))
        clip_ok, exp_ok, emb_ok, norm_ok, root_ok, hits_ok, count_ok, idx_ok, split_ok = (m.sem(n) for n in (
            "clip_ok", "exp_ok", "emb_ok", "norm_ok", "root_ok", "hits_ok", "count_ok", "idx_ok", "split_ok"))
        emb_st, stored, tr_ok, xt_ok, mm_ok, tab_ok, tab_st = (m.sem(n) for n in (
            "emb_st", "stored", "tr_ok", "xt_ok", "mm_ok", "tab_ok", "tab_st"))

        with nc.Block() as block:

            @block.sync
            def _(e):
                for q in range(ECH):
                    e.dma_start(emb[NB * q:NB * q + NB, :],
                                a["length"][q:q + 1, :].to_broadcast([NB, cols])).then_inc(ld_len, 16)
                e.dma_start(dst_i[:], a["dst"]).then_inc(ld_edge, 16)
                e.dma_start(start_i[:], a["start"].to_broadcast([P, LTILES // 2])).then_inc(ld_edge, 16)
                e.dma_start(type_i[:], a["type"]).then_inc(ld_edge, 16)
                e.dma_start(src_i[:], a["src"]).then_inc(ld_edge, 16)
                e.dma_start(k["start"][:], a["start"]).then_inc(ld_edge, 16)
                e.dma_start(vec, a["vec"]).then_inc(ld_vec, 16)
                e.wait_ge(emb_ok, 1)
                for g in range(ECH // 2):
                    e.dma_start(dram["emb"][SPC * g:SPC * g + SPC].rearrange("s r n -> r s n"),
                                emb[2 * NB * g:2 * NB * (g + 1), :].rearrange("r (s n) -> r s n", s=SPC))\
                        .then_inc(emb_st, 16)
                e.wait_ge(clear_ok, 1)
                for s in range(3):
                    e.dma_start(dram["emb"][STEPS + s], k["zero"][0:2 * NB, :]).then_inc(stored, 16)
                e.wait_ge(idx_ok, 2)
                e.dma_start(dram["p_idx"], p_idx[:]).then_inc(stored, 16)
                e.dma_start(dram["q_idx"], q_idx[:]).then_inc(stored, 16)
                e.wait_ge(split_ok, 1)
                for r, part in enumerate((b2_hi, b2_mid, b2_lo)):
                    for half in range(2):
                        e.dma_start(w["b2"][r:r + 1, P * half:P * (half + 1)], part[r:r + 1, :])\
                            .then_inc(stored, 16)
                e.wait_ge(stored, 16 * (3 + 2 + 6))
                e.wait_ge(emb_st, 16 * (ECH // 2))

            @block.scalar
            def _(e):
                e.wait_ge(up_clear, 1)
                e.dma_start(w_up[0:MUL, 0:MUL], a["W_up0"]).then_inc(ld_up, 16)
                for c in range(3):
                    e.dma_start(w_up[MUL + c:MUL + c + 3 * (MUL - 1) + 1:3, MUL * (c + 1):MUL * (c + 2)],
                                a["W_up1"]).then_inc(ld_up, 16)
                e.wait_ge(w_clear, 3)
                for half in range(2):
                    lo, hi = HID * half, HID * (half + 1)
                    e.dma_start(w["w0"][NB * half:NB * (half + 1), lo:hi], a["mlp_w0"]).then_inc(ld_w, 16)
                    e.dma_start(w["w1"][lo:hi, lo:hi], a["mlp_w1"]).then_inc(ld_w, 16)
                    e.dma_start(w["w2"][lo:hi, P * half:P * (half + 1)], a["mlp_w2"]).then_inc(ld_w, 16)
                    e.dma_start(w["b0"][lo:hi, :], a["mlp_b0"]).then_inc(ld_w, 16)
                    e.dma_start(w["b1"][lo:hi, :], a["mlp_b1"]).then_inc(ld_w, 16)
                e.dma_start(b2f[:], a["mlp_b2"].to_broadcast([3, P])).then_inc(ld_b2, 16)
                e.wait_ge(clip_ok, 1)
                e.activation(emb, emb, ACT.Square, bias=centre[:], scale=float(NB - 1)).then_inc(s_own, 1)
                e.wait_ge(s_own, 1)
                e.activation(emb, emb, ACT.Exp, scale=-0.5).then_inc(exp_ok, 1)
                e.wait_ge(norm_ok, 1)
                e.activation(norm2[:], norm2[:], ACT.Sqrt).then_inc(root_ok, 1)
                with e.Fori(0, NG) as g:
                    e.wait_ge(mm_ok, g + 1)
                    e.wait_ge(tab_free, g + 1)
                    e.activation(tab[:], ps_m[:, 0:GRP, :], ACT.Copy, scale=float(MUL) ** -0.5)\
                        .then_inc(tab_ok, 1)
                e.wait_ge(ld_w, 16 * 10)

            @block.gpsimd
            def _(e):
                own = Own(e, g_own)
                e.memset(w_up[:], 0.0).then_inc(up_clear, 1)
                own.then(e.memset(k["ident"][:], 0.0))
                own.then(e.affine_select(out=k["ident"][:], in_=k["ident"][:], compare_op=ALU.not_equal,
                                         fill=1.0, base=0, pattern=[[-1, P]], channel_multiplier=1))
                own.then(e.iota(centre_i[:], pattern=[[0, 1]], base=0, channel_multiplier=1))
                e.iota(k["iota"][:], pattern=[[1, T * P]], base=0, channel_multiplier=0,
                       allow_small_or_imprecise_dtypes=True)
                e.memset(w["w0"][:], 0.0).then_inc(w_clear, 1)
                e.memset(w["w1"][:], 0.0).then_inc(w_clear, 1)
                e.memset(w["w2"][:], 0.0).then_inc(w_clear, 1)
                e.memset(k["zero"][:], 0.0).then_inc(clear_ok, 1)
                x_g = a["x"].rearrange("(t p) f -> p t f", p=P)
                node0_g = dram["node0"].rearrange("(t p) f -> p t f", p=P)
                e.sem_inc(tab_free, 1)
                with e.Fori(0, NG) as g:
                    e.wait_ge(tr_ok, g + 1)
                    e.sem_inc(gate, 1)
                    e.dma_start(x_in[:], x_g[:, bass.ds(g * GRP, GRP), :]).then_inc(ld_x, 16)
                    e.wait_ge(tab_ok, g + 1)
                    e.sem_inc(gate, 1)
                    e.dma_start(node0_g[:, bass.ds(g * GRP, GRP), :], tab[:]).then_inc(tab_st, 16)
                    e.wait_ge(tab_st, g * 16 + 16)
                    e.sem_inc(tab_free, 1)

            @block.vector
            def _(e):
                own = Own(e, v_own)
                e.wait_ge(g_own, 3)
                own.then(e.tensor_scalar(centre_i[:], centre_i[:], NB - 1, None, ALU.bitwise_and))
                own.then(e.tensor_scalar(centre[:], centre_i[:], -1.0, None, ALU.mult))
                e.wait_ge(ld_len, 16 * ECH)
                own.did(e.tensor_scalar(mask, emb, 1.0, float(NB) ** 0.5, ALU.is_le, ALU.mult))
                e.wait_ge(v_own, own.n)
                e.tensor_scalar(emb, emb, 0.0, 1.0, ALU.max, ALU.min).then_inc(clip_ok, 1)
                e.wait_ge(ld_vec, 16)
                own.then(e.tensor_tensor(vec2, vec, vec, ALU.mult))
                e.tensor_reduce(norm2[:], vec2, AX.X, ALU.add).then_inc(norm_ok, 1)
                e.wait_ge(ld_edge, 16 * 5)
                own.did(e.tensor_copy(dstf[:], dst_i[:]))
                own.did(e.tensor_copy(startf[:], start_i[:]))
                own.did(e.tensor_copy(k["typef"][:], type_i[:]))
                own.then(e.tensor_copy(srcf[:], src_i[:]))
                pairs = "p (g t) -> p g t"
                own.did(e.scalar_tensor_tensor(p_idx[:], srcf[:], float(T), k["typef"][:], ALU.mult, ALU.add))
                own.did(e.scalar_tensor_tensor(q_idx[:], dstf[:], float(T), k["typef"][:], ALU.mult, ALU.add))
                own.then(e.tensor_tensor(k["dloc"][:].rearrange(pairs, t=2), dstf[:].rearrange(pairs, t=2),
                                         spread(startf[:], 2, 2), ALU.subtract))
                e.sem_inc(idx_ok, 2)
                own.did(e.scalar_tensor_tensor(k["key"][:], k["dloc"][:], float(T), k["typef"][:],
                                               ALU.mult, ALU.add))
                own.then(e.tensor_scalar(hit[:], k["dloc"][:], 0.0, None, ALU.is_ge))
                own.then(e.scalar_tensor_tensor(hit[:], k["dloc"][:], float(WIN), hit[:], ALU.is_lt, ALU.mult))
                own.did(e.scalar_tensor_tensor(k["left"][:], hit[:], -FAR, dstf[:], ALU.mult, ALU.add))
                own.did(e.memset(one[:], 1.0))
                e.memset(w["ones"][:], 1.0)
                e.tensor_reduce(n_hit[:], hit[:, 0:TILES], AX.X, ALU.add).then_inc(hits_ok, 1)
                e.wait_ge(root_ok, 1)
                own.then(e.tensor_scalar(norm2[:], norm2[:], 1e-12, None, ALU.add))
                own.then(e.reciprocal(norm2[:], norm2[:]))
                own.then(e.tensor_scalar(norm2[:], norm2[:], 3.0 ** 0.5, None, ALU.mult))
                own.did(e.tensor_tensor(w["y"][:], vec, spread(norm2[:], 2, 3), ALU.mult))
                e.wait_ge(count_ok, 1)
                own.did(e.tensor_scalar(k["n_left"][:], ps_n[:], -1.0, float(P * TILES), ALU.mult, ALU.add))
                e.wait_ge(exp_ok, 1)
                e.tensor_tensor(emb, emb, mask, ALU.mult).then_inc(emb_ok, 1)
                e.wait_ge(ld_b2, 16)
                split3(e, own, b2f[:], b2_hi[:], b2_mid[:], b2_lo[:], b2f[:])
                e.sem_inc(split_ok, 1)
                with e.Fori(0, NG) as g:
                    e.wait_ge(tr_ok, g + 2)
                    e.tensor_copy(x_t[:].rearrange("p (t n) -> p t n", t=GRP), ps_t[:, 0:GRP, :])\
                        .then_inc(xt_ok, 1)
                e.wait_ge(emb_st, 16 * (ECH // 2))
                e.wait_ge(v_own, own.n)
                e.wait_ge(emb_ok, 1)
                e.memset(acc[:], 0.0)

            @block.tensor
            def _(e):
                e.wait_ge(hits_ok, 1)
                e.matmul(ps_n[:], n_hit[:], one[:], start=True, stop=True).then_inc(count_ok, 1)
                e.wait_ge(g_own, 2)
                e.wait_ge(ld_up, 16 * 4)
                e.sem_inc(tr_ok, 1)
                with e.Fori(0, NG) as g:
                    e.wait_ge(ld_x, g * 16 + 16)
                    for t in range(GRP):
                        last = e.transpose(ps_t[:, t, :], x_in[:, t, :], k["ident"][:])
                    last.then_inc(tr_ok, 1)
                    e.wait_ge(xt_ok, g + 1)
                    for t in range(GRP):
                        last = e.matmul(ps_m[:, t, :], x_t[:, t * P:(t + 1) * P], w_up[:], start=True, stop=True)
                    last.then_inc(mm_ok, 1)


def start_registers(e, tag):
    return [e.alloc_register(f"{tag}_start{p}") for p in range(PPS)]


def run_starts(e, k, j, regs):
    e.load(regs, k["start"][0:1, bass.ds(j * PPS, PPS)])
    return [e.snap(r, min_val=0, max_val=N) for r in regs]


def gather_loop(e, idx, idx_in, table, buf, landed, used, gate):
    with e.Fori(0, STEPS // 2) as i:
        for h in range(2):
            e.wait_ge(idx_in[h], i * 16 + 16)
            e.sem_inc(gate, 1)
            e.wait_ge(used, i * 2 + (h + 1))
            e.sem_inc(gate, 1)
            for t in range(TPS):
                e.indirect_dma_start(
                    out=buf[:, h, t, :], out_offset=None, in_=table,
                    in_offset=bass.IndirectOffsetOnAxis(ap=idx[:, h, t:t + 1], axis=0),
                ).then_inc(landed[h], 16)


def tiles_of(x):
    return x.rearrange("p t (i m) -> p t i m", m=MUL)


def upper(x):
    return x.bitcast(bf16).rearrange("p (n two) -> p n two", two=2)[:, :, 1]


def layer0_mlp1(e, w, emb, ps_h):
    return e.matmul(ps_h[:], w["w0"][:], emb, start=True, stop=True)


def layer0_mlp3(e, w, h2, ps_w):
    for t in range(PPS):
        ps = ps_w[:, 2 * t:2 * t + 2, :]
        e.matmul(ps, w["ones"][:], w["b2"][:], start=True, stop=False)
        last = e.matmul(ps, h2[:, t * P:(t + 1) * P], w["w2"][:], start=False, stop=True)
    return last


class Messages:

    def __init__(self, m, tag=""):
        self.msg = m.sb("msg" + tag, [P, 2, TPS * H])
        self.rest = m.sb("rest" + tag, [P, 2, TPS * H])
        self.low = m.sb("low" + tag, [P, 2, TPS * H], bf16)
        self.ws = m.sb("ws" + tag, [P, TPS, MUL])
        self.vy = m.sb("vy" + tag, [P, TPS, 3, MUL])
        self.cols = [self.msg[:, b, :].rearrange("p (t i m) -> p t i m", t=TPS, m=MUL) for b in range(2)]

    def ws_product(self, e, wt, s):
        return e.tensor_tensor(self.ws[:], wt[:, :, 1, :], s, ALU.mult)

    def vy_product(self, e, v, y):
        return e.tensor_tensor(self.vy[:], v, spread(y, 3, MUL), ALU.mult)

    def w0_product(self, e, wt, s):
        return e.tensor_tensor(self.cols[0][:, :, 3, :], wt[:, :, 0, :], s, ALU.mult)

    def w2_product(self, e, wt, v):
        return e.tensor_tensor(self.cols[0][:, :, 0:3, :], spread(wt[:, :, 2, :], 2, 3), v, ALU.mult)

    def dot_sum(self, e, c):
        return e.tensor_tensor(self.vy[:, :, 0, :], self.vy[:, :, 0, :], self.vy[:, :, c, :], ALU.add)

    def w3_product(self, e, wt):
        return e.tensor_tensor(self.cols[1][:, :, 3, :], wt[:, :, 3, :], self.vy[:, :, 0, :], ALU.mult)

    def by_component(self, e, tile, y):
        for c in range(3):
            last = e.activation(self.cols[1][:, tile, c, :], self.ws[:, tile, :], ACT.Copy, scale=y[:, c:c + 1])
        return last

    def split_rest(self, e, b):
        return e.tensor_tensor(self.rest[:, b, :], self.msg[:, b, :], upper(self.msg[:, b, :]), ALU.subtract)

    def split_low(self, e, b):
        return e.tensor_tensor(self.low[:, b, :], self.rest[:, b, :], upper(self.rest[:, b, :]), ALU.subtract)

    def parts(self, tile, b):
        at = slice(tile * H, (tile + 1) * H)
        return [upper(self.msg[:, b, at]), upper(self.rest[:, b, at]), self.low[:, b, at]]


def edges0(nc, a, k, dram, w):
    with ExitStack() as ctx:
        m = Mem(nc, ctx)
        idx = m.sb("idx0", [P, 2, TPS], u32)
        emb = m.sb("emb0", [2 * NB, 2, HALF])
        gx = m.sb("gx0", [P, 2, TPS, H])
        h1, h2 = m.sb("h1", [P, HALF]), m.sb("h2", [P, HALF])
        msgs = [Messages(m, str(h)) for h in range(2)]
        hot = m.sb("hot0", [P, 2, TPS, WIN], bf16)
        ps_h1, ps_h2 = m.ps("ps_h1", [P, HALF]), m.ps("ps_h2", [P, HALF])
        ps_w = m.ps("ps_w", [P, 2, TPS, H])
        ps_a = m.ps("ps_a", [P, 2, 2 * PPS, 2, WIN])
        idx_in, emb_in, landed = m.sems("idx_in", 2), m.sems("emb_in", 2), m.sems("landed", 2)
        used, gate, h1_mm, h1_ok, h2_mm, h2_ok, w_mm, plain_ok, ws_ok, y_ok, own, msg_ok, sum_mm, acc_own = (
            m.sem(n) for n in ("used", "gate0", "h1_mm", "h1_ok", "h2_mm", "h2_ok", "w_mm", "plain_ok", "ws_ok",
                               "y_ok", "own0", "msg_ok", "sum_mm", "acc_own"))
        src_v = a["src"].bitcast(u32)

        with nc.Block() as block:

            @block.sync
            def _(e):
                for h in range(2):
                    e.dma_start(idx[:, h, :], src_v[:, h * TPS:(h + 1) * TPS]).then_inc(idx_in[h], 16)
                    e.dma_start(emb[:, h, :], dram["emb"][h]).then_inc(emb_in[h], 16)
                with e.Fori(0, STEPS // 2) as i:
                    for h in range(2):
                        e.wait_ge(h1_mm, i * 2 + (h + 1))
                        e.dma_start(emb[:, h, :], dram["emb"][bass.ds(i * 2 + (h + 2), 1)]
                                    .rearrange("s r n -> (s r) n")).then_inc(emb_in[h], 16)
                        e.wait_ge(landed[h], i * (16 * TPS) + 16 * TPS)
                        e.dma_start(idx[:, h, :], src_v[:, bass.ds(i * (2 * TPS) + (h + 2) * TPS, TPS)])\
                            .then_inc(idx_in[h], 16)
                e.wait_ge(h1_mm, STEPS + 1)
                e.dma_start(emb[:, 0, :], dram["emb"][STEPS + 2]).then_inc(emb_in[0], 16)
                for h in range(2):
                    e.wait_ge(emb_in[h], 16 * (STEPS // 2 + 2 - h))
                    e.wait_ge(idx_in[h], 16 * (STEPS // 2 + 1))

            @block.gpsimd
            def _(e):
                gather_loop(e, idx, idx_in, dram["node0"], gx, landed, used, gate)

            @block.scalar
            def _(e):
                def silu(out, ps, bias, mm, ok, value):
                    e.wait_ge(mm, value)
                    e.activation(out[:], ps[:], ACT.Silu, bias=bias[:]).then_inc(ok, 1)

                e.preload_act_table(ACT.Silu)
                for n in range(2):
                    silu(h1, ps_h1, w["b0"], h1_mm, h1_ok, n + 1)
                    silu(h2, ps_h2, w["b1"], h2_mm, h2_ok, n + 1)
                silu(h1, ps_h1, w["b0"], h1_mm, h1_ok, 3)
                with e.Fori(0, STEPS // 2) as i:
                    for h in range(2):
                        e.wait_ge(ws_ok, i * 2 + (h + 1))
                        for t in range(TPS):
                            last = msgs[h].by_component(e, t, w["y"][:, bass.ds(i * (2 * TPS) + (h * TPS + t), 1), :]
                                                        .rearrange("p t c -> p (t c)"))
                        last.then_inc(y_ok, 1)
                        silu(h2, ps_h2, w["b1"], h2_mm, h2_ok, i * 2 + (h + 3))
                        silu(h1, ps_h1, w["b0"], h1_mm, h1_ok, i * 2 + (h + 4))

            @block.tensor
            def _(e):
                def first(h, emb_value):
                    e.wait_ge(emb_in[h], emb_value)
                    layer0_mlp1(e, w, emb[:, h, :], ps_h1).then_inc(h1_mm, 1)

                def second(value):
                    e.wait_ge(h1_ok, value)
                    e.matmul(ps_h2[:], w["w1"][:], h1[:], start=True, stop=True).then_inc(h2_mm, 1)

                def third(h, value):
                    e.wait_ge(h2_ok, value)
                    layer0_mlp3(e, w, h2, ps_w[:, h]).then_inc(w_mm, 1)

                first(0, 16)
                second(1)
                first(1, 16)
                third(0, 1)
                second(2)
                first(0, 32)
                e.sem_inc(plain_ok, 1)
                with e.Fori(0, STEPS // 2) as i:
                    for h in range(2):
                        e.wait_ge(plain_ok, i * 2 + (h + 1))
                        third(1 - h, i * 2 + (h + 2))
                        second(i * 2 + (h + 3))
                        first(1 - h, i * 16 + (32 + 16 * h))
                        e.wait_ge(msg_ok, i * 2 + (h + 1))
                        for p in range(PPS):
                            for b in range(2):
                                for t in range(2):
                                    for n, part in enumerate(msgs[h].parts(2 * p + t, b)):
                                        last = e.matmul(ps_a[:, h, p, b, :], part, hot[:, h, 2 * p + t, :],
                                                        start=t + n == 0, stop=t + n == 3)
                        last.then_inc(sum_mm, 1)

            @block.vector
            def _(e):
                acc = k["acc"][:, 0:2 * NACC].rearrange("p (b n) -> p b n", b=2)
                regs = start_registers(e, "sum0")

                def messages(i, h, before):
                    j = i * 2 + h
                    tiles = bass.ds(j * TPS, TPS)
                    wt, x, mine = tiles_of(ps_w[:, h]), tiles_of(gx[:, h]), msgs[h]
                    s, v, y = x[:, :, 0, :], x[:, :, 1:4, :], w["y"][:, tiles, :]
                    done = [0]

                    def did(ins):
                        ins.then_inc(own, 1)
                        done[0] += 1
                        return j * OWN + done[0]

                    add = (lambda p: None) if not before else start_windows(j - 1, 1 - h)
                    e.tensor_tensor(hot[:, h], spread(k["iota"][:, 0:WIN], 1, TPS),
                                    spread(k["dloc"][:, tiles], 2, WIN), ALU.is_equal)
                    e.wait_ge(landed[h], i * (16 * TPS) + 16 * TPS)
                    e.wait_ge(w_mm, j + 1)
                    mine.ws_product(e, wt, s).then_inc(ws_ok, 1)
                    vy = did(mine.vy_product(e, v, y))
                    w0 = did(mine.w0_product(e, wt, s))
                    e.wait_ge(own, vy)
                    sum_1 = did(mine.dot_sum(e, 1))
                    w2 = did(mine.w2_product(e, wt, v))
                    e.wait_ge(own, sum_1)
                    sum_2 = did(mine.dot_sum(e, 2))
                    add(0)
                    e.wait_ge(own, w2)
                    e.sem_inc(used, 1)
                    rest = did(mine.split_rest(e, 0))
                    e.wait_ge(own, sum_2)
                    mine.w3_product(e, wt).then_inc(plain_ok, 1)
                    add(1)
                    e.wait_ge(own, rest)
                    mine.split_low(e, 0)
                    add(2)
                    e.wait_ge(y_ok, j + 1)
                    e.wait_ge(plain_ok, j + 2)
                    rest = did(mine.split_rest(e, 1))
                    add(3)
                    e.wait_ge(own, rest)
                    mine.split_low(e, 1).then_inc(msg_ok, 1)
                    assert done[0] == OWN and PPS == 4

                def start_windows(j, h):
                    starts = run_starts(e, k, j, regs)

                    def add(p):
                        at = acc[:, :, bass.ds(starts[p], WIN)]
                        e.wait_ge(sum_mm, j + 1)
                        e.wait_ge(acc_own, j * PPS + (p + 1))
                        e.tensor_tensor(at, at, ps_a[:, h, p], ALU.add).then_inc(acc_own, 1)
                    return add

                OWN = 7
                e.sem_inc(used, 2)
                e.sem_inc(acc_own, 1)
                messages(0, 0, False)
                with e.Fori(0, STEPS // 2 - 1) as i:
                    messages(i, 1, True)
                    messages(i + 1, 0, True)
                messages(STEPS // 2 - 1, 1, True)
                add = start_windows(STEPS - 1, 1)
                for p in range(PPS):
                    add(p)
                e.wait_ge(acc_own, STEPS * PPS + 1)


class Turns:

    def __init__(self, turn, gate):
        self.turn, self.gate = turn, gate

    def length(self, plan):
        return sum(x[0] * self.length(x[1]) if isinstance(x[0], int) else 1 for x in plan)

    def emit(self, e, name, plan, done=0, index=()):
        for x in plan:
            if isinstance(x[0], int):
                count, body = x
                size = self.length(body)
                with e.Fori(0, count) as r:
                    self.emit(e, name, body, r * size + done, (*index, r))
                done = done + count * size
            else:
                who, work = x
                if who == name:
                    e.wait_ge(self.turn, done + 1)
                    e.sem_inc(self.gate, 1)
                    work(e, index).then_inc(self.turn, 1)
                done = done + 1


def run_if_left(nc, k, m, layer, plan):
    turns = Turns(m.sem("turn"), m.sem("turn_gate"))
    with nc.Block() as block:
        def part(name):
            def run(e):
                flag = e.alloc_register(f"left{layer}_{name}")
                e.load([flag], k["n_left"][0:1, 0:1])
                with e.If_ne(flag, 0):
                    if name == "sync":
                        e.sem_inc(turns.turn, 1)
                    turns.emit(e, name, plan)
            return run
        for name, where in (("sync", block.sync), ("gpsimd", block.gpsimd), ("scalar", block.scalar),
                            ("tensor", block.tensor), ("vector", block.vector)):
            where(part(name))


def arrived(e, sem, value, turn_nop):
    e.wait_ge(sem, value)
    e.sem_inc(turn_nop, 1)
    return e.nop()


def gather_all(e, idx, table, buf, sem):
    for t in range(TPS):
        e.indirect_dma_start(out=buf[:, t, :], out_offset=None, in_=table,
                             in_offset=bass.IndirectOffsetOnAxis(ap=idx[:, t:t + 1], axis=0)).then_inc(sem, 16)


def leftover0(nc, a, k, dram, w):
    with ExitStack() as ctx:
        m = Mem(nc, ctx)
        idx, emb = m.sb("idx_l", [P, TPS], u32), m.sb("emb_l", [2 * NB, HALF])
        gx, msgs = m.sb("gx_l", [P, TPS, H]), Messages(m, "_l")
        h1, h2 = m.sb("h1_l", [P, HALF]), m.sb("h2_l", [P, HALF])
        hot, at_node = m.sb("hot_l", [P, TPS, P], bf16), m.sb("at_node", [P, TPS])
        ps_h, ps_w, ps_a = m.ps("ps_hl", [P, HALF]), m.ps("ps_wl", [P, TPS, H]), m.ps("ps_al", [P, 2, P])
        in_l, gather_l, nop = m.sem("in_l"), m.sem("gather_l"), m.sem("nop_l")
        src_v = a["src"].bitcast(u32)
        acc = k["acc"][:, 0:2 * NACC].rearrange("p (b n) -> p b n", b=2)
        wt, x = tiles_of(ps_w[:]), tiles_of(gx[:])

        def load(e, index):
            j, = index
            e.dma_start(emb[:], dram["emb"][bass.ds(j, 1)].rearrange("s r n -> (s r) n")).then_inc(in_l, 16)
            e.dma_start(idx[:], src_v[:, bass.ds(j * TPS, TPS)]).then_inc(in_l, 16)
            return arrived(e, in_l, j * 32 + 32, nop)

        def gather(e, index):
            gather_all(e, idx, dram["node0"], gx, gather_l)
            return arrived(e, gather_l, index[0] * (16 * TPS) + 16 * TPS, nop)

        def messages(e, index):
            e.tensor_copy(at_node[:], k["left"][:, bass.ds(index[0] * TPS, TPS)])
            msgs.ws_product(e, wt, x[:, :, 0, :])
            msgs.w0_product(e, wt, x[:, :, 0, :])
            msgs.w2_product(e, wt, x[:, :, 1:4, :])
            return msgs.vy_product(e, x[:, :, 1:4, :], w["y"][:, bass.ds(index[0] * TPS, TPS), :])

        def by_component(e, index):
            for t in range(TPS):
                last = msgs.by_component(e, t, w["y"][:, bass.ds(index[0] * TPS + t, 1), :]
                                         .rearrange("p t c -> p (t c)"))
            return last

        def both(split):
            def work(e, index):
                split(e, 0)
                return split(e, 1)
            return work

        def match(e, index):
            return e.tensor_tensor(hot[:], spread(k["iota"][:, 0:P], 1, TPS), spread(at_node[:], 2, P),
                                   ALU.is_equal)

        def sums(e, index):
            for b in range(2):
                for t in range(TPS):
                    for n, part in enumerate(msgs.parts(t, b)):
                        last = e.matmul(ps_a[:, b, :], part, hot[:, t, :], start=t + n == 0,
                                        stop=t + n == TPS + 1)
            return last

        def add(e, index):
            at = acc[:, :, bass.ds(index[1] * P, P)]
            e.tensor_scalar(at_node[:], at_node[:], float(P), None, ALU.subtract)
            return e.tensor_tensor(at, at, ps_a[:], ALU.add)

        run_if_left(nc, k, m, 0, [(STEPS, [
            ("sync", load), ("gpsimd", gather),
            ("tensor", lambda e, _: layer0_mlp1(e, w, emb[:], ps_h)),
            ("scalar", lambda e, _: e.activation(h1[:], ps_h[:], ACT.Silu, bias=w["b0"][:])),
            ("tensor", lambda e, _: e.matmul(ps_h[:], w["w1"][:], h1[:], start=True, stop=True)),
            ("scalar", lambda e, _: e.activation(h2[:], ps_h[:], ACT.Silu, bias=w["b1"][:])),
            ("tensor", lambda e, _: layer0_mlp3(e, w, h2, ps_w)),
            ("vector", messages), ("scalar", by_component),
            ("vector", lambda e, _: msgs.dot_sum(e, 1)), ("vector", lambda e, _: msgs.dot_sum(e, 2)),
            ("vector", lambda e, _: msgs.w3_product(e, wt)),
            ("vector", both(msgs.split_rest)), ("vector", both(msgs.split_low)),
            (NT, [("vector", match), ("tensor", sums), ("vector", add)]),
        ])])


def leftover1(nc, k, dram):
    with ExitStack() as ctx:
        m = Mem(nc, ctx)
        idx, idx_q = m.sb("idx_r", [P, TPS], u32), m.sb("idx_rq", [P, TPS], u32)
        gp, gq = m.sb("gp_r", [P, TPS, PW]), m.sb("gq_r", [P, TPS, PW])
        hid, score = m.sb("hid_r", [P, TPS, H]), m.sb("score_r", [P, TPS])
        sc_t = m.sb("sc_tr", [P, TPS, T])
        hot, hot_n = m.sb("hot_r", [P, TPS, T * P]), m.sb("hot_nr", [P, TPS, P])
        at_key, at_node = m.sb("at_key", [P, TPS]), m.sb("at_node_r", [P, TPS])
        ps_g, ps_s = m.ps("ps_gr", [P, T * P]), m.ps("ps_sr", [T, P])
        in_r, gather_r, nop = m.sem("in_r"), m.sem("gather_r"), m.sem("nop_r")

        def load(e, index):
            j, = index
            cols = bass.ds(j * TPS, TPS)
            e.dma_start(idx[:], dram["p_idx"][:, cols]).then_inc(in_r, 16)
            e.dma_start(idx_q[:], dram["q_idx"][:, cols]).then_inc(in_r, 16)
            return arrived(e, in_r, j * 32 + 32, nop)

        def gather(e, index):
            gather_all(e, idx, dram["p_tab"], gp, gather_r)
            gather_all(e, idx_q, dram["q_tab"], gq, gather_r)
            return arrived(e, gather_r, index[0] * (32 * TPS) + 32 * TPS, nop)

        def add_rows(e, index):
            cols = bass.ds(index[0] * TPS, TPS)
            e.tensor_copy(at_node[:], k["left"][:, cols])
            e.scalar_tensor_tensor(at_key[:], k["left"][:, cols], float(T), k["typef"][:, cols], ALU.mult, ALU.add)
            e.tensor_tensor(sc_t[:], spread(k["iota"][:, 0:T], 1, TPS), spread(k["typef"][:, cols], 2, T),
                            ALU.is_equal)
            return e.tensor_tensor(gp[:], gp[:], gq[:], ALU.add)

        def hidden(e, index):
            for t in range(TPS):
                last = e.activation(hid[:, t, :], gp[:, t, 0:H], ACT.Relu, scale=score[:, t:t + 1])
            return last

        def match(e, index):
            e.tensor_tensor(hot_n[:], spread(k["iota"][:, 0:P], 1, TPS), spread(at_node[:], 2, P), ALU.is_equal)
            return e.tensor_tensor(hot[:], spread(k["iota"][:], 1, TPS), spread(at_key[:], 2, T * P), ALU.is_equal)

        def sums(e, index):
            for t in range(TPS):
                e.matmul(ps_g[:], hid[:, t, :], hot[:, t, :], start=t == 0, stop=t == TPS - 1)
            for t in range(TPS):
                last = e.matmul(ps_s[:], sc_t[:, t, :], hot_n[:, t, :], start=t == 0, stop=t == TPS - 1)
            return last

        def add(e, index):
            at = k["acc"][:, bass.ds(index[1] * (T * P), T * P)]
            at_s = k["acc_s"][0:T, bass.ds(index[1] * P, P)]
            e.tensor_scalar(at_node[:], at_node[:], float(P), None, ALU.subtract)
            e.tensor_scalar(at_key[:], at_key[:], float(T * P), None, ALU.subtract)
            e.tensor_tensor(at_s, at_s, ps_s[:], ALU.add)
            return e.tensor_tensor(at, at, ps_g[:], ALU.add)

        run_if_left(nc, k, m, 1, [(STEPS, [
            ("sync", load), ("gpsimd", gather), ("vector", add_rows),
            ("scalar", lambda e, _: e.activation(score[:], gp[:, :, H], ACT.Sigmoid)),
            ("vector", lambda e, _: e.tensor_tensor(sc_t[:], sc_t[:], spread(score[:], 2, T), ALU.mult)),
            ("scalar", hidden),
            (NT, [("vector", match), ("tensor", sums), ("vector", add)]),
        ])])


def between(nc, a, k, dram):
    with ExitStack() as ctx:
        m = Mem(nc, ctx)
        half_n = GRP * P // 2
        out_a, out_b = m.sb("out_a", [P, MUL]), m.sb("out_b", [P, MUL])
        w_out = m.sb("w_out", [P, 2, H])
        w_p, w_q, bias_q = m.sb("w_p", [P, T, PW]), m.sb("w_q", [P, T, PW]), m.sb("bias_q", [P, T, PW])
        att, att_b = m.sb("att", [P, 2, T]), m.sb("att_b", [P, T])
        x_in, x1 = m.sb("x_in1", [P, GRP, H]), m.sb("x1", [P, GRP, H])
        o_t, x1_t = m.sb("o_t", [P, GRP * P]), m.sb("x1_t", [P, GRP * P])
        p_buf, q_buf = m.sb("p_buf", [P, GRP, T * PW]), m.sb("q_buf", [P, GRP, T * PW])
        stats, mv, rstd = m.sb("stats", [P, GRP, 6]), m.sb("mv", [P, GRP, 2]), m.sb("rstd", [P, GRP])
        ps_o, ps_t = m.ps("ps_o", [P, 2, 512]), m.ps("ps_t1", [P, 8, P])
        ps_p, ps_q = m.ps("ps_p", [P, 2, 512]), m.ps("ps_q", [P, 2, 512])
        ld_w, w_clear, w_ok, own_s, x_ld, x_used, o_mm, o_ok, t_mm, sum_ok, var_ok, root_ok, x1_ok = (
            m.sem(n + "_b") for n in ("ld_w", "w_clear", "w_ok", "own", "x_ld", "x_used", "o_mm", "o_ok", "t_mm",
                                      "sum_ok", "var_ok", "root_ok", "x1_ok"))
        gate = m.sem("gate_b")
        t1_mm, t1_ok, p_mm, q_mm, p_ok, q_ok, x1_st, p_st, q_st, z_st = (
            m.sem(n + "_b") for n in ("t1_mm", "t1_ok", "p_mm", "q_mm", "p_ok", "q_ok", "x1_st", "p_st", "q_st", "z_st"))
        x_g = a["x"].rearrange("(t p) f -> p t f", p=P)
        x1_g = dram["x1"].rearrange("(t p) f -> p t f", p=P)
        p_g = dram["p_tab"].rearrange("(t p y) f -> p t (y f)", p=P, y=T)
        q_g = dram["q_tab"][0:NP * T, :].rearrange("(t p y) f -> p t (y f)", p=P, y=T)

        with nc.Block() as block:

            @block.sync
            def _(e):
                for c in range(3):
                    e.dma_start(out_a[MUL * c:MUL * (c + 1), :], a["W_out1"][MUL:2 * MUL, :]).then_inc(ld_w, 16)
                    e.dma_start(out_b[MUL * c:MUL * (c + 1), :], a["W_out1"][0:MUL, :]).then_inc(ld_w, 16)
                e.dma_start(out_a[3 * MUL:P, :], a["W_out0"][0:MUL, :]).then_inc(ld_w, 16)
                e.dma_start(out_b[3 * MUL:P, :], a["W_out0"][MUL:2 * MUL, :]).then_inc(ld_w, 16)
                for part, tab in enumerate((w_p, w_q)):
                    e.dma_start(att[:, part, :], a["attn_wT"][H * part:H * (part + 1), :]).then_inc(ld_w, 16)
                    e.dma_start(tab[:, :, 0:H], a["W1"][:, H * part:H * (part + 1), :]
                                .rearrange("t i o -> i t o")).then_inc(ld_w, 16)
                e.dma_start(bias_q[:, :, 0:H], spread(a["b1"], 0, P)).then_inc(ld_w, 16)
                e.dma_start(att_b[:], a["attn_b"].to_broadcast([P, T])).then_inc(ld_w, 16)
                pad = (NACC - NP) * T
                e.dma_start(dram["q_tab"][NP * T:NACC * T, :], k["zero"][0:pad, 0:PW]).then_inc(z_st, 16)
                for s in (p_st, q_st):
                    e.sem_inc(s, 16)
                with e.Fori(0, NG) as g:
                    rows = bass.ds(g * GRP, GRP)
                    e.wait_ge(x_used, g + 1)
                    e.dma_start(x_in[:], x_g[:, rows, :]).then_inc(x_ld, 16)
                    e.wait_ge(x1_ok, g + 1)
                    e.dma_start(x1_g[:, rows, :], x1[:]).then_inc(x1_st, 16)
                    e.wait_ge(p_ok, g * GRP + GRP)
                    e.dma_start(p_g[:, rows, :], p_buf[:]).then_inc(p_st, 16)
                    e.wait_ge(q_ok, g * GRP + GRP)
                    e.dma_start(q_g[:, rows, :], q_buf[:]).then_inc(q_st, 16)
                for s, v in ((x1_st, NG), (p_st, NG + 1), (q_st, NG + 1), (z_st, 1), (ld_w, 14)):
                    e.wait_ge(s, 16 * v)

            @block.gpsimd
            def _(e):
                e.memset(w_out[:], 0.0).then_inc(w_clear, 1)

            @block.scalar
            def _(e):
                with e.Fori(0, NG) as g:
                    e.wait_ge(o_mm, g + 1)
                    e.activation(o_t[:].rearrange("p (b n) -> p b n", b=2), ps_o[:, :, 0:half_n], ACT.Copy)\
                        .then_inc(o_ok, 1)
                    e.wait_ge(var_ok, g + 1)
                    e.activation(rstd[:], rstd[:], ACT.Sqrt).then_inc(root_ok, 1)
                    e.wait_ge(t1_mm, g + 1)
                    e.activation(x1_t[:].rearrange("p (t n) -> p t n", t=GRP), ps_t[:, 0:GRP, :], ACT.Copy)\
                        .then_inc(t1_ok, 1)
                    for t in range(GRP):
                        e.wait_ge(p_mm, g * GRP + (t + 1))
                        if t == 0:
                            e.wait_ge(p_st, g * 16 + 16)
                        e.activation(p_buf[:, t, :].rearrange("p (b n) -> p b n", b=2), ps_p[:, :, 0:2 * PW],
                                     ACT.Copy).then_inc(p_ok, 1)

            @block.tensor
            def _(e):
                acc = k["acc"][:, 0:2 * NACC].rearrange("p (b n) -> p b n", b=2)
                wp, wq = (x[:].rearrange("p t n -> p (t n)") for x in (w_p, w_q))
                e.wait_ge(w_ok, 1)
                with e.Fori(0, NG) as g:
                    for b in range(2):
                        for v in range(2):
                            last = e.matmul(ps_o[:, b, 0:half_n], w_out[:, v, :],
                                            acc[:, v, bass.ds(g * (GRP * P) + b * half_n, half_n)],
                                            start=v == 0, stop=v == 1)
                    last.then_inc(o_mm, 1)
                    e.wait_ge(o_ok, g + 1)
                    for t in range(GRP):
                        last = e.transpose(ps_t[:, t, :], o_t[:, t * P:(t + 1) * P], k["ident"][:])
                    last.then_inc(t_mm, 1)
                    e.wait_ge(x1_ok, g + 1)
                    for t in range(GRP):
                        last = e.transpose(ps_t[:, t, :], x1[:, t, :], k["ident"][:])
                    last.then_inc(t1_mm, 1)
                    e.wait_ge(t1_ok, g + 1)
                    for t in range(GRP):
                        lhs = x1_t[:, t * P:(t + 1) * P]
                        for wt, ps, mm, ok in ((wp, ps_p, p_mm, p_ok), (wq, ps_q, q_mm, q_ok)):
                            if t:
                                e.wait_ge(ok, g * GRP + t)
                            for b in range(2):
                                last = e.matmul(ps[:, b, 0:2 * PW], lhs, wt[:, 2 * PW * b:2 * PW * (b + 1)],
                                                start=True, stop=True)
                            last.then_inc(mm, 1)

            @block.vector
            def _(e):
                own = Own(e, own_s)
                e.wait_ge(ld_w, 16 * 14)
                e.wait_ge(w_clear, 1)
                for c in range(3):
                    rows, vec = slice(MUL * c, MUL * (c + 1)), slice(MUL + c, MUL + c + 3 * (MUL - 1) + 1, 3)
                    e.tensor_copy(w_out[rows, 0, vec], out_a[rows, :])
                    e.tensor_copy(w_out[rows, 1, vec], out_b[rows, :])
                e.tensor_copy(w_out[3 * MUL:P, 0, 0:MUL], out_a[3 * MUL:P, :])
                e.tensor_scalar(w_out[3 * MUL:P, 1, 0:MUL], out_b[3 * MUL:P, :], 3.0 ** -0.5, None, ALU.mult)
                e.tensor_copy(bias_q[:, :, H], att_b[:])
                e.tensor_copy(w_p[:, :, H], att[:, 0, :])
                e.tensor_copy(w_q[:, :, H], att[:, 1, :]).then_inc(w_ok, 1)
                e.sem_inc(x_used, 1)
                bias = bias_q[:].rearrange("p t n -> p (t n)")
                with e.Fori(0, NG) as g:
                    e.wait_ge(t_mm, g + 1)
                    e.wait_ge(x_ld, g * 16 + 16)
                    e.scalar_tensor_tensor(x1[:], ps_t[:, 0:GRP, :], 1.0 / ((2 * MUL) ** 0.5 * 16.0), x_in[:],
                                           ALU.mult, ALU.add).then_inc(sum_ok, 1)
                    e.wait_ge(sum_ok, g * 4 + 1)
                    e.sem_inc(x_used, 1)
                    norm_stats(e, x1, stats, mv, rstd, sum_ok, g * 4 + 1, var_ok, gate)
                    e.wait_ge(root_ok, g + 1)
                    norm_apply(e, x1, x1, mv, rstd, sum_ok, g * 4 + 4).then_inc(x1_ok, 1)
                    for t in range(GRP):
                        e.wait_ge(q_mm, g * GRP + (t + 1))
                        if t == 0:
                            e.wait_ge(q_st, g * 16 + 16)
                        e.tensor_tensor(q_buf[:, t, :].rearrange("p (b n) -> p b n", b=2), ps_q[:, :, 0:2 * PW],
                                        bias.rearrange("p (b n) -> p b n", b=2), ALU.add).then_inc(q_ok, 1)


def norm_stats(e, x, stats, mv, rstd, own, at, var_ok, gate):
    for t in range(GRP):
        last = e.bn_stats(stats[:, t, :], x[:, t, :])
    last.then_inc(own, 1)
    e.wait_ge(own, at + 1)
    e.sem_inc(gate, 1)
    for t in range(GRP):
        last = e.bn_aggr(mv[:, t, :], stats[:, t, :])
    last.then_inc(own, 1)
    e.wait_ge(own, at + 2)
    e.tensor_scalar(rstd[:], mv[:, :, 1], LN_EPS, None, ALU.add).then_inc(var_ok, 1)


def norm_apply(e, x, out, mv, rstd, own, at):
    e.reciprocal(rstd[:], rstd[:]).then_inc(own, 1)
    e.wait_ge(own, at)
    for t in range(GRP):
        last = e.tensor_scalar(out[:, t, :], x[:, t, :], mv[:, t, 0:1], rstd[:, t:t + 1],
                               ALU.subtract, ALU.mult)
    return last


def clear_sums(nc, k):
    with ExitStack() as ctx:
        with nc.Block() as block:
            half = T * NACC // 2

            @block.vector
            def _(e):
                e.memset(k["acc"][:, 0:half], 0.0)

            @block.gpsimd
            def _(e):
                e.memset(k["acc"][:, half:], 0.0)
                e.memset(k["acc_s"][0:T, :], 0.0)


def edges1(nc, k, dram):
    with ExitStack() as ctx:
        m = Mem(nc, ctx)
        QT = TPS // 2
        UN = 4
        idx = m.sb("idx1", [P, 2, TPS], u32)
        gp = m.sb("gp", [P, 2, TPS, PW])
        win = m.sb("win", [P, 2, PPS, PW])
        hot = m.sb("hot1", [P, UN, TPS, P], bf16)
        hot_n = m.sb("hot_n", [P, UN, TPS, WIN], bf16)
        hot_t = m.sb("hot_t", [P, UN, TPS, T])
        hot_x = m.sb("hot_x", [P, 2, TPS, P])
        ident16 = m.sb("ident16", [P, P], bf16)
        pre = m.sb("pre", [P, 2, TPS, PW])
        hid = m.sb("hid", [P, 2, TPS, H])
        hid_rest, hid_low = m.sb("hid_rest", [P, TPS, H]), m.sb("hid_low", [P, TPS, H], bf16)
        score = m.sb("score", [P, 2, TPS])
        sc, sc_rest, sc_low = m.sb("sc", [P, TPS, T]), m.sb("sc_rest", [P, TPS, T]), m.sb("sc_low", [P, TPS, T], bf16)
        ps_x = m.ps("ps_x", [P, 2, TPS, P], bf16)
        ps_e = m.ps("ps_e", [P, TPS, 2 * P])
        ps_g = m.ps("ps_g", [P, PPS, P])
        ps_s = m.ps("ps_s", [T, PPS, P])
        idx_in, win_in, landed = m.sems("idx_in1", 2), m.sems("win_in", 2), m.sems("landed1", 2)
        (used, gate, id_ok, hot_ok, x_mm, x_ok, e_mm, pre_ok, score_ok, hid_ok, own, split_ok, sum_mm, acc_own,
         score_own) = (
            m.sem(n + "_1") for n in ("used", "gate", "id_ok", "hot_ok", "x_mm", "x_ok", "e_mm", "pre_ok",
                                      "score_ok", "hid_ok", "own", "split_ok", "sum_mm", "acc_own", "score_own"))

        with nc.Block() as block:

            @block.sync
            def _(e):
                regs = start_registers(e, "window")

                def load_windows(j, h):
                    for p, start in enumerate(run_starts(e, k, j, regs)):
                        e.dma_start(win[:, h, p, :], dram["q_tab"][bass.ds(start * T, P), :]).then_inc(win_in[h], 16)

                for h in range(2):
                    e.dma_start(idx[:, h, :], dram["p_idx"][:, h * TPS:(h + 1) * TPS]).then_inc(idx_in[h], 16)
                    load_windows(h, h)
                with e.Fori(0, STEPS // 2) as i:
                    for h in range(2):
                        e.wait_ge(e_mm, i * 4 + (2 * h + 2))
                        load_windows(i * 2 + (h + 2), h)
                        e.wait_ge(landed[h], i * (16 * TPS) + 16 * TPS)
                        e.dma_start(idx[:, h, :], dram["p_idx"][:, bass.ds(i * (2 * TPS) + (h + 2) * TPS, TPS)])\
                            .then_inc(idx_in[h], 16)
                for h in range(2):
                    e.wait_ge(win_in[h], 16 * PPS * (STEPS // 2 + 1))
                    e.wait_ge(idx_in[h], 16 * (STEPS // 2 + 1))

            @block.gpsimd
            def _(e):
                gather_loop(e, idx, idx_in, dram["p_tab"], gp, landed, used, gate)

            @block.scalar
            def _(e):
                def copy_x(h, value):
                    e.wait_ge(x_mm, value)
                    e.activation(hot_x[:, h], ps_x[:, h], ACT.Copy).then_inc(x_ok, 1)

                e.preload_act_table(ACT.Sigmoid)
                for n in range(2):
                    copy_x(n, n + 1)
                with e.Fori(0, STEPS // UN) as i:
                    for u in range(UN):
                        h = u % 2
                        for q in range(2):
                            e.wait_ge(pre_ok, i * (2 * UN) + (2 * u + q + 1))
                            mine = slice(QT * q, QT * (q + 1))
                            e.activation(score[:, h, mine], pre[:, h, mine, H], ACT.Sigmoid).then_inc(score_ok, 1)
                            e.wait_ge(score_ok, i * (2 * UN) + (2 * u + q + 1))
                            for t in range(QT * q, QT * (q + 1)):
                                last = e.activation(hid[:, h, t, :], pre[:, h, t, 0:H], ACT.Relu,
                                                    scale=score[:, h, t:t + 1])
                            last.then_inc(hid_ok, 1)
                        copy_x(h, i * UN + (u + 3))

            @block.tensor
            def _(e):
                def transposes(buf, h, value):
                    e.wait_ge(hot_ok, value)
                    for t in range(TPS):
                        last = e.transpose(ps_x[:, h, t, :], hot[:, buf, t, :], ident16[:])
                    last.then_inc(x_mm, 1)

                def receivers(h, value, win_value, pre_value):
                    e.wait_ge(x_ok, value)
                    e.wait_ge(win_in[h], win_value)
                    for q in range(2):
                        e.wait_ge(pre_ok, pre_value + q)
                        for t in range(QT * q, QT * (q + 1)):
                            last = e.matmul(ps_e[:, t, 0:PW], hot_x[:, h, t, :], win[:, h, t // 2, :],
                                            start=True, stop=True)
                        last.then_inc(e_mm, 1)

                def parts(f, rest, low, t):
                    return enumerate((upper(f[:, t, :]), upper(rest[:, t, :]), low[:, t, :]))

                e.wait_ge(id_ok, 1)
                transposes(0, 0, 1)
                transposes(1, 1, 2)
                e.wait_ge(x_ok, 1)
                e.wait_ge(win_in[0], 16 * PPS)
                for t in range(TPS):
                    last = e.matmul(ps_e[:, t, 0:PW], hot_x[:, 0, t, :], win[:, 0, t // 2, :], start=True, stop=True)
                    if t % QT == QT - 1:
                        last.then_inc(e_mm, 1)
                with e.Fori(0, STEPS // UN) as i:
                    for u in range(UN):
                        h = u % 2
                        receivers(1 - h, i * UN + (u + 2),
                                  i * (16 * PPS * UN // 2) + 16 * PPS * ((u + 1) // 2 + 1),
                                  i * (2 * UN) + (2 * u + 1))
                        transposes((u + 2) % UN, h, i * UN + (u + 3))
                        e.wait_ge(split_ok, i * (3 * UN) + (3 * u + 1))
                        for p in range(PPS):
                            for t in range(2 * p, 2 * p + 2):
                                for n, part in parts(sc, sc_rest, sc_low, t):
                                    e.matmul(ps_s[:, p, 0:WIN], part, hot_n[:, u, t, :],
                                             start=t % 2 + n == 0, stop=t % 2 + n == 3)
                        for q in range(2):
                            e.wait_ge(split_ok, i * (3 * UN) + (3 * u + 2 + q))
                            for p in range(PPS // 2 * q, PPS // 2 * (q + 1)):
                                for t in range(2 * p, 2 * p + 2):
                                    for n, part in parts(hid[:, h], hid_rest, hid_low, t):
                                        last = e.matmul(ps_g[:, p, :], part, hot[:, u, t, :],
                                                        start=t % 2 + n == 0, stop=t % 2 + n == 3)
                        last.then_inc(sum_mm, 1)

            @block.vector
            def _(e):
                def one_hot_small(tiles, buf):
                    e.tensor_tensor(hot_n[:, buf], spread(k["iota"][:, 0:WIN], 1, TPS),
                                    spread(k["dloc"][:, tiles], 2, WIN), ALU.is_equal)
                    e.tensor_tensor(hot_t[:, buf], spread(k["iota"][:, 0:T], 1, TPS),
                                    spread(k["typef"][:, tiles], 2, T), ALU.is_equal)

                def one_hot_key(tiles, buf):
                    e.tensor_tensor(hot[:, buf], spread(k["iota"][:, 0:P], 1, TPS),
                                    spread(k["key"][:, tiles], 2, P), ALU.is_equal).then_inc(hot_ok, 1)

                regs = start_registers(e, "sum1")

                def start_windows(j):
                    starts = run_starts(e, k, j, regs)

                    def add(p):
                        at = k["acc"][:, bass.ds(starts[p] * T, P)]
                        at_s = k["acc_s"][0:T, bass.ds(starts[p], WIN)]
                        e.wait_ge(sum_mm, j + 1)
                        e.wait_ge(acc_own, j * PPS + (p + 1))
                        e.tensor_tensor(at, at, ps_g[:, p, :], ALU.add).then_inc(acc_own, 1)
                        e.wait_ge(score_own, j * PPS + (p + 1))
                        e.tensor_tensor(at_s, at_s, ps_s[:, p, 0:WIN], ALU.add).then_inc(score_own, 1)
                    return add

                def edge_rows(i, u, before):
                    j, h = i * UN + u, u % 2
                    add = start_windows(j - 1) if before else (lambda p: None)
                    ahead, buf = bass.ds(j * TPS + 2 * TPS, TPS), (u + 2) % UN
                    e.wait_ge(landed[h], i * (16 * TPS * UN // 2) + 16 * TPS * (u // 2 + 1))
                    for q in range(2):
                        mine = slice(QT * q, QT * (q + 1))
                        e.wait_ge(e_mm, j * 2 + (q + 1))
                        e.tensor_tensor(pre[:, h, mine, :], ps_e[:, mine, 0:PW], gp[:, h, mine, :],
                                        ALU.add).then_inc(pre_ok, 1)
                    add(0)
                    e.wait_ge(pre_ok, j * 2 + 2)
                    e.sem_inc(used, 1)
                    one_hot_small(ahead, buf)
                    add(1)
                    one_hot_key(ahead, buf)
                    add(2)
                    e.wait_ge(score_ok, j * 2 + 2)
                    e.wait_ge(hot_ok, j + 1)
                    e.tensor_tensor(sc[:], hot_t[:, u], spread(score[:, h, :], 2, T), ALU.mult).then_inc(own, 1)
                    add(3)
                    parts = [(x[:].rearrange("p t n -> p (t n)"), y[:].rearrange("p t n -> p (t n)"))
                             for x, y in ((sc, sc_rest), (sc_rest, sc_low))]
                    for n, (whole, part) in enumerate(parts):
                        e.wait_ge(own, j * 4 + (1 + n))
                        last = e.tensor_tensor(part, whole, upper(whole), ALU.subtract)
                        last.then_inc((own, split_ok)[n], 1)
                    for q in range(2):
                        mine = slice(QT * q, QT * (q + 1))
                        whole, rest, low = (x.rearrange("p t n -> p (t n)") for x in (
                            hid[:, h, mine, :], hid_rest[:, mine, :], hid_low[:, mine, :]))
                        e.wait_ge(hid_ok, j * 2 + (q + 1))
                        e.tensor_tensor(rest, whole, upper(whole), ALU.subtract).then_inc(own, 1)
                        e.wait_ge(own, j * 4 + (3 + q))
                        e.tensor_tensor(low, rest, upper(rest), ALU.subtract).then_inc(split_ok, 1)

                e.tensor_copy(ident16[:], k["ident"][:]).then_inc(id_ok, 1)
                e.sem_inc(used, 2)
                for s in (acc_own, score_own):
                    e.sem_inc(s, 1)
                for u in range(2):
                    one_hot_small(bass.ds(u * TPS, TPS), u)
                    one_hot_key(bass.ds(u * TPS, TPS), u)
                for u in range(UN):
                    edge_rows(0, u, u > 0)
                with e.Fori(1, STEPS // UN) as i:
                    for u in range(UN):
                        edge_rows(i, u, True)
                add = start_windows(STEPS - 1)
                for p in range(PPS):
                    add(p)
                for s in (acc_own, score_own):
                    e.wait_ge(s, STEPS * PPS + 1)


def update(nc, a, k, dram, out):
    with ExitStack() as ctx:
        m = Mem(nc, ctx)
        half_n = GRP * P // 2
        w2, b2 = m.sb("w2_1", [P, T, H]), m.sb("b2_1", [T, H])
        w_ih, w_hh = m.sb("w_ih", [P, 3 * H]), m.sb("w_hh", [P, 3 * H])
        bf = m.sb("bf", [6, 4 * H])
        b_hi, b_mid, b_lo = (m.sb(n, [6, 4 * H], bf16) for n in ("bg_hi", "bg_mid", "bg_lo"))
        bias, ones = m.sb("bias_g", [6, 4 * H], bf16), m.sb("ones_g", [6, P], bf16)
        gamma, beta = m.sb("gamma", [P, H]), m.sb("beta", [P, H])
        x1, x1_t, agg_t = m.sb("x1u", [P, GRP, H]), m.sb("x1_tu", [P, GRP * P]), m.sb("agg_t", [P, GRP * P])
        rz, cand, d = m.sb("rz", [P, GRP, 2 * H]), m.sb("cand", [P, GRP, H]), m.sb("d", [P, GRP, H])
        u, y = m.sb("u", [P, GRP, H]), m.sb("yu", [P, GRP, H])
        stats, mv, rstd = m.sb("stats_u", [P, GRP, 6]), m.sb("mv_u", [P, GRP, 2]), m.sb("rstd_u", [P, GRP])
        ps_t, ps_a = m.ps("ps_tu", [P, 8, P]), m.ps("ps_au", [P, 2, 512])
        ps_u = m.ps("ps_u", [P, 4, 512])
        ld_w, clear_b, own_s, split_ok, b_mv, x_ld, x_used, t_mm, t_ok, a_mm, a_ok, u_mm = (
            m.sem(n + "_u") for n in ("ld_w", "clear_b", "own", "split_ok", "b_mv", "x_ld", "x_used", "t_mm",
                                      "t_ok", "a_mm", "a_ok", "u_mm"))
        gate = m.sem("gate_u")
        gate_ok, cand_ok, tanh_ok, step, var_ok, root_ok, out_ok, out_st, r_own, r2_own = (
            m.sem(n + "_u") for n in ("gate_ok", "cand_ok", "tanh_ok", "step", "var_ok", "root_ok", "out_ok",
                                      "out_st", "r_own", "r2_own"))
        x1_g = dram["x1"].rearrange("(t p) f -> p t f", p=P)
        out_g = out.rearrange("(t p) f -> p t f", p=P)

        with nc.Block() as block:

            @block.sync
            def _(e):
                e.wait_ge(clear_b, 1)
                e.dma_start(bf[0:3, 0:3 * H], a["b_ih"].to_broadcast([3, 3 * H])).then_inc(ld_w, 16)
                e.dma_start(bf[3:6, 0:2 * H], a["b_hh"][:, 0:2 * H].to_broadcast([3, 2 * H])).then_inc(ld_w, 16)
                e.dma_start(bf[3:6, 3 * H:4 * H], a["b_hh"][:, 2 * H:3 * H].to_broadcast([3, H])).then_inc(ld_w, 16)
                e.dma_start(w2[:], a["W2"].rearrange("t i o -> i t o")).then_inc(ld_w, 16)
                e.dma_start(b2[:], a["b2"]).then_inc(ld_w, 16)
                e.dma_start(w_ih[:], a["w_ihT"]).then_inc(ld_w, 16)
                e.dma_start(w_hh[:], a["w_hhT"]).then_inc(ld_w, 16)
                e.dma_start(gamma[:], a["gamma"].to_broadcast([P, H])).then_inc(ld_w, 16)
                e.dma_start(beta[:], a["beta"].to_broadcast([P, H])).then_inc(ld_w, 16)
                e.wait_ge(split_ok, 1)
                for r, part in enumerate((b_hi, b_mid, b_lo)):
                    e.dma_start(bias[r:r + 1, :], part[r:r + 1, :]).then_inc(b_mv, 16)
                    e.dma_start(bias[3 + r:4 + r, :], part[3 + r:4 + r, :]).then_inc(b_mv, 16)
                e.sem_inc(out_st, 16)
                with e.Fori(0, NG) as g:
                    rows = bass.ds(g * GRP, GRP)
                    e.wait_ge(x_used, g + 1)
                    e.dma_start(x1[:], x1_g[:, rows, :]).then_inc(x_ld, 16)
                    e.wait_ge(out_ok, g + 1)
                    e.dma_start(out_g[:, rows, :], y[:]).then_inc(out_st, 16)
                e.wait_ge(out_st, 16 * (NG + 1))

            @block.scalar
            def _(e):
                with e.Fori(0, NG) as g:
                    e.wait_ge(t_mm, g + 1)
                    e.activation(x1_t[:].rearrange("p (t n) -> p t n", t=GRP), ps_t[:, 0:GRP, :], ACT.Copy)\
                        .then_inc(t_ok, 1)
                    e.wait_ge(a_mm, g + 1)
                    e.activation(agg_t[:].rearrange("p (b n) -> p b n", b=2), ps_a[:, :, 0:half_n], ACT.Copy)\
                        .then_inc(a_ok, 1)
                    for t in range(GRP):
                        e.wait_ge(u_mm, g * GRP + (t + 1))
                        e.activation(rz[:, t, :], ps_u[:, t % 4, 0:2 * H], ACT.Sigmoid).then_inc(gate_ok, 1)
                    e.wait_ge(cand_ok, g * GRP + GRP)
                    e.activation(cand[:], cand[:], ACT.Tanh).then_inc(tanh_ok, 1)
                    for n in range(2):
                        e.wait_ge(var_ok, g * 2 + (n + 1))
                        e.activation(rstd[:], rstd[:], ACT.Sqrt).then_inc(root_ok, 1)

            @block.tensor
            def _(e):
                acc = k["acc"][:].rearrange("p (n t) -> p t n", t=T)
                e.wait_ge(ld_w, 16 * 9)
                e.wait_ge(b_mv, 16 * 6)
                with e.Fori(0, NG) as g:
                    e.wait_ge(x_ld, g * 16 + 16)
                    for t in range(GRP):
                        last = e.transpose(ps_t[:, t, :], x1[:, t, :], k["ident"][:])
                    last.then_inc(t_mm, 1)
                    for b in range(2):
                        nodes = bass.ds(g * (GRP * P) + b * half_n, half_n)
                        for t in range(T):
                            e.matmul(ps_a[:, b, 0:half_n], w2[:, t, :], acc[:, t, nodes], start=t == 0, stop=False)
                        last = e.matmul(ps_a[:, b, 0:half_n], b2[:], k["acc_s"][0:T, nodes], start=False, stop=True)
                    last.then_inc(a_mm, 1)
                    e.wait_ge(t_ok, g + 1)
                    e.wait_ge(a_ok, g + 1)
                    for t in range(GRP):
                        ps, at = ps_u[:, t % 4, :], slice(t * P, (t + 1) * P)
                        if t >= 4:
                            e.wait_ge(cand_ok, g * GRP + (t - 3))
                        for cols, parts in ((slice(0, 2 * H), ((agg_t, w_ih[:, 0:2 * H]), (x1_t, w_hh[:, 0:2 * H]))),
                                            (slice(2 * H, 3 * H), ((agg_t, w_ih[:, 2 * H:3 * H]),)),
                                            (slice(3 * H, 4 * H), ((x1_t, w_hh[:, 2 * H:3 * H]),))):
                            e.matmul(ps[:, cols], ones[:], bias[:, cols], start=True, stop=False)
                            for lhs, rhs in parts:
                                last = e.matmul(ps[:, cols], lhs[:, at], rhs, start=False, stop=lhs is parts[-1][0])
                        last.then_inc(u_mm, 1)

            @block.vector
            def _(e):
                own = Own(e, own_s)
                e.memset(ones[:], 1.0)
                e.memset(bf[:], 0.0).then_inc(clear_b, 1)
                e.wait_ge(ld_w, 16 * 9)
                split3(e, own, bf[:], b_hi[:], b_mid[:], b_lo[:], bf[:])
                e.sem_inc(split_ok, 1)
                e.sem_inc(x_used, 1)
                SC = 11
                with e.Fori(0, NG) as g:
                    for t in range(GRP):
                        e.wait_ge(gate_ok, g * GRP + (t + 1))
                        e.tensor_tensor(cand[:, t, :], rz[:, t, 0:H], ps_u[:, t % 4, 3 * H:4 * H], ALU.mult)\
                            .then_inc(r_own, 1)
                        e.wait_ge(r_own, g * GRP + (t + 1))
                        e.tensor_tensor(cand[:, t, :], cand[:, t, :], ps_u[:, t % 4, 2 * H:3 * H], ALU.add)\
                            .then_inc(cand_ok, 1)
                    e.wait_ge(tanh_ok, g + 1)
                    n = [0]

                    def then(ins):
                        n[0] += 1
                        ins.then_inc(step, 1)
                        e.wait_ge(step, g * SC + n[0])

                    then(e.tensor_tensor(d[:], x1[:], cand[:], ALU.subtract))
                    then(e.tensor_tensor(d[:], d[:], rz[:, :, H:2 * H], ALU.mult))
                    then(e.tensor_tensor(u[:], x1[:], cand[:], ALU.add))
                    then(e.tensor_tensor(u[:], u[:], d[:], ALU.add))
                    norm_stats(e, u, stats, mv, rstd, step, g * SC + 4, var_ok, gate)
                    e.wait_ge(root_ok, g * 2 + 1)
                    n[0] = 7
                    then(norm_apply(e, u, u, mv, rstd, step, g * SC + 7))
                    then(e.tensor_tensor(u[:], u[:], spread(gamma[:], 1, GRP), ALU.mult))
                    then(e.tensor_tensor(u[:], u[:], spread(beta[:], 1, GRP), ALU.add))
                    then(e.tensor_tensor(u[:], u[:], x1[:], ALU.add))
                    e.sem_inc(x_used, 1)
                    norm_stats(e, u, stats, mv, rstd, r2_own, g * 3, var_ok, gate)
                    e.wait_ge(root_ok, g * 2 + 2)
                    e.wait_ge(out_st, g * 16 + 16)
                    norm_apply(e, u, y, mv, rstd, r2_own, g * 3 + 3).then_inc(out_ok, 1)


_OUTS = [((NP, H), "float32")]


def kernel(**inputs):
    import numpy as np
    import concourse.bacc as bacc
    from concourse.bass_utils import run_bass_kernel_spmd

    arrays = lay_out(np, inputs)
    nc = bacc.Bacc("TRN2", target_bir_lowering=False, num_devices=1)
    aps = {n: nc.dram_tensor(f"in_{n}", v.shape, mybir.dt.from_np(v.dtype), kind="ExternalInput").ap()
           for n, v in arrays.items()}
    out = nc.dram_tensor("out", (NP, H), f32, kind="ExternalOutput").ap()
    build(nc, aps, out)
    r = run_bass_kernel_spmd(nc, [{f"in_{n}": v for n, v in arrays.items()}], core_ids=[0])
    return r.results[0]["out"][0:N]


def lay_out(np, inputs):
    def flat(v, fill, n):
        v = np.asarray(v)
        pad = np.full((n - v.shape[0],) + v.shape[1:], fill, v.dtype)
        return np.concatenate([v, pad])

    def by_partition(v, tiles):
        v = v.reshape(tiles, P, *v.shape[1:]).swapaxes(0, 1)
        return np.ascontiguousarray(v)

    dst = flat(inputs["dst"], N, LTILES * P)
    length = flat(inputs["edge_weight"], 0.0, TILES * P).reshape(ECH // 2, SPC, PPS, 2, P)
    L0, L1 = "L0_gnn_", "L1_gnn_"
    arrays = {
        "x": flat(inputs["x"], 0.0, NP),
        "src": by_partition(flat(inputs["src"], 0, LTILES * P), LTILES),
        "dst": by_partition(dst, LTILES),
        "type": by_partition(flat(inputs["edge_type_4"], 0, LTILES * P), LTILES),
        "start": dst[::2 * P].reshape(1, LTILES // 2),
        "vec": by_partition(flat(inputs["edge_attr_3"], 0.0, TILES * P), TILES),
        "length": length.transpose(0, 3, 1, 2, 4).reshape(ECH, SPC * HALF),
        "mlp_b0": inputs[L0 + "mlp_b0"].reshape(HID, 1),
        "mlp_b1": inputs[L0 + "mlp_b1"].reshape(HID, 1),
        "mlp_b2": inputs[L0 + "mlp_b2"].reshape(1, P),
        "attn_wT": inputs[L1 + "attn_w"].T,
        "attn_b": inputs[L1 + "attn_b"].reshape(1, T),
        "w_ihT": inputs[L1 + "w_ih"].T,
        "w_hhT": inputs[L1 + "w_hh"].T,
        "b_ih": inputs[L1 + "b_ih"].reshape(1, 3 * H),
        "b_hh": inputs[L1 + "b_hh"].reshape(1, 3 * H),
        "gamma": inputs[L1 + "ln_gamma"].reshape(1, H),
        "beta": inputs[L1 + "ln_beta"].reshape(1, H),
    }
    for n in ("W_up0", "W_up1", "mlp_w0", "mlp_w1", "mlp_w2", "W_out0", "W_out1"):
        arrays[n] = inputs[L0 + n]
    for n in ("W1", "b1", "W2", "b2"):
        arrays[n] = inputs[L1 + n]
    return {n: np.ascontiguousarray(v) for n, v in arrays.items()}
```

```python
import concourse.bass as bass
from concourse import mybir
from concourse.alu_op_type import AluOpType as ALU
from contextlib import ExitStack

P = 128
N = 6250
E = 106250
H = 128
MUL = 32
NB = 8
T = 4
WIN = 32
TPS = 8
PPS = TPS // 2
SPLIT = TPS - 2
STEPS = -(-E // (P * TPS))
TILES = STEPS * TPS
LTILES = TILES + 2 * TPS
NT = -(-N // P)
NP = NT * P
NACC = NP + 16
GRP = 7
NG = NT // GRP
PW = H + 1
HID = 64
ECH = 16
SPC = STEPS // (ECH // 2)
HALF = P * TPS // 2
LN_EPS = 1e-5
FAR = 1.0e6

f32, bf16 = mybir.dt.float32, mybir.dt.bfloat16
i32, u32 = mybir.dt.int32, mybir.dt.uint32
ACT = mybir.ActivationFunctionType
AX = mybir.AxisListType


def spread(ap, at, n):
    ap = ap.unsqueeze(at)
    shape = list(ap.shape)
    shape[at] = n
    return ap.to_broadcast(shape)


class Own:

    def __init__(self, eng, sem):
        self.eng, self.sem, self.n = eng, sem, 0

    def did(self, ins):
        self.n += 1
        ins.then_inc(self.sem, 1)
        return self.n

    def then(self, ins):
        self.eng.wait_ge(self.sem, self.did(ins))


class Mem:

    def __init__(self, nc, ctx):
        self.nc, self.ctx = nc, ctx

    def sb(self, name, shape, dt=f32):
        return self.ctx.enter_context(self.nc.sbuf_tensor(name, shape, dt))

    def ps(self, name, shape, dt=f32):
        return self.ctx.enter_context(self.nc.psum_tensor(name, shape, dt))

    def sem(self, name):
        return self.ctx.enter_context(self.nc.semaphore(name))

    def sems(self, name, n):
        return [self.sem(f"{name}{k}") for k in range(n)]


def build(nc, a, out):
    top = ExitStack()
    with top:
        m = Mem(nc, top)
        k = dict(
            acc=m.sb("acc", [P, T * NACC]),
            ident=m.sb("ident", [P, P]),
            iota=m.sb("iota", [P, T * P]),
            key=m.sb("key", [P, LTILES]),
            dloc=m.sb("dloc", [P, LTILES]),
            typef=m.sb("typef", [P, LTILES]),
            left=m.sb("left", [P, LTILES]),
            start=m.sb("start", [1, LTILES // 2], i32),
            n_left=m.sb("n_left", [1, 1], i32),
            zero=m.sb("zero", [P, 512]),
        )
        dram = dict(
            emb=nc.dram_tensor("emb_d", [STEPS + 3, 2 * NB, HALF], f32).ap(),
            node0=nc.dram_tensor("node0_d", [NP, H], f32).ap(),
            p_idx=nc.dram_tensor("p_idx_d", [P, LTILES], u32).ap(),
            q_idx=nc.dram_tensor("q_idx_d", [P, LTILES], u32).ap(),
            x1=nc.dram_tensor("x1_d", [NP, H], f32).ap(),
            x1_t=nc.dram_tensor("x1_t_d", [P, NP], f32).ap(),
            p_tab=nc.dram_tensor("p_tab_d", [NP * T, PW], f32).ap(),
            q_tab=nc.dram_tensor("q_tab_d", [NACC * T, PW], f32).ap(),
        )
        later = update_weights(nc, m)
        with ExitStack() as until_edges1:
            later.update(between_weights(nc, Mem(nc, until_edges1)))
            with ExitStack() as layer0:
                w = layer0_weights(nc, Mem(nc, layer0))
                prepare(nc, a, k, dram, w)
                edges0(nc, a, k, dram, w, later)
                leftover0(nc, a, k, dram, w)
            between(nc, a, k, dram, later)
        k["acc_s"] = m.sb("acc_s", [P, NACC])
        edges1(nc, k, dram)
        leftover1(nc, k, dram)
        update(nc, k, dram, later, out)


def layer0_weights(nc, m):
    return dict(
        w0=m.sb("w0", [2 * NB, P]), b0=m.sb("b0", [P, 1]),
        w1=m.sb("w1", [P, P]), b1=m.sb("b1", [P, 1]),
        w2=m.sb("w2", [P, 2 * P]),
        b2=m.sb("b2", [3, 4 * P], bf16), ones=m.sb("ones", [3, P], bf16),
        y=m.sb("y", [P, TILES, 3]),
    )


def between_weights(nc, m):
    return dict(
        out_a=m.sb("out_a", [P, MUL]), out_b=m.sb("out_b", [P, MUL]), att=m.sb("att", [P, 2, T]),
        att_b=m.sb("att_b", [P, T]), w_p=m.sb("w_p", [P, T, PW]), w_q=m.sb("w_q", [P, T, PW]),
        bias_q=m.sb("bias_q", [P, T, PW]),
    )


def update_weights(nc, m):
    return dict(
        w2=m.sb("w2_1", [P, T, H]), b2=m.sb("b2_1", [T, H]), w_ih=m.sb("w_ih", [P, 3 * H]),
        w_hh=m.sb("w_hh", [P, 3 * H]), b_ih=m.sb("b_ih", [P, 3]), b_hh=m.sb("b_hh", [P, 3]),
        gamma=m.sb("gamma", [P, H]), beta=m.sb("beta", [P, H]),
    )


def load_later(e, a, w, sem):
    pairs = []
    for c in range(3):
        rows = slice(MUL * c, MUL * (c + 1))
        pairs += [(w["out_a"][rows, :], a["W_out1"][MUL:2 * MUL, :]), (w["out_b"][rows, :], a["W_out1"][0:MUL, :])]
    pairs += [(w["out_a"][3 * MUL:P, :], a["W_out0"][0:MUL, :]), (w["out_b"][3 * MUL:P, :], a["W_out0"][MUL:2 * MUL, :])]
    for part, tab in enumerate((w["w_p"], w["w_q"])):
        rows = slice(H * part, H * (part + 1))
        pairs += [(w["att"][:, part, :], a["attn_wT"][rows, :]),
                  (tab[:, :, 0:H], a["W1"][:, rows, :].rearrange("t i o -> i t o"))]
    pairs += [(w["bias_q"][:, :, 0:H], spread(a["b1"], 0, P)), (w["att_b"][:], a["attn_b"].to_broadcast([P, T])),
              (w["w2"][:], a["W2"].rearrange("t i o -> i t o")), (w["b2"][:], a["b2"]),
              (w["w_ih"][:], a["w_ihT"]), (w["w_hh"][:], a["w_hhT"]), (w["b_ih"][:], a["b_ihT"]),
              (w["b_hh"][:], a["b_hhT"]), (w["gamma"][:], a["gamma"].to_broadcast([P, H])),
              (w["beta"][:], a["beta"].to_broadcast([P, H]))]
    for to, source in pairs:
        e.dma_start(to, source).then_inc(sem, 16)
    return len(pairs)


def split3(e, own, src, hi, mid, lo, rest):
    own.then(e.tensor_copy(hi, src))
    own.then(e.tensor_tensor(rest, src, hi, ALU.subtract))
    own.then(e.tensor_copy(mid, rest))
    own.then(e.tensor_tensor(rest, rest, mid, ALU.subtract))
    own.then(e.tensor_copy(lo, rest))


def prepare(nc, a, k, dram, w):
    with ExitStack() as ctx:
        m = Mem(nc, ctx)
        acc = k["acc"]
        cols = SPC * HALF
        at = 2 * NACC
        emb = acc[:, at:at + cols]
        mask = m.sb("mask", [P, cols], bf16)
        vec = acc[:, at + cols:at + cols + 3 * TILES].rearrange("p (t c) -> p t c", c=3)
        vec2 = acc[:, at + cols + 3 * TILES:at + cols + 6 * TILES].rearrange("p (t c) -> p t c", c=3)
        EARLY = 3
        spans = [slice(lo * HALF, hi * HALF) for lo, hi in ((0, SPC // 2), (SPC // 2, SPC))]
        src_i, dst_i, type_i = (m.sb(n, [P, LTILES], i32) for n in ("src_i", "dst_i", "type_i"))
        start_i = m.sb("start_i", [P, LTILES // 2], i32)
        dstf, srcf, hit = (m.sb(n, [P, LTILES]) for n in ("dstf", "srcf", "hit"))
        startf = m.sb("startf", [P, LTILES // 2])
        p_idx, q_idx = m.sb("p_idx", [P, LTILES], u32), m.sb("q_idx", [P, LTILES], u32)
        n_hit, one = m.sb("n_hit", [P, 1]), m.sb("one", [P, 1])
        norm2 = m.sb("norm2", [P, TILES])
        centre_i, centre = m.sb("centre_i", [P, 1], i32), m.sb("centre", [P, 1])
        b2f = m.sb("b2f", [3, P])
        b2_hi, b2_mid, b2_lo = (m.sb(n, [3, P], bf16) for n in ("b2_hi", "b2_mid", "b2_lo"))
        w_up = m.sb("w_up", [P, P])
        x_in = m.sb("x_in", [P, 2, GRP, H])
        x_t = m.sb("x_t", [P, GRP * P])
        tab = m.sb("tab", [P, GRP, H])
        ps_t = m.ps("ps_t", [P, 8, P])
        ps_m = m.ps("ps_m", [P, 8, P])
        ps_n = m.ps("ps_n", [1, 1])
        ld_edge, ld_len, ld_vec, ld_w, ld_up, ld_b2 = (m.sem(n) for n in (
            "ld_edge", "ld_len", "ld_vec", "ld_w", "ld_up", "ld_b2"))
        ld_x = m.sems("ld_x", 2)
        clear_ok, up_clear, w_clear, gate = (m.sem(n) for n in ("clear_ok", "up_clear", "w_clear", "gate"))
        v_own, s_own, g_own = (m.sem(n) for n in ("v_own", "s_own", "g_own"))
        clip_ok, exp_ok, emb_ok, norm_ok, root_ok, hits_ok, count_ok, idx_ok, split_ok = (m.sem(n) for n in (
            "clip_ok", "exp_ok", "emb_ok", "norm_ok", "root_ok", "hits_ok", "count_ok", "idx_ok", "split_ok"))
        emb_st, stored, tr_ok, xt_ok, mm_ok, tab_ok, tab_st = (m.sem(n) for n in (
            "emb_st", "stored", "tr_ok", "xt_ok", "mm_ok", "tab_ok", "tab_st"))

        with nc.Block() as block:

            @block.sync
            def _(e):
                for q in range(ECH):
                    e.dma_start(emb[NB * q:NB * q + NB, :],
                                a["length"][q:q + 1, :].to_broadcast([NB, cols])).then_inc(ld_len, 16)
                e.dma_start(dst_i[:], a["dst"]).then_inc(ld_edge, 16)
                e.dma_start(start_i[:], a["start"].to_broadcast([P, LTILES // 2])).then_inc(ld_edge, 16)
                e.dma_start(type_i[:], a["type"]).then_inc(ld_edge, 16)
                e.dma_start(src_i[:], a["src"]).then_inc(ld_edge, 16)
                e.dma_start(k["start"][:], a["start"]).then_inc(ld_edge, 16)
                e.dma_start(vec, a["vec"]).then_inc(ld_vec, 16)
                e.wait_ge(w_clear, 3)
                for half in range(2):
                    lo, hi = HID * half, HID * (half + 1)
                    e.dma_start(w["w0"][NB * half:NB * (half + 1), lo:hi], a["mlp_w0"]).then_inc(ld_w, 16)
                    e.dma_start(w["w1"][lo:hi, lo:hi], a["mlp_w1"]).then_inc(ld_w, 16)
                    e.dma_start(w["w2"][lo:hi, P * half:P * (half + 1)], a["mlp_w2"]).then_inc(ld_w, 16)
                    e.dma_start(w["b0"][lo:hi, :], a["mlp_b0"]).then_inc(ld_w, 16)
                    e.dma_start(w["b1"][lo:hi, :], a["mlp_b1"]).then_inc(ld_w, 16)
                e.dma_start(b2f[:], a["mlp_b2"].to_broadcast([3, P])).then_inc(ld_b2, 16)
                for n, span in enumerate(spans):
                    e.wait_ge(emb_ok, n + 1)
                    first, steps = span.start // HALF, (span.stop - span.start) // HALF
                    for g in range(ECH // 2):
                        at_step = SPC * g + first
                        e.dma_start(dram["emb"][at_step:at_step + steps].rearrange("s r n -> r s n"),
                                    emb[2 * NB * g:2 * NB * (g + 1), span].rearrange("r (s n) -> r s n", s=steps))\
                            .then_inc(emb_st, 16)
                e.wait_ge(clear_ok, 1)
                for s in range(3):
                    e.dma_start(dram["emb"][STEPS + s], k["zero"][0:2 * NB, :]).then_inc(stored, 16)
                e.wait_ge(idx_ok, 2)
                e.dma_start(dram["p_idx"], p_idx[:]).then_inc(stored, 16)
                e.dma_start(dram["q_idx"], q_idx[:]).then_inc(stored, 16)
                e.wait_ge(split_ok, 1)
                for r, part in enumerate((b2_hi, b2_mid, b2_lo)):
                    for tile in range(4):
                        e.dma_start(w["b2"][r:r + 1, P * tile:P * (tile + 1)], part[r:r + 1, :])\
                            .then_inc(stored, 16)
                e.wait_ge(stored, 16 * (3 + 2 + 12))
                e.wait_ge(emb_st, 16 * ECH)
                e.wait_ge(ld_w, 16 * 10)

            @block.scalar
            def _(e):
                e.wait_ge(up_clear, 1)
                e.dma_start(w_up[0:MUL, 0:MUL], a["W_up0"]).then_inc(ld_up, 16)
                for c in range(3):
                    e.dma_start(w_up[MUL + c:MUL + c + 3 * (MUL - 1) + 1:3, MUL * (c + 1):MUL * (c + 2)],
                                a["W_up1"]).then_inc(ld_up, 16)

                def node_table(g):
                    e.wait_ge(tr_ok, g + 1)
                    e.activation(x_t[:].rearrange("p (t n) -> p t n", t=GRP), ps_t[:, 0:GRP, :], ACT.Copy)\
                        .then_inc(xt_ok, 1)
                    e.wait_ge(mm_ok, g + 1)
                    if not isinstance(g, int):
                        e.wait_ge(tab_st, g * 16)
                    e.activation(tab[:], ps_m[:, 0:GRP, :], ACT.Copy, scale=float(MUL) ** -0.5)\
                        .then_inc(tab_ok, 1)

                node_table(0)
                with e.Fori(1, EARLY) as g:
                    node_table(g)
                e.wait_ge(g_own, 3)
                for n, span in enumerate(spans):
                    e.wait_ge(clip_ok, n + 1)
                    e.activation(emb[:, span], emb[:, span], ACT.Square, bias=centre[:], scale=float(NB - 1))\
                        .then_inc(s_own, 1)
                    e.wait_ge(s_own, n + 1)
                    e.activation(emb[:, span], emb[:, span], ACT.Exp, scale=-0.5).then_inc(exp_ok, 1)
                e.wait_ge(norm_ok, 1)
                e.activation(norm2[:], norm2[:], ACT.Sqrt).then_inc(root_ok, 1)
                with e.Fori(EARLY, NG) as g:
                    node_table(g)

            @block.gpsimd
            def _(e):
                own = Own(e, g_own)
                e.memset(w_up[:], 0.0).then_inc(up_clear, 1)
                own.then(e.memset(k["ident"][:], 0.0))
                own.then(e.affine_select(out=k["ident"][:], in_=k["ident"][:], compare_op=ALU.not_equal,
                                         fill=1.0, base=0, pattern=[[-1, P]], channel_multiplier=1))
                own.then(e.iota(centre_i[:], pattern=[[0, 1]], base=0, channel_multiplier=1))
                e.iota(k["iota"][:], pattern=[[1, T * P]], base=0, channel_multiplier=0,
                       allow_small_or_imprecise_dtypes=True)
                e.memset(w["w0"][:], 0.0).then_inc(w_clear, 1)
                e.memset(w["w1"][:], 0.0).then_inc(w_clear, 1)
                e.memset(w["w2"][:], 0.0).then_inc(w_clear, 1)
                e.memset(k["zero"][:], 0.0).then_inc(clear_ok, 1)
                x_g = a["x"].rearrange("(t p) f -> p t f", p=P)
                node0_g = dram["node0"].rearrange("(t p) f -> p t f", p=P)

                def load(g, h):
                    e.dma_start(x_in[:, h], x_g[:, bass.ds(g * GRP, GRP), :]).then_inc(ld_x[h], 16)

                def load_again(g, h):
                    e.wait_ge(tr_ok, g - 1)
                    e.sem_inc(gate, 1)
                    load(g, h)

                def store(g):
                    e.wait_ge(tab_ok, g + 1)
                    e.sem_inc(gate, 1)
                    e.dma_start(node0_g[:, bass.ds(g * GRP, GRP), :], tab[:]).then_inc(tab_st, 16)

                for g in range(2):
                    load(g, g)
                with e.Fori(0, (NG - 3) // 2) as i:
                    for h in range(2):
                        load_again(i * 2 + (h + 2), h)
                        store(i * 2 + h)
                load_again(NG - 1, 0)
                for g in range(NG - 3, NG):
                    store(g)
                e.wait_ge(tab_st, 16 * NG)

            @block.vector
            def _(e):
                own = Own(e, v_own)
                e.wait_ge(g_own, 3)
                own.then(e.tensor_scalar(centre_i[:], centre_i[:], NB - 1, None, ALU.bitwise_and))
                own.then(e.tensor_scalar(centre[:], centre_i[:], -1.0, None, ALU.mult))
                e.memset(acc[:, 0:2 * NACC], 0.0)
                e.wait_ge(ld_len, 16 * ECH)
                for span in spans:
                    own.then(e.tensor_scalar(mask[:, span], emb[:, span], 1.0, None, ALU.is_le))
                    e.tensor_scalar(emb[:, span], emb[:, span], 0.0, 1.0, ALU.max, ALU.min).then_inc(clip_ok, 1)
                e.wait_ge(ld_vec, 16)
                own.then(e.tensor_tensor(vec2, vec, vec, ALU.mult))
                e.tensor_reduce(norm2[:], vec2, AX.X, ALU.add).then_inc(norm_ok, 1)
                e.wait_ge(ld_edge, 16 * 5)
                own.did(e.tensor_copy(dstf[:], dst_i[:]))
                own.did(e.tensor_copy(startf[:], start_i[:]))
                own.did(e.tensor_copy(k["typef"][:], type_i[:]))
                own.then(e.tensor_copy(srcf[:], src_i[:]))
                pairs = "p (g t) -> p g t"
                own.did(e.scalar_tensor_tensor(p_idx[:], srcf[:], float(T), k["typef"][:], ALU.mult, ALU.add))
                own.did(e.scalar_tensor_tensor(q_idx[:], dstf[:], float(T), k["typef"][:], ALU.mult, ALU.add))
                own.then(e.tensor_tensor(k["dloc"][:].rearrange(pairs, t=2), dstf[:].rearrange(pairs, t=2),
                                         spread(startf[:], 2, 2), ALU.subtract))
                e.sem_inc(idx_ok, 2)
                for n, span in enumerate(spans):
                    e.wait_ge(exp_ok, n + 1)
                    e.scalar_tensor_tensor(emb[:, span], emb[:, span], float(NB) ** 0.5, mask[:, span],
                                           ALU.mult, ALU.mult).then_inc(emb_ok, 1)
                own.did(e.scalar_tensor_tensor(k["key"][:], k["dloc"][:], float(T), k["typef"][:],
                                               ALU.mult, ALU.add))
                own.then(e.tensor_scalar(hit[:], k["dloc"][:], 0.0, None, ALU.is_ge))
                own.then(e.scalar_tensor_tensor(hit[:], k["dloc"][:], float(WIN), hit[:], ALU.is_lt, ALU.mult))
                own.did(e.scalar_tensor_tensor(k["left"][:], hit[:], -FAR, dstf[:], ALU.mult, ALU.add))
                own.did(e.memset(one[:], 1.0))
                e.memset(w["ones"][:], 1.0)
                e.tensor_reduce(n_hit[:], hit[:, 0:TILES], AX.X, ALU.add).then_inc(hits_ok, 1)
                e.wait_ge(root_ok, 1)
                own.then(e.tensor_scalar(norm2[:], norm2[:], 1e-12, None, ALU.add))
                own.then(e.reciprocal(norm2[:], norm2[:]))
                own.then(e.tensor_scalar(norm2[:], norm2[:], 3.0 ** 0.5, None, ALU.mult))
                own.did(e.tensor_tensor(w["y"][:], vec, spread(norm2[:], 2, 3), ALU.mult))
                e.wait_ge(ld_b2, 16)
                split3(e, own, b2f[:], b2_hi[:], b2_mid[:], b2_lo[:], b2f[:])
                e.sem_inc(split_ok, 1)
                e.wait_ge(count_ok, 1)
                e.tensor_scalar(k["n_left"][:], ps_n[:], -1.0, float(P * TILES), ALU.mult, ALU.add)

            @block.tensor
            def _(e):
                e.wait_ge(g_own, 2)
                e.wait_ge(ld_up, 16 * 4)

                def node_table(g, h, loaded):
                    e.wait_ge(ld_x[h], loaded)
                    for t in range(GRP):
                        last = e.transpose(ps_t[:, t, :], x_in[:, h, t, :], k["ident"][:])
                    last.then_inc(tr_ok, 1)
                    e.wait_ge(xt_ok, g + 1)
                    if not isinstance(g, int) or g:
                        e.wait_ge(tab_ok, g)
                    for t in range(GRP):
                        last = e.matmul(ps_m[:, t, :], x_t[:, t * P:(t + 1) * P], w_up[:], start=True, stop=True)
                    last.then_inc(mm_ok, 1)

                node_table(0, 0, 16)
                with e.Fori(0, (NG - 1) // 2) as i:
                    node_table(i * 2 + 1, 1, i * 16 + 16)
                    node_table(i * 2 + 2, 0, i * 16 + 32)
                e.wait_ge(hits_ok, 1)
                e.matmul(ps_n[:], n_hit[:], one[:], start=True, stop=True).then_inc(count_ok, 1)


def start_registers(e, tag):
    return [e.alloc_register(f"{tag}_start{p}") for p in range(PPS)]


def run_starts(e, k, j, regs):
    e.load(regs, k["start"][0:1, bass.ds(j * PPS, PPS)])
    return [e.snap(r, min_val=0, max_val=N) for r in regs]


def gather_loop(e, idx, idx_in, table, buf, landed, used, gate):
    with e.Fori(0, STEPS // 2) as i:
        for h in range(2):
            e.wait_ge(idx_in[h], i * 16 + 16)
            e.sem_inc(gate, 1)
            e.wait_ge(used, i * 2 + (h + 1))
            e.sem_inc(gate, 1)
            for t in range(TPS):
                e.indirect_dma_start(
                    out=buf[:, h, t, :], out_offset=None, in_=table,
                    in_offset=bass.IndirectOffsetOnAxis(ap=idx[:, h, t:t + 1], axis=0),
                ).then_inc(landed[h], 16)


def tiles_of(x):
    return x.rearrange("p t (i m) -> p t i m", m=MUL)


def upper(x):
    return x.bitcast(bf16).rearrange("p (n two) -> p n two", two=2)[:, :, 1]


def layer0_mlp1(e, w, emb, ps_h):
    return e.matmul(ps_h[:], w["w0"][:], emb, start=True, stop=True)


def layer0_mlp3(e, w, h2, ps_w):
    for bank in range(2):
        e.matmul(ps_w[:, 4 * bank:4 * bank + 4, :], w["ones"][:], w["b2"][:], start=True, stop=False)
    for t in range(PPS):
        last = e.matmul(ps_w[:, 2 * t:2 * t + 2, :], h2[:, t * P:(t + 1) * P], w["w2"][:], start=False,
                        stop=t % 2 == 1)
    return last


class Messages:

    def __init__(self, m, tag, tiles):
        self.split = slice(0, tiles * H)
        self.msg = m.sb("msg" + tag, [P, 2, TPS * H])
        self.rest = m.sb("rest" + tag, [P, 2, tiles * H])
        self.low = m.sb("low" + tag, [P, 2, tiles * H], bf16)
        self.ws = m.sb("ws" + tag, [P, TPS, MUL])
        self.vy = m.sb("vy" + tag, [P, TPS, 3, MUL])
        self.cols = [self.msg[:, b, :].rearrange("p (t i m) -> p t i m", t=TPS, m=MUL) for b in range(2)]

    def ws_product(self, e, wt, s):
        return e.tensor_tensor(self.ws[:], wt[:, :, 1, :], s, ALU.mult)

    def vy_product(self, e, v, y):
        return e.tensor_tensor(self.vy[:], v, spread(y, 3, MUL), ALU.mult)

    def w0_product(self, e, wt, s):
        return e.tensor_tensor(self.cols[0][:, :, 3, :], wt[:, :, 0, :], s, ALU.mult)

    def w2_product(self, e, wt, v):
        return e.tensor_tensor(self.cols[0][:, :, 0:3, :], spread(wt[:, :, 2, :], 2, 3), v, ALU.mult)

    def dot_sum(self, e, c):
        return e.tensor_tensor(self.vy[:, :, 0, :], self.vy[:, :, 0, :], self.vy[:, :, c, :], ALU.add)

    def w3_product(self, e, wt):
        return e.tensor_tensor(self.cols[1][:, :, 3, :], wt[:, :, 3, :], self.vy[:, :, 0, :], ALU.mult)

    def by_component(self, e, tile, y):
        for c in range(3):
            last = e.activation(self.cols[1][:, tile, c, :], self.ws[:, tile, :], ACT.Copy, scale=y[:, c:c + 1])
        return last

    def split_rest(self, e, b):
        whole = self.msg[:, b, self.split]
        return e.tensor_tensor(self.rest[:, b, :], whole, upper(whole), ALU.subtract)

    def split_low(self, e, b):
        return e.tensor_tensor(self.low[:, b, :], self.rest[:, b, :], upper(self.rest[:, b, :]), ALU.subtract)

    def whole(self, tile, b):
        return self.msg[:, b, tile * H:(tile + 1) * H]

    def parts(self, tile, b):
        at = slice(tile * H, (tile + 1) * H)
        return [upper(self.msg[:, b, at]), upper(self.rest[:, b, at]), self.low[:, b, at]]


def edges0(nc, a, k, dram, w, later):
    with ExitStack() as ctx:
        m = Mem(nc, ctx)
        idx = m.sb("idx0", [P, 2, TPS], u32)
        emb = m.sb("emb0", [2 * NB, 2, HALF])
        gx = m.sb("gx0", [P, 2, TPS, H])
        h1, h2 = m.sb("h1", [P, HALF]), m.sb("h2", [P, HALF])
        msgs = [Messages(m, str(h), SPLIT) for h in range(2)]
        hot = m.sb("hot0", [P, 2, SPLIT, WIN], bf16)
        hot32 = m.sb("hot32", [P, 2, TPS - SPLIT, WIN])
        ps_h1, ps_h2 = m.ps("ps_h1", [P, HALF]), m.ps("ps_h2", [P, HALF])
        ps_w = m.ps("ps_w", [P, 2, TPS, H])
        ps_a = m.ps("ps_a", [P, 2, 2 * PPS, 2, WIN])
        idx_in, emb_in, landed = m.sems("idx_in", 2), m.sems("emb_in", 2), m.sems("landed", 2)
        used, gate, h1_mm, h1_ok, h2_mm, h2_ok, w_mm, plain_ok, ws_ok, y_ok, own, msg_ok, sum_mm, acc_own = (
            m.sem(n) for n in ("used", "gate0", "h1_mm", "h1_ok", "h2_mm", "h2_ok", "w_mm", "plain_ok", "ws_ok",
                               "y_ok", "own0", "msg_ok", "sum_mm", "acc_own"))
        later_ld = m.sem("later_ld")
        src_v = a["src"].bitcast(u32)

        with nc.Block() as block:

            @block.sync
            def _(e):
                for h in range(2):
                    e.dma_start(idx[:, h, :], src_v[:, h * TPS:(h + 1) * TPS]).then_inc(idx_in[h], 16)
                    e.dma_start(emb[:, h, :], dram["emb"][h]).then_inc(emb_in[h], 16)
                n_later = load_later(e, a, later, later_ld)
                with e.Fori(0, STEPS // 2) as i:
                    for h in range(2):
                        e.wait_ge(h1_mm, i * 2 + (h + 1))
                        e.dma_start(emb[:, h, :], dram["emb"][bass.ds(i * 2 + (h + 2), 1)]
                                    .rearrange("s r n -> (s r) n")).then_inc(emb_in[h], 16)
                        e.wait_ge(landed[h], i * (16 * TPS) + 16 * TPS)
                        e.dma_start(idx[:, h, :], src_v[:, bass.ds(i * (2 * TPS) + (h + 2) * TPS, TPS)])\
                            .then_inc(idx_in[h], 16)
                e.wait_ge(later_ld, 16 * n_later)
                e.wait_ge(h1_mm, STEPS + 1)
                e.dma_start(emb[:, 0, :], dram["emb"][STEPS + 2]).then_inc(emb_in[0], 16)
                for h in range(2):
                    e.wait_ge(emb_in[h], 16 * (STEPS // 2 + 2 - h))
                    e.wait_ge(idx_in[h], 16 * (STEPS // 2 + 1))

            @block.gpsimd
            def _(e):
                gather_loop(e, idx, idx_in, dram["node0"], gx, landed, used, gate)

            @block.scalar
            def _(e):
                def silu(out, ps, bias, mm, ok, value):
                    e.wait_ge(mm, value)
                    e.activation(out[:], ps[:], ACT.Silu, bias=bias[:]).then_inc(ok, 1)

                e.preload_act_table(ACT.Silu)
                for n in range(2):
                    silu(h1, ps_h1, w["b0"], h1_mm, h1_ok, n + 1)
                    silu(h2, ps_h2, w["b1"], h2_mm, h2_ok, n + 1)
                with e.Fori(0, STEPS // 2) as i:
                    for h in range(2):
                        e.wait_ge(ws_ok, i * 2 + (h + 1))
                        for t in range(TPS):
                            last = msgs[h].by_component(e, t, w["y"][:, bass.ds(i * (2 * TPS) + (h * TPS + t), 1), :]
                                                        .rearrange("p t c -> p (t c)"))
                        last.then_inc(y_ok, 1)
                        silu(h1, ps_h1, w["b0"], h1_mm, h1_ok, i * 2 + (h + 3))
                        silu(h2, ps_h2, w["b1"], h2_mm, h2_ok, i * 2 + (h + 3))

            @block.tensor
            def _(e):
                def first(h, emb_value):
                    e.wait_ge(emb_in[h], emb_value)
                    layer0_mlp1(e, w, emb[:, h, :], ps_h1).then_inc(h1_mm, 1)

                def second(value):
                    e.wait_ge(h1_ok, value)
                    e.matmul(ps_h2[:], w["w1"][:], h1[:], start=True, stop=True).then_inc(h2_mm, 1)

                def third(h, value):
                    e.wait_ge(h2_ok, value)
                    layer0_mlp3(e, w, h2, ps_w[:, h]).then_inc(w_mm, 1)

                first(0, 16)
                second(1)
                first(1, 16)
                third(0, 1)
                second(2)
                first(0, 32)
                e.sem_inc(plain_ok, 1)
                with e.Fori(0, STEPS // 2) as i:
                    for h in range(2):
                        e.wait_ge(plain_ok, i * 2 + (h + 1))
                        third(1 - h, i * 2 + (h + 2))
                        second(i * 2 + (h + 3))
                        first(1 - h, i * 16 + (32 + 16 * h))
                        e.wait_ge(msg_ok, i * 2 + (h + 1))
                        for p in range(PPS):
                            for b in range(2):
                                terms = []
                                for tile in (2 * p, 2 * p + 1):
                                    if tile < SPLIT:
                                        terms += [(part, hot[:, h, tile, :]) for part in msgs[h].parts(tile, b)]
                                    else:
                                        terms.append((msgs[h].whole(tile, b), hot32[:, h, tile - SPLIT, :]))
                                for n, (lhs, rhs) in enumerate(terms):
                                    last = e.matmul(ps_a[:, h, p, b, :], lhs, rhs, start=n == 0,
                                                    stop=n == len(terms) - 1)
                        last.then_inc(sum_mm, 1)

            @block.vector
            def _(e):
                acc = k["acc"][:, 0:2 * NACC].rearrange("p (b n) -> p b n", b=2)
                regs = start_registers(e, "sum0")

                def one_hot(j, h):
                    for to, lo, n in ((hot, 0, SPLIT), (hot32, SPLIT, TPS - SPLIT)):
                        e.tensor_tensor(to[:, h], spread(k["iota"][:, 0:WIN], 1, n),
                                        spread(k["dloc"][:, bass.ds(j * TPS + lo, n)], 2, WIN), ALU.is_equal)

                def messages(i, h, before):
                    j = i * 2 + h
                    wt, x, mine = tiles_of(ps_w[:, h]), tiles_of(gx[:, h]), msgs[h]
                    s, v, y = x[:, :, 0, :], x[:, :, 1:4, :], w["y"][:, bass.ds(j * TPS, TPS), :]
                    done = [0]

                    def did(ins):
                        ins.then_inc(own, 1)
                        done[0] += 1
                        return j * OWN + done[0]

                    add = (lambda p: None) if not before else start_windows(j - 1, 1 - h)
                    e.wait_ge(landed[h], i * (16 * TPS) + 16 * TPS)
                    e.wait_ge(w_mm, j + 1)
                    mine.ws_product(e, wt, s).then_inc(ws_ok, 1)
                    vy = did(mine.vy_product(e, v, y))
                    w0 = did(mine.w0_product(e, wt, s))
                    e.wait_ge(own, vy)
                    sum_1 = did(mine.dot_sum(e, 1))
                    w2 = did(mine.w2_product(e, wt, v))
                    e.wait_ge(own, sum_1)
                    sum_2 = did(mine.dot_sum(e, 2))
                    add(0)
                    e.wait_ge(own, w2)
                    e.sem_inc(used, 1)
                    rest = did(mine.split_rest(e, 0))
                    e.wait_ge(own, sum_2)
                    mine.w3_product(e, wt).then_inc(plain_ok, 1)
                    add(1)
                    e.wait_ge(own, rest)
                    mine.split_low(e, 0)
                    add(2)
                    one_hot(j + 1, 1 - h)
                    add(3)
                    e.wait_ge(y_ok, j + 1)
                    e.wait_ge(plain_ok, j + 2)
                    rest = did(mine.split_rest(e, 1))
                    e.wait_ge(own, rest)
                    mine.split_low(e, 1).then_inc(msg_ok, 1)
                    assert done[0] == OWN and PPS == 4

                def start_windows(j, h):
                    starts = run_starts(e, k, j, regs)

                    def add(p):
                        at = acc[:, :, bass.ds(starts[p], WIN)]
                        e.wait_ge(sum_mm, j + 1)
                        e.wait_ge(acc_own, j * PPS + (p + 1))
                        e.tensor_tensor(at, at, ps_a[:, h, p], ALU.add).then_inc(acc_own, 1)
                    return add

                OWN = 7
                e.sem_inc(used, 2)
                e.sem_inc(acc_own, 1)
                one_hot(0, 0)
                messages(0, 0, False)
                with e.Fori(0, STEPS // 2 - 1) as i:
                    messages(i, 1, True)
                    messages(i + 1, 0, True)
                messages(STEPS // 2 - 1, 1, True)
                add = start_windows(STEPS - 1, 1)
                for p in range(PPS):
                    add(p)
                e.wait_ge(acc_own, STEPS * PPS + 1)


class Turns:

    def __init__(self, turn, gate):
        self.turn, self.gate = turn, gate

    def length(self, plan):
        return sum(x[0] * self.length(x[1]) if isinstance(x[0], int) else 1 for x in plan)

    def emit(self, e, name, plan, done=0, index=()):
        for x in plan:
            if isinstance(x[0], int):
                count, body = x
                size = self.length(body)
                with e.Fori(0, count) as r:
                    self.emit(e, name, body, r * size + done, (*index, r))
                done = done + count * size
            else:
                who, work = x
                if who == name:
                    e.wait_ge(self.turn, done + 1)
                    e.sem_inc(self.gate, 1)
                    work(e, index).then_inc(self.turn, 1)
                done = done + 1


def run_if_left(nc, k, m, layer, plan):
    turns = Turns(m.sem("turn"), m.sem("turn_gate"))
    with nc.Block() as block:
        def part(name):
            def run(e):
                flag = e.alloc_register(f"left{layer}_{name}")
                e.load([flag], k["n_left"][0:1, 0:1])
                with e.If_ne(flag, 0):
                    if name == "sync":
                        e.sem_inc(turns.turn, 1)
                    turns.emit(e, name, plan)
            return run
        for name, where in (("sync", block.sync), ("gpsimd", block.gpsimd), ("scalar", block.scalar),
                            ("tensor", block.tensor), ("vector", block.vector)):
            where(part(name))


def arrived(e, sem, value, turn_nop):
    e.wait_ge(sem, value)
    e.sem_inc(turn_nop, 1)
    return e.nop()


def gather_all(e, idx, table, buf, sem):
    for t in range(TPS):
        e.indirect_dma_start(out=buf[:, t, :], out_offset=None, in_=table,
                             in_offset=bass.IndirectOffsetOnAxis(ap=idx[:, t:t + 1], axis=0)).then_inc(sem, 16)


def leftover0(nc, a, k, dram, w):
    with ExitStack() as ctx:
        m = Mem(nc, ctx)
        idx, emb = m.sb("idx_l", [P, TPS], u32), m.sb("emb_l", [2 * NB, HALF])
        gx, msgs = m.sb("gx_l", [P, TPS, H]), Messages(m, "_l", TPS)
        h1, h2 = m.sb("h1_l", [P, HALF]), m.sb("h2_l", [P, HALF])
        hot, at_node = m.sb("hot_l", [P, TPS, P], bf16), m.sb("at_node", [P, TPS])
        ps_h, ps_w, ps_a = m.ps("ps_hl", [P, HALF]), m.ps("ps_wl", [P, TPS, H]), m.ps("ps_al", [P, 2, P])
        in_l, gather_l, nop = m.sem("in_l"), m.sem("gather_l"), m.sem("nop_l")
        src_v = a["src"].bitcast(u32)
        acc = k["acc"][:, 0:2 * NACC].rearrange("p (b n) -> p b n", b=2)
        wt, x = tiles_of(ps_w[:]), tiles_of(gx[:])

        def load(e, index):
            j, = index
            e.dma_start(emb[:], dram["emb"][bass.ds(j, 1)].rearrange("s r n -> (s r) n")).then_inc(in_l, 16)
            e.dma_start(idx[:], src_v[:, bass.ds(j * TPS, TPS)]).then_inc(in_l, 16)
            return arrived(e, in_l, j * 32 + 32, nop)

        def gather(e, index):
            gather_all(e, idx, dram["node0"], gx, gather_l)
            return arrived(e, gather_l, index[0] * (16 * TPS) + 16 * TPS, nop)

        def messages(e, index):
            e.tensor_copy(at_node[:], k["left"][:, bass.ds(index[0] * TPS, TPS)])
            msgs.ws_product(e, wt, x[:, :, 0, :])
            msgs.w0_product(e, wt, x[:, :, 0, :])
            msgs.w2_product(e, wt, x[:, :, 1:4, :])
            return msgs.vy_product(e, x[:, :, 1:4, :], w["y"][:, bass.ds(index[0] * TPS, TPS), :])

        def by_component(e, index):
            for t in range(TPS):
                last = msgs.by_component(e, t, w["y"][:, bass.ds(index[0] * TPS + t, 1), :]
                                         .rearrange("p t c -> p (t c)"))
            return last

        def both(split):
            def work(e, index):
                split(e, 0)
                return split(e, 1)
            return work

        def match(e, index):
            return e.tensor_tensor(hot[:], spread(k["iota"][:, 0:P], 1, TPS), spread(at_node[:], 2, P),
                                   ALU.is_equal)

        def sums(e, index):
            for b in range(2):
                for t in range(TPS):
                    for n, part in enumerate(msgs.parts(t, b)):
                        last = e.matmul(ps_a[:, b, :], part, hot[:, t, :], start=t + n == 0,
                                        stop=t + n == TPS + 1)
            return last

        def add(e, index):
            at = acc[:, :, bass.ds(index[1] * P, P)]
            e.tensor_scalar(at_node[:], at_node[:], float(P), None, ALU.subtract)
            return e.tensor_tensor(at, at, ps_a[:], ALU.add)

        run_if_left(nc, k, m, 0, [(STEPS, [
            ("sync", load), ("gpsimd", gather),
            ("tensor", lambda e, _: layer0_mlp1(e, w, emb[:], ps_h)),
            ("scalar", lambda e, _: e.activation(h1[:], ps_h[:], ACT.Silu, bias=w["b0"][:])),
            ("tensor", lambda e, _: e.matmul(ps_h[:], w["w1"][:], h1[:], start=True, stop=True)),
            ("scalar", lambda e, _: e.activation(h2[:], ps_h[:], ACT.Silu, bias=w["b1"][:])),
            ("tensor", lambda e, _: layer0_mlp3(e, w, h2, ps_w)),
            ("vector", messages), ("scalar", by_component),
            ("vector", lambda e, _: msgs.dot_sum(e, 1)), ("vector", lambda e, _: msgs.dot_sum(e, 2)),
            ("vector", lambda e, _: msgs.w3_product(e, wt)),
            ("vector", both(msgs.split_rest)), ("vector", both(msgs.split_low)),
            (NT, [("vector", match), ("tensor", sums), ("vector", add)]),
        ])])


def leftover1(nc, k, dram):
    with ExitStack() as ctx:
        m = Mem(nc, ctx)
        idx, idx_q = m.sb("idx_r", [P, TPS], u32), m.sb("idx_rq", [P, TPS], u32)
        gp, gq = m.sb("gp_r", [P, TPS, PW]), m.sb("gq_r", [P, TPS, PW])
        hid, score = m.sb("hid_r", [P, TPS, H]), m.sb("score_r", [P, TPS])
        sc_t = m.sb("sc_tr", [P, TPS, T])
        hot, hot_n = m.sb("hot_r", [P, TPS, T * P]), m.sb("hot_nr", [P, TPS, P])
        at_key, at_node = m.sb("at_key", [P, TPS]), m.sb("at_node_r", [P, TPS])
        ps_g, ps_s = m.ps("ps_gr", [P, T * P]), m.ps("ps_sr", [T, P])
        in_r, gather_r, nop = m.sem("in_r"), m.sem("gather_r"), m.sem("nop_r")

        def load(e, index):
            j, = index
            cols = bass.ds(j * TPS, TPS)
            e.dma_start(idx[:], dram["p_idx"][:, cols]).then_inc(in_r, 16)
            e.dma_start(idx_q[:], dram["q_idx"][:, cols]).then_inc(in_r, 16)
            return arrived(e, in_r, j * 32 + 32, nop)

        def gather(e, index):
            gather_all(e, idx, dram["p_tab"], gp, gather_r)
            gather_all(e, idx_q, dram["q_tab"], gq, gather_r)
            return arrived(e, gather_r, index[0] * (32 * TPS) + 32 * TPS, nop)

        def add_rows(e, index):
            cols = bass.ds(index[0] * TPS, TPS)
            e.tensor_copy(at_node[:], k["left"][:, cols])
            e.scalar_tensor_tensor(at_key[:], k["left"][:, cols], float(T), k["typef"][:, cols], ALU.mult, ALU.add)
            e.tensor_tensor(sc_t[:], spread(k["iota"][:, 0:T], 1, TPS), spread(k["typef"][:, cols], 2, T),
                            ALU.is_equal)
            return e.tensor_tensor(gp[:], gp[:], gq[:], ALU.add)

        def hidden(e, index):
            for t in range(TPS):
                last = e.activation(hid[:, t, :], gp[:, t, 0:H], ACT.Relu, scale=score[:, t:t + 1])
            return last

        def match(e, index):
            e.tensor_tensor(hot_n[:], spread(k["iota"][:, 0:P], 1, TPS), spread(at_node[:], 2, P), ALU.is_equal)
            return e.tensor_tensor(hot[:], spread(k["iota"][:], 1, TPS), spread(at_key[:], 2, T * P), ALU.is_equal)

        def sums(e, index):
            for t in range(TPS):
                e.matmul(ps_g[:], hid[:, t, :], hot[:, t, :], start=t == 0, stop=t == TPS - 1)
            for t in range(TPS):
                last = e.matmul(ps_s[:], sc_t[:, t, :], hot_n[:, t, :], start=t == 0, stop=t == TPS - 1)
            return last

        def add(e, index):
            at = k["acc"][:, bass.ds(index[1] * (T * P), T * P)]
            at_s = k["acc_s"][0:T, bass.ds(index[1] * P, P)]
            e.tensor_scalar(at_node[:], at_node[:], float(P), None, ALU.subtract)
            e.tensor_scalar(at_key[:], at_key[:], float(T * P), None, ALU.subtract)
            e.tensor_tensor(at_s, at_s, ps_s[:], ALU.add)
            return e.tensor_tensor(at, at, ps_g[:], ALU.add)

        run_if_left(nc, k, m, 1, [(STEPS, [
            ("sync", load), ("gpsimd", gather), ("vector", add_rows),
            ("scalar", lambda e, _: e.activation(score[:], gp[:, :, H], ACT.Sigmoid)),
            ("vector", lambda e, _: e.tensor_tensor(sc_t[:], sc_t[:], spread(score[:], 2, T), ALU.mult)),
            ("scalar", hidden),
            (NT, [("vector", match), ("tensor", sums), ("vector", add)]),
        ])])


def between(nc, a, k, dram, later):
    with ExitStack() as ctx:
        m = Mem(nc, ctx)
        out_a, out_b, att, att_b, w_p, w_q, bias_q = (later[n] for n in (
            "out_a", "out_b", "att", "att_b", "w_p", "w_q", "bias_q"))
        w_out = m.sb("w_out", [P, 2, H])
        x_in, x1 = m.sb("x_in1", [P, GRP, H]), m.sb("x1", [P, GRP, H])
        x1_t = m.sb("x1_t", [P, GRP * P])
        sums = m.sb("sums", [P, 2, GRP * P])
        zero = m.sb("zero_b", [P, GRP * P])
        p_buf, q_buf = m.sb("p_buf", [P, GRP, T * PW]), m.sb("q_buf", [P, GRP, T * PW])
        stats, mv, rstd = m.sb("stats", [P, GRP, 6]), m.sb("mv", [P, GRP, 2]), m.sb("rstd", [P, GRP])
        ps_o, ps_t = m.ps("ps_o", [P, 8, P]), m.ps("ps_t1", [P, 8, P])
        ps_p, ps_q = m.ps("ps_p", [P, 2, 512]), m.ps("ps_q", [P, 2, 512])
        w_clear, w_ok, x_ld, x_used, o_mm, sum_ok, var_ok, root_ok, x1_ok, gate = (
            m.sem(n + "_b") for n in ("w_clear", "w_ok", "x_ld", "x_used", "o_mm",
                                      "sum_ok", "var_ok", "root_ok", "x1_ok", "gate"))
        gate_v, sums_ok = m.sem("gate_vb"), m.sem("sums_ok")
        t1_mm, t1_ok, p_mm, q_mm, p_ok, q_ok, x1_st, xt_st, z_st = (
            m.sem(n + "_b") for n in ("t1_mm", "t1_ok", "p_mm", "q_mm", "p_ok", "q_ok", "x1_st", "xt_st", "z_st"))
        p_st, q_st = m.sems("p_st", 2), m.sems("q_st", 2)
        pieces = (slice(0, 4), slice(4, GRP))
        x_g = a["x"].rearrange("(t p) f -> p t f", p=P)
        x1_g = dram["x1"].rearrange("(t p) f -> p t f", p=P)
        p_g = dram["p_tab"].rearrange("(t p y) f -> p t (y f)", p=P, y=T)
        q_g = dram["q_tab"][0:NP * T, :].rearrange("(t p y) f -> p t (y f)", p=P, y=T)

        with nc.Block() as block:

            @block.sync
            def _(e):
                pad = (NACC - NP) * T
                e.dma_start(dram["q_tab"][NP * T:NACC * T, :], k["zero"][0:pad, 0:PW]).then_inc(z_st, 16)
                for s in (*p_st, *q_st, x1_st, xt_st):
                    e.sem_inc(s, 16)

                def store_x1(g):
                    e.wait_ge(x1_ok, g + 1)
                    e.dma_start(x1_g[:, bass.ds(g * GRP, GRP), :], x1[:]).then_inc(x1_st, 16)

                def store_x1_t(g):
                    e.wait_ge(t1_ok, g + 1)
                    e.dma_start(dram["x1_t"][:, bass.ds(g * (GRP * P), GRP * P)], x1_t[:]).then_inc(xt_st, 16)

                def store_tables(g, n):
                    piece = pieces[n]
                    some = bass.ds(g * GRP + piece.start, piece.stop - piece.start)
                    for ok, to, buf, st in ((p_ok, p_g, p_buf, p_st[n]), (q_ok, q_g, q_buf, q_st[n])):
                        e.wait_ge(ok, g * GRP + (piece.stop + 1))
                        e.dma_start(to[:, some, :], buf[:, piece, :]).then_inc(st, 16)

                store_x1(0)
                store_x1_t(0)
                with e.Fori(0, NG - 1) as g:
                    store_tables(g, 0)
                    store_x1(g + 1)
                    store_tables(g, 1)
                    store_x1_t(g + 1)
                for n in range(2):
                    store_tables(NG - 1, n)
                for s in (*p_st, *q_st, x1_st, xt_st):
                    e.wait_ge(s, 16 * (NG + 1))
                e.wait_ge(z_st, 16)

            @block.gpsimd
            def _(e):
                e.memset(w_out[:], 0.0).then_inc(w_clear, 1)
                acc = k["acc"][:, 0:2 * NACC].rearrange("p (b n) -> p b n", b=2)
                e.sem_inc(o_mm, 1)
                e.sem_inc(x_used, 1)

                def load(g):
                    e.wait_ge(x_used, g + 1)
                    e.sem_inc(gate, 1)
                    e.dma_start(x_in[:], x_g[:, bass.ds(g * GRP, GRP), :]).then_inc(x_ld, 16)

                def copy(g):
                    e.wait_ge(o_mm, g + 1)
                    e.tensor_copy(sums[:], acc[:, :, bass.ds(g * (GRP * P), GRP * P)]).then_inc(sums_ok, 1)

                copy(0)
                load(0)
                with e.Fori(1, NG) as g:
                    load(g)
                    copy(g)
                e.memset(acc[:, :, NP:], 0.0)
                e.memset(k["acc"][:, 2 * NACC:], 0.0)

            @block.scalar
            def _(e):
                def root(g):
                    e.wait_ge(var_ok, g + 1)
                    e.activation(rstd[:], rstd[:], ACT.Sqrt).then_inc(root_ok, 1)

                def nodes_t(g):
                    e.wait_ge(t1_mm, g + 1)
                    e.wait_ge(xt_st, g * 16 + 16)
                    e.activation(x1_t[:].rearrange("p (t n) -> p t n", t=GRP), ps_t[:, 0:GRP, :], ACT.Copy)\
                        .then_inc(t1_ok, 1)

                def sender(g, t):
                    e.wait_ge(p_mm, g * GRP + (t + 1))
                    for n, piece in enumerate(pieces):
                        if t == piece.start:
                            e.wait_ge(p_st[n], g * 16 + 16)
                    e.activation(p_buf[:, t, :].rearrange("p (b n) -> p b n", b=2), ps_p[:, :, 0:2 * PW],
                                 ACT.Copy).then_inc(p_ok, 1)

                e.preload_act_table(ACT.Sqrt)
                root(0)
                nodes_t(0)
                with e.Fori(0, NG - 1) as g:
                    for t in range(GRP):
                        sender(g, t)
                        if t == 3:
                            root(g + 1)
                    nodes_t(g + 1)
                for t in range(GRP):
                    sender(NG - 1, t)

            @block.tensor
            def _(e):
                wp, wq = (x[:].rearrange("p t n -> p (t n)") for x in (w_p, w_q))

                def layer0_out(g):
                    e.wait_ge(sums_ok, g + 1)
                    for t in range(GRP):
                        for b in range(2):
                            last = e.matmul(ps_o[:, t, :], sums[:, b, t * P:(t + 1) * P],
                                            w_out[:, b, :], start=b == 0, stop=b == 1)
                    last.then_inc(o_mm, 1)

                def transposes(g):
                    e.wait_ge(x1_ok, g + 1)
                    for t in range(GRP):
                        last = e.transpose(ps_t[:, t, :], x1[:, t, :], k["ident"][:])
                    last.then_inc(t1_mm, 1)

                def tables(g):
                    e.wait_ge(t1_ok, g + 1)
                    for t in range(GRP):
                        lhs = x1_t[:, t * P:(t + 1) * P]
                        for wt, ps, mm, ok in ((wp, ps_p, p_mm, p_ok), (wq, ps_q, q_mm, q_ok)):
                            e.wait_ge(ok, g * GRP + (t + 1))
                            for b in range(2):
                                last = e.matmul(ps[:, b, 0:2 * PW], lhs, wt[:, 2 * PW * b:2 * PW * (b + 1)],
                                                start=True, stop=True)
                            last.then_inc(mm, 1)

                for s in (p_ok, q_ok):
                    e.sem_inc(s, 1)
                e.wait_ge(w_ok, 1)
                layer0_out(0)
                transposes(0)
                layer0_out(1)
                with e.Fori(0, NG - 2) as g:
                    tables(g)
                    transposes(g + 1)
                    layer0_out(g + 2)
                tables(NG - 2)
                transposes(NG - 1)
                tables(NG - 1)

            @block.vector
            def _(e):
                e.wait_ge(w_clear, 1)
                for c in range(3):
                    rows, vec = slice(MUL * c, MUL * (c + 1)), slice(MUL + c, MUL + c + 3 * (MUL - 1) + 1, 3)
                    e.tensor_copy(w_out[rows, 0, vec], out_a[rows, :])
                    e.tensor_copy(w_out[rows, 1, vec], out_b[rows, :])
                e.tensor_copy(w_out[3 * MUL:P, 0, 0:MUL], out_a[3 * MUL:P, :])
                e.tensor_scalar(w_out[3 * MUL:P, 1, 0:MUL], out_b[3 * MUL:P, :], 3.0 ** -0.5, None, ALU.mult)
                e.tensor_copy(bias_q[:, :, H], att_b[:])
                e.tensor_copy(w_p[:, :, H], att[:, 0, :])
                e.tensor_copy(w_q[:, :, H], att[:, 1, :]).then_inc(w_ok, 1)
                bias = bias_q[:].rearrange("p (b t) n -> p b (t n)", b=2)
                acc = k["acc"][:, 0:2 * NACC].rearrange("p (b n) -> p b n", b=2)
                zeros = spread(zero[:], 1, 2)
                e.memset(zero[:], 0.0).then_inc(w_clear, 1)

                def residual(g):
                    e.wait_ge(o_mm, g + 2)
                    e.wait_ge(x_ld, g * 16 + 16)
                    e.wait_ge(x1_st, g * 16 + 16)
                    e.scalar_tensor_tensor(x1[:], ps_o[:, 0:GRP, :], 1.0 / ((2 * MUL) ** 0.5 * 16.0), x_in[:],
                                           ALU.mult, ALU.add).then_inc(sum_ok, 1)

                def statistics(g, tiles):
                    if tiles.start == 0:
                        e.wait_ge(sum_ok, g * 4 + 1)
                        e.sem_inc(x_used, 1)
                    for t in range(tiles.start, tiles.stop):
                        last = e.bn_stats(stats[:, t, :], x1[:, t, :])
                    if tiles.stop == GRP:
                        last.then_inc(sum_ok, 1)

                def variance(g):
                    e.wait_ge(sum_ok, g * 4 + 2)
                    e.sem_inc(gate_v, 1)
                    for t in range(GRP):
                        last = e.bn_aggr(mv[:, t, :], stats[:, t, :])
                    last.then_inc(sum_ok, 1)
                    e.wait_ge(sum_ok, g * 4 + 3)
                    e.tensor_scalar(rstd[:], mv[:, :, 1], LN_EPS, None, ALU.add).then_inc(var_ok, 1)

                def normalise(g, tiles):
                    if tiles.start == 0:
                        e.wait_ge(root_ok, g + 1)
                        e.reciprocal(rstd[:], rstd[:]).then_inc(sum_ok, 1)
                        e.wait_ge(sum_ok, g * 4 + 4)
                    last = norm_apply(e, x1, x1, mv, rstd, tiles)
                    if tiles.stop == GRP:
                        last.then_inc(x1_ok, 1)

                low, high = pieces
                stages = (residual, lambda g: statistics(g, low), lambda g: statistics(g, high), variance,
                          lambda g: normalise(g, low), lambda g: normalise(g, high), lambda g: clear(g))
                assert len(stages) == GRP

                def clear(g):
                    e.wait_ge(sums_ok, g + 1)
                    e.tensor_copy(acc[:, :, bass.ds(g * (GRP * P), GRP * P)], zeros)

                def receiver(g, t):
                    e.wait_ge(q_mm, g * GRP + (t + 1))
                    for n, piece in enumerate(pieces):
                        if t == piece.start:
                            e.wait_ge(q_st[n], g * 16 + 16)
                    e.tensor_tensor(q_buf[:, t, :].rearrange("p (b n) -> p b n", b=2), ps_q[:, :, 0:2 * PW],
                                    bias, ALU.add).then_inc(q_ok, 1)

                e.wait_ge(w_clear, 2)
                for stage in stages:
                    stage(0)
                with e.Fori(0, NG - 1) as g:
                    for t in range(GRP):
                        receiver(g, t)
                        stages[t](g + 1)
                for t in range(GRP):
                    receiver(NG - 1, t)


def norm_stats(e, x, stats, mv, rstd, own, at, var_ok, gate):
    for t in range(GRP):
        last = e.bn_stats(stats[:, t, :], x[:, t, :])
    last.then_inc(own, 1)
    e.wait_ge(own, at + 1)
    e.sem_inc(gate, 1)
    for t in range(GRP):
        last = e.bn_aggr(mv[:, t, :], stats[:, t, :])
    last.then_inc(own, 1)
    e.wait_ge(own, at + 2)
    e.tensor_scalar(rstd[:], mv[:, :, 1], LN_EPS, None, ALU.add).then_inc(var_ok, 1)


def norm_apply(e, x, out, mv, rstd, tiles=slice(0, GRP)):
    for t in range(tiles.start, tiles.stop):
        last = e.tensor_scalar(out[:, t, :], x[:, t, :], mv[:, t, 0:1], rstd[:, t:t + 1],
                               ALU.subtract, ALU.mult)
    return last


def edges1(nc, k, dram):
    with ExitStack() as ctx:
        m = Mem(nc, ctx)
        QT = TPS // 2
        UN = 4
        idx = m.sb("idx1", [P, 2, TPS], u32)
        gp = m.sb("gp", [P, 2, TPS, PW])
        win = m.sb("win", [P, 2, PPS, PW])
        hot = m.sb("hot1", [P, UN, TPS, P], bf16)
        hot_n = m.sb("hot_n", [P, UN, TPS, WIN], bf16)
        hot_t = m.sb("hot_t", [P, UN, TPS, T])
        hot_x = m.sb("hot_x", [P, 2, TPS, P])
        ident16 = m.sb("ident16", [P, P], bf16)
        pre = m.sb("pre", [P, 2, TPS, PW])
        hid = m.sb("hid", [P, 2, TPS, H])
        hid_rest, hid_low = m.sb("hid_rest", [P, TPS, H]), m.sb("hid_low", [P, TPS, H], bf16)
        score = m.sb("score", [P, 2, TPS])
        sc, sc_rest, sc_low = m.sb("sc", [P, TPS, T]), m.sb("sc_rest", [P, TPS, T]), m.sb("sc_low", [P, TPS, T], bf16)
        ps_x = m.ps("ps_x", [P, 2, TPS, P], bf16)
        ps_e = m.ps("ps_e", [P, TPS, 2 * P])
        ps_g = m.ps("ps_g", [P, PPS, P])
        ps_s = m.ps("ps_s", [T, PPS, P])
        idx_in, win_in, landed = m.sems("idx_in1", 2), m.sems("win_in", 2), m.sems("landed1", 2)
        (used, gate, id_ok, hot_ok, x_mm, x_ok, e_mm, pre_ok, score_ok, hid_ok, own, split_ok, sum_mm, acc_own,
         score_own) = (
            m.sem(n + "_1") for n in ("used", "gate", "id_ok", "hot_ok", "x_mm", "x_ok", "e_mm", "pre_ok",
                                      "score_ok", "hid_ok", "own", "split_ok", "sum_mm", "acc_own", "score_own"))

        with nc.Block() as block:

            @block.sync
            def _(e):
                regs = start_registers(e, "window")

                def load_windows(j, h):
                    for p, start in enumerate(run_starts(e, k, j, regs)):
                        e.dma_start(win[:, h, p, :], dram["q_tab"][bass.ds(start * T, P), :]).then_inc(win_in[h], 16)

                for h in range(2):
                    e.dma_start(idx[:, h, :], dram["p_idx"][:, h * TPS:(h + 1) * TPS]).then_inc(idx_in[h], 16)
                    load_windows(h, h)
                with e.Fori(0, STEPS // 2) as i:
                    for h in range(2):
                        e.wait_ge(e_mm, i * 4 + (2 * h + 2))
                        load_windows(i * 2 + (h + 2), h)
                        e.wait_ge(landed[h], i * (16 * TPS) + 16 * TPS)
                        e.dma_start(idx[:, h, :], dram["p_idx"][:, bass.ds(i * (2 * TPS) + (h + 2) * TPS, TPS)])\
                            .then_inc(idx_in[h], 16)
                for h in range(2):
                    e.wait_ge(win_in[h], 16 * PPS * (STEPS // 2 + 1))
                    e.wait_ge(idx_in[h], 16 * (STEPS // 2 + 1))

            @block.gpsimd
            def _(e):
                gather_loop(e, idx, idx_in, dram["p_tab"], gp, landed, used, gate)

            @block.scalar
            def _(e):
                def copy_x(h, value):
                    e.wait_ge(x_mm, value)
                    e.activation(hot_x[:, h], ps_x[:, h], ACT.Copy).then_inc(x_ok, 1)

                e.preload_act_table(ACT.Sigmoid)
                for n in range(2):
                    copy_x(n, n + 1)
                with e.Fori(0, STEPS // UN) as i:
                    for u in range(UN):
                        h = u % 2
                        for q in range(2):
                            e.wait_ge(pre_ok, i * (2 * UN) + (2 * u + q + 1))
                            mine = slice(QT * q, QT * (q + 1))
                            e.activation(score[:, h, mine], pre[:, h, mine, H], ACT.Sigmoid).then_inc(score_ok, 1)
                            e.wait_ge(score_ok, i * (2 * UN) + (2 * u + q + 1))
                            for t in range(QT * q, QT * (q + 1)):
                                last = e.activation(hid[:, h, t, :], pre[:, h, t, 0:H], ACT.Relu,
                                                    scale=score[:, h, t:t + 1])
                            last.then_inc(hid_ok, 1)
                        copy_x(h, i * UN + (u + 3))

            @block.tensor
            def _(e):
                def transposes(buf, h, value):
                    e.wait_ge(hot_ok, value)
                    for t in range(TPS):
                        last = e.transpose(ps_x[:, h, t, :], hot[:, buf, t, :], ident16[:])
                    last.then_inc(x_mm, 1)

                def receivers(h, value, win_value, pre_value):
                    e.wait_ge(x_ok, value)
                    e.wait_ge(win_in[h], win_value)
                    for q in range(2):
                        e.wait_ge(pre_ok, pre_value + q)
                        for t in range(QT * q, QT * (q + 1)):
                            last = e.matmul(ps_e[:, t, 0:PW], hot_x[:, h, t, :], win[:, h, t // 2, :],
                                            start=True, stop=True)
                        last.then_inc(e_mm, 1)

                def parts(f, rest, low, t):
                    return enumerate((upper(f[:, t, :]), upper(rest[:, t, :]), low[:, t, :]))

                e.wait_ge(id_ok, 1)
                transposes(0, 0, 1)
                transposes(1, 1, 2)
                e.wait_ge(x_ok, 1)
                e.wait_ge(win_in[0], 16 * PPS)
                for t in range(TPS):
                    last = e.matmul(ps_e[:, t, 0:PW], hot_x[:, 0, t, :], win[:, 0, t // 2, :], start=True, stop=True)
                    if t % QT == QT - 1:
                        last.then_inc(e_mm, 1)
                with e.Fori(0, STEPS // UN) as i:
                    for u in range(UN):
                        h = u % 2
                        receivers(1 - h, i * UN + (u + 2),
                                  i * (16 * PPS * UN // 2) + 16 * PPS * ((u + 1) // 2 + 1),
                                  i * (2 * UN) + (2 * u + 1))
                        transposes((u + 2) % UN, h, i * UN + (u + 3))
                        e.wait_ge(split_ok, i * (3 * UN) + (3 * u + 1))
                        for p in range(PPS):
                            for t in range(2 * p, 2 * p + 2):
                                for n, part in parts(sc, sc_rest, sc_low, t):
                                    e.matmul(ps_s[:, p, 0:WIN], part, hot_n[:, u, t, :],
                                             start=t % 2 + n == 0, stop=t % 2 + n == 3)
                        for q in range(2):
                            e.wait_ge(split_ok, i * (3 * UN) + (3 * u + 2 + q))
                            for p in range(PPS // 2 * q, PPS // 2 * (q + 1)):
                                for t in range(2 * p, 2 * p + 2):
                                    for n, part in parts(hid[:, h], hid_rest, hid_low, t):
                                        last = e.matmul(ps_g[:, p, :], part, hot[:, u, t, :],
                                                        start=t % 2 + n == 0, stop=t % 2 + n == 3)
                        last.then_inc(sum_mm, 1)

            @block.vector
            def _(e):
                def one_hot_small(tiles, buf):
                    e.tensor_tensor(hot_n[:, buf], spread(k["iota"][:, 0:WIN], 1, TPS),
                                    spread(k["dloc"][:, tiles], 2, WIN), ALU.is_equal)
                    e.tensor_tensor(hot_t[:, buf], spread(k["iota"][:, 0:T], 1, TPS),
                                    spread(k["typef"][:, tiles], 2, T), ALU.is_equal)

                def one_hot_key(tiles, buf):
                    e.tensor_tensor(hot[:, buf], spread(k["iota"][:, 0:P], 1, TPS),
                                    spread(k["key"][:, tiles], 2, P), ALU.is_equal).then_inc(hot_ok, 1)

                regs = start_registers(e, "sum1")

                def start_windows(j):
                    starts = run_starts(e, k, j, regs)

                    def add(p):
                        at = k["acc"][:, bass.ds(starts[p] * T, P)]
                        at_s = k["acc_s"][0:T, bass.ds(starts[p], WIN)]
                        e.wait_ge(sum_mm, j + 1)
                        e.wait_ge(acc_own, j * PPS + (p + 1))
                        e.tensor_tensor(at, at, ps_g[:, p, :], ALU.add).then_inc(acc_own, 1)
                        e.wait_ge(score_own, j * PPS + (p + 1))
                        e.tensor_tensor(at_s, at_s, ps_s[:, p, 0:WIN], ALU.add).then_inc(score_own, 1)
                    return add

                def edge_rows(i, u, before):
                    j, h = i * UN + u, u % 2
                    add = start_windows(j - 1) if before else (lambda p: None)
                    ahead, buf = bass.ds(j * TPS + 2 * TPS, TPS), (u + 2) % UN
                    e.wait_ge(landed[h], i * (16 * TPS * UN // 2) + 16 * TPS * (u // 2 + 1))
                    for q in range(2):
                        mine = slice(QT * q, QT * (q + 1))
                        e.wait_ge(e_mm, j * 2 + (q + 1))
                        e.tensor_tensor(pre[:, h, mine, :], ps_e[:, mine, 0:PW], gp[:, h, mine, :],
                                        ALU.add).then_inc(pre_ok, 1)
                    add(0)
                    e.wait_ge(pre_ok, j * 2 + 2)
                    e.sem_inc(used, 1)
                    one_hot_small(ahead, buf)
                    add(1)
                    one_hot_key(ahead, buf)
                    add(2)
                    e.wait_ge(score_ok, j * 2 + 2)
                    e.wait_ge(hot_ok, j + 1)
                    e.tensor_tensor(sc[:], hot_t[:, u], spread(score[:, h, :], 2, T), ALU.mult).then_inc(own, 1)
                    add(3)
                    parts = [(x[:].rearrange("p t n -> p (t n)"), y[:].rearrange("p t n -> p (t n)"))
                             for x, y in ((sc, sc_rest), (sc_rest, sc_low))]
                    for n, (whole, part) in enumerate(parts):
                        e.wait_ge(own, j * 4 + (1 + n))
                        last = e.tensor_tensor(part, whole, upper(whole), ALU.subtract)
                        last.then_inc((own, split_ok)[n], 1)
                    for q in range(2):
                        mine = slice(QT * q, QT * (q + 1))
                        whole, rest, low = (x.rearrange("p t n -> p (t n)") for x in (
                            hid[:, h, mine, :], hid_rest[:, mine, :], hid_low[:, mine, :]))
                        e.wait_ge(hid_ok, j * 2 + (q + 1))
                        e.tensor_tensor(rest, whole, upper(whole), ALU.subtract).then_inc(own, 1)
                        e.wait_ge(own, j * 4 + (3 + q))
                        e.tensor_tensor(low, rest, upper(rest), ALU.subtract).then_inc(split_ok, 1)

                e.tensor_copy(ident16[:], k["ident"][:]).then_inc(id_ok, 1)
                e.memset(k["acc_s"][0:T, :], 0.0)
                e.sem_inc(used, 2)
                for s in (acc_own, score_own):
                    e.sem_inc(s, 1)
                for u in range(2):
                    one_hot_small(bass.ds(u * TPS, TPS), u)
                    one_hot_key(bass.ds(u * TPS, TPS), u)
                for u in range(UN):
                    edge_rows(0, u, u > 0)
                with e.Fori(1, STEPS // UN) as i:
                    for u in range(UN):
                        edge_rows(i, u, True)
                add = start_windows(STEPS - 1)
                for p in range(PPS):
                    add(p)
                for s in (acc_own, score_own):
                    e.wait_ge(s, STEPS * PPS + 1)


def update(nc, k, dram, later, out):
    with ExitStack() as ctx:
        m = Mem(nc, ctx)
        half_n = GRP * P // 2
        w2, b2, w_ih, w_hh, b_ih, b_hh, gamma, beta = (later[n] for n in (
            "w2", "b2", "w_ih", "w_hh", "b_ih", "b_hh", "gamma", "beta"))
        b_rz = m.sb("b_rz", [P, 2])
        x1_t, agg_t = m.sb("x1_tu", [P, 2, half_n]), m.sb("agg_t", [P, 2, half_n])
        r, z, cand, diff, both, new_t = (m.sb(n + "_u", [P, 2, half_n]) for n in (
            "r", "z", "cand", "diff", "both", "new_t"))
        x1, x1_beta, new, mid, y = (m.sb(n + "_u", [P, GRP, H]) for n in ("x1", "x1_beta", "new", "mid", "y"))
        stats, mv, rstd = m.sb("stats_u", [P, GRP, 6]), m.sb("mv_u", [P, GRP, 2]), m.sb("rstd_u", [P, GRP])
        ps_a, ps_n = m.ps("ps_au", [P, 2, 512]), m.ps("ps_nu", [P, 8, P])
        ps_r, ps_z, ps_i, ps_h = (m.ps(f"ps_{n}u", [P, 512])[:, 0:half_n] for n in "rzih")
        b_ok, xt_ld, xt_used, x_ld, x_used, a_mm, a_ok, gate_mm, rz_ok, mul_ok, cand_ok, tanh_ok = (
            m.sem(n + "_u") for n in ("b_ok", "xt_ld", "xt_used", "x_ld", "x_used", "a_mm", "a_ok",
                                      "gate_mm", "rz_ok", "mul_ok", "cand_ok", "tanh_ok"))
        (both_ok, new_t_ok, n_mm, new_ok, beta_ok, var_ok, root_ok, out_ok, out_st, own_f, own_n, res_ok,
         gate_p, gate_v) = (
            m.sem(n + "_u") for n in ("both_ok", "new_t_ok", "n_mm", "new_ok", "beta_ok", "var_ok", "root_ok", "out_ok",
                                      "out_st", "own_f", "own_n", "res_ok", "gate_p", "gate_v"))
        new_used = m.sem("new_used")
        minus_half, half_ok = m.sb("minus_half", [P, GRP]), m.sem("half_ok")
        x1_g = dram["x1"].rearrange("(t p) f -> p t f", p=P)
        out_g = out.rearrange("(t p) f -> p t f", p=P)

        with nc.Block() as block:

            @block.sync
            def _(e):
                e.sem_inc(xt_used, 2)
                e.sem_inc(x_used, 1)
                with e.Fori(0, NG) as g:
                    rows = bass.ds(g * GRP, GRP)
                    e.wait_ge(xt_used, g * 2 + 2)
                    e.dma_start(x1_t[:], dram["x1_t"][:, bass.ds(g * (GRP * P), GRP * P)]
                                .rearrange("p (b n) -> p b n", b=2)).then_inc(xt_ld, 16)
                    e.wait_ge(x_used, g + 1)
                    e.dma_start(x1[:], x1_g[:, rows, :]).then_inc(x_ld, 16)

            @block.gpsimd
            def _(e):
                def both_sum(g, b):
                    e.wait_ge(tanh_ok, g * 2 + (b + 1))
                    e.tensor_tensor(both[:, b, :], x1_t[:, b, :], cand[:, b, :], ALU.add).then_inc(both_ok, 1)

                def beta_sum(g):
                    e.wait_ge(x_ld, g * 16 + 16)
                    e.wait_ge(res_ok, g + 1)
                    e.tensor_tensor(x1_beta[:], x1[:], spread(beta[:], 1, GRP), ALU.add).then_inc(beta_ok, 1)
                    e.wait_ge(beta_ok, g + 1)
                    e.sem_inc(x_used, 1)

                def root(g, n):
                    e.wait_ge(var_ok, g * 2 + (n + 1))
                    e.tensor_tensor(rstd[:], rstd[:], minus_half[:], ALU.pow).then_inc(root_ok, 1)

                def group(g, norm):
                    e.wait_ge(xt_ld, g * 16 + 16)
                    both_sum(g, 0)
                    if norm:
                        root(g - 1, 0)
                    both_sum(g, 1)
                    e.wait_ge(both_ok, g * 2 + 2)
                    e.sem_inc(xt_used, 1)
                    beta_sum(g)
                    if norm:
                        root(g - 1, 1)
                        store(g - 1)

                def store(g):
                    e.wait_ge(out_ok, g + 2)
                    e.sem_inc(gate_p, 1)
                    e.dma_start(out_g[:, bass.ds(g * GRP, GRP), :], y[:]).then_inc(out_st, 16)

                e.memset(minus_half[:], -0.5).then_inc(half_ok, 1)
                e.wait_ge(half_ok, 1)
                group(0, False)
                with e.Fori(1, NG) as g:
                    group(g, True)
                root(NG - 1, 0)
                root(NG - 1, 1)
                store(NG - 1)
                e.wait_ge(out_st, 16 * NG)

            @block.scalar
            def _(e):
                def gates(g, b):
                    for out_s, ps, bias, n in ((r, ps_r, b_rz[:, 0:1], 1), (z, ps_z, b_rz[:, 1:2], 2)):
                        e.wait_ge(gate_mm, g * 8 + (b * 4 + n))
                        e.activation(out_s[:, b, :], ps, ACT.Sigmoid, bias=bias).then_inc(rz_ok, 1)
                    e.wait_ge(cand_ok, g * 2 + (b + 2))
                    e.activation(cand[:, b, :], cand[:, b, :], ACT.Tanh, bias=b_ih[:, 2:3]).then_inc(tanh_ok, 1)

                def sums(g, b):
                    e.wait_ge(a_mm, g * 2 + (b + 1))
                    e.activation(agg_t[:, b, :], ps_a[:, b, 0:half_n], ACT.Copy).then_inc(a_ok, 1)

                def nodes(g):
                    e.wait_ge(n_mm, g + 1)
                    e.wait_ge(new_used, g + 1)
                    e.activation(new[:], ps_n[:, 0:GRP, :], ACT.Copy).then_inc(new_ok, 1)

                def group(g):
                    for b in range(2):
                        gates(g, b)

                e.preload_act_table(ACT.Sigmoid)
                e.wait_ge(b_ok, 1)
                sums(0, 0)
                sums(0, 1)
                with e.Fori(0, NG - 1) as g:
                    group(g)
                    sums(g + 1, 0)
                    sums(g + 1, 1)
                    nodes(g)
                group(NG - 1)
                nodes(NG - 1)

            @block.tensor
            def _(e):
                acc = k["acc"][:].rearrange("p (n t) -> p t n", t=T)

                def sums(g):
                    for b in range(2):
                        nodes = bass.ds(g * (GRP * P) + b * half_n, half_n)
                        for t in range(T):
                            e.matmul(ps_a[:, b, 0:half_n], w2[:, t, :], acc[:, t, nodes], start=t == 0, stop=False)
                        e.matmul(ps_a[:, b, 0:half_n], b2[:], k["acc_s"][0:T, nodes], start=False, stop=True)\
                            .then_inc(a_mm, 1)

                def gates(g):
                    e.wait_ge(xt_ld, g * 16 + 16)
                    for b in range(2):
                        e.wait_ge(a_ok, g * 2 + (b + 1))
                        for ps, free, value, parts in (
                                (ps_r, rz_ok, g * 4 + (2 * b + 1), ((agg_t, w_ih, 0), (x1_t, w_hh, 0))),
                                (ps_z, rz_ok, g * 4 + (2 * b + 2), ((agg_t, w_ih, 1), (x1_t, w_hh, 1))),
                                (ps_h, mul_ok, g * 2 + (b + 1), ((x1_t, w_hh, 2),)),
                                (ps_i, cand_ok, g * 2 + (b + 1), ((agg_t, w_ih, 2),))):
                            e.wait_ge(free, value)
                            for s, (x, wt, c) in enumerate(parts):
                                last = e.matmul(ps, wt[:, c * H:(c + 1) * H], x[:, b, :], start=s == 0,
                                                stop=s == len(parts) - 1)
                            last.then_inc(gate_mm, 1)

                def transposes(g):
                    e.wait_ge(new_t_ok, g * 2 + 2)
                    if not isinstance(g, int) or g:
                        e.wait_ge(new_ok, g)
                    for t in range(GRP):
                        last = e.transpose(ps_n[:, t, :], new_t[:].rearrange("p b n -> p (b n)")[:, t * P:(t + 1) * P],
                                           k["ident"][:])
                    last.then_inc(n_mm, 1)

                e.sem_inc(rz_ok, 2)
                for s in (mul_ok, cand_ok, out_ok, res_ok, new_used):
                    e.sem_inc(s, 1)
                sums(0)
                gates(0)
                sums(1)
                transposes(0)
                with e.Fori(1, NG - 1) as g:
                    gates(g)
                    sums(g + 1)
                    transposes(g)
                gates(NG - 1)
                transposes(NG - 1)

            @block.vector
            def _(e):
                NORM = 6

                def candidate(g, b):
                    e.wait_ge(rz_ok, g * 4 + (2 * b + 3))
                    e.wait_ge(gate_mm, g * 8 + (4 * b + 3))
                    e.scalar_tensor_tensor(cand[:, b, :], ps_h, b_hh[:, 2:3], r[:, b, :], ALU.add, ALU.mult)\
                        .then_inc(mul_ok, 1)
                    e.wait_ge(mul_ok, g * 2 + (b + 2))
                    e.wait_ge(gate_mm, g * 8 + (4 * b + 4))
                    e.tensor_tensor(cand[:, b, :], cand[:, b, :], ps_i, ALU.add).then_inc(cand_ok, 1)

                def blend(g, b):
                    e.wait_ge(tanh_ok, g * 2 + (b + 1))
                    e.tensor_tensor(diff[:, b, :], x1_t[:, b, :], cand[:, b, :], ALU.subtract).then_inc(own_f, 1)
                    e.wait_ge(own_f, g * 4 + (2 * b + 1))
                    if b:
                        e.sem_inc(xt_used, 1)
                    e.wait_ge(rz_ok, g * 4 + (2 * b + 4))
                    e.tensor_tensor(diff[:, b, :], diff[:, b, :], z[:, b, :], ALU.mult).then_inc(own_f, 1)
                    e.wait_ge(own_f, g * 4 + (2 * b + 2))
                    e.wait_ge(both_ok, g * 2 + (b + 1))
                    e.tensor_tensor(new_t[:, b, :], both[:, b, :], diff[:, b, :], ALU.add).then_inc(new_t_ok, 1)

                def statistics(g):
                    e.wait_ge(new_ok, g + 1)
                    norm_stats(e, new, stats, mv, rstd, own_n, g * NORM, var_ok, gate_v)

                def norms(g):
                    e.wait_ge(root_ok, g * 2 + 1)
                    norm_apply(e, new, mid, mv, rstd).then_inc(own_n, 1)
                    e.wait_ge(own_n, g * NORM + 3)
                    e.sem_inc(new_used, 1)
                    e.tensor_tensor(mid[:], mid[:], spread(gamma[:], 1, GRP), ALU.mult).then_inc(own_n, 1)
                    e.wait_ge(own_n, g * NORM + 4)
                    e.wait_ge(beta_ok, g + 1)
                    e.tensor_tensor(mid[:], mid[:], x1_beta[:], ALU.add).then_inc(res_ok, 1)
                    e.wait_ge(res_ok, g + 2)
                    norm_stats(e, mid, stats, mv, rstd, own_n, g * NORM + 4, var_ok, gate_v)
                    e.wait_ge(root_ok, g * 2 + 2)
                    if not isinstance(g, int) or g:
                        e.wait_ge(out_st, g * 16)
                    norm_apply(e, mid, y, mv, rstd).then_inc(out_ok, 1)

                def group(g, norm):
                    candidate(g, 0)
                    if norm:
                        statistics(g - 1)
                    blend(g, 0)
                    candidate(g, 1)
                    blend(g, 1)
                    if norm:
                        norms(g - 1)

                e.tensor_tensor(b_rz[:], b_ih[:, 0:2], b_hh[:, 0:2], ALU.add).then_inc(b_ok, 1)
                group(0, False)
                with e.Fori(1, NG) as g:
                    group(g, True)
                statistics(NG - 1)
                norms(NG - 1)


def kernel(**inputs):
    import numpy as np
    import concourse.bacc as bacc
    from concourse.bass_utils import run_bass_kernel_spmd

    arrays = lay_out(np, inputs)
    nc = bacc.Bacc("TRN2", target_bir_lowering=False, num_devices=1)
    aps = {n: nc.dram_tensor(f"in_{n}", v.shape, mybir.dt.from_np(v.dtype), kind="ExternalInput").ap()
           for n, v in arrays.items()}
    out = nc.dram_tensor("out", (NP, H), f32, kind="ExternalOutput").ap()
    build(nc, aps, out)
    r = run_bass_kernel_spmd(nc, [{f"in_{n}": v for n, v in arrays.items()}], core_ids=[0])
    return r.results[0]["out"][0:N]


def lay_out(np, inputs):
    def flat(v, fill, n):
        v = np.asarray(v)
        pad = np.full((n - v.shape[0],) + v.shape[1:], fill, v.dtype)
        return np.concatenate([v, pad])

    def by_partition(v, tiles):
        v = v.reshape(tiles, P, *v.shape[1:]).swapaxes(0, 1)
        return np.ascontiguousarray(v)

    dst = flat(inputs["dst"], N, LTILES * P)
    length = flat(inputs["edge_weight"], 0.0, TILES * P).reshape(ECH // 2, SPC, PPS, 2, P)
    L0, L1 = "L0_gnn_", "L1_gnn_"
    arrays = {
        "x": flat(inputs["x"], 0.0, NP),
        "src": by_partition(flat(inputs["src"], 0, LTILES * P), LTILES),
        "dst": by_partition(dst, LTILES),
        "type": by_partition(flat(inputs["edge_type_4"], 0, LTILES * P), LTILES),
        "start": dst[::2 * P].reshape(1, LTILES // 2),
        "vec": by_partition(flat(inputs["edge_attr_3"], 0.0, TILES * P), TILES),
        "length": length.transpose(0, 3, 1, 2, 4).reshape(ECH, SPC * HALF),
        "mlp_b0": inputs[L0 + "mlp_b0"].reshape(HID, 1),
        "mlp_b1": inputs[L0 + "mlp_b1"].reshape(HID, 1),
        "mlp_b2": inputs[L0 + "mlp_b2"].reshape(1, P),
        "attn_wT": inputs[L1 + "attn_w"].T,
        "attn_b": inputs[L1 + "attn_b"].reshape(1, T),
        "w_ihT": inputs[L1 + "w_ih"].T,
        "w_hhT": inputs[L1 + "w_hh"].T,
        "b_ihT": inputs[L1 + "b_ih"].reshape(3, H).T,
        "b_hhT": inputs[L1 + "b_hh"].reshape(3, H).T,
        "gamma": inputs[L1 + "ln_gamma"].reshape(1, H),
        "beta": inputs[L1 + "ln_beta"].reshape(1, H),
    }
    for n in ("W_up0", "W_up1", "mlp_w0", "mlp_w1", "mlp_w2", "W_out0", "W_out1"):
        arrays[n] = inputs[L0 + n]
    for n in ("W1", "b1", "W2", "b2"):
        arrays[n] = inputs[L1 + n]
    return {n: np.ascontiguousarray(v) for n, v in arrays.items()}
```
